# Optimizing a Trainium2 kernel written in Bass

```python
import numpy as np
import jax
import jax.numpy as jnp

def _softmax(x, axis=-1):
    return jax.nn.softmax(x, axis=axis)

def _gelu(x):
    return jax.nn.gelu(x, approximate=True)

def _silu(x):
    return jax.nn.silu(x)

def _sigmoid(x):
    return jax.nn.sigmoid(x)

def _layernorm(x, axis=-1, eps=1e-05):
    m = jnp.mean(x, axis=axis, keepdims=True)
    v = jnp.var(x, axis=axis, keepdims=True)
    return (x - m) / jnp.sqrt(v + eps)

def _scatter_add(tgt, idx, src, axis=0):
    return tgt.at[idx].add(src)

def _segment_sum(src, seg, n):
    return jax.ops.segment_sum(src, seg, n)
kernel_name = 'mk_adaln_d2_jaxref_r4_345262'

def setup_inputs(seed: int=0):
    np.random.seed(seed)
    _w = jnp.asarray

    def _L0_attn_setup():
        import jax, jax.numpy as jnp
        import numpy as np
        HIDDEN = 256
        D_MEM = 64
        BATCH = 4
        SEQ = 256
        EPS = 1e-06

        def elu_plus_one(x):
            return jnp.where(x > 0, x + 1.0, jnp.exp(x))

        def _retrieve(sigma_x, memory, memory_norm):
            a_unnorm = jnp.matmul(sigma_x, memory)
            norm = jnp.clip(jnp.matmul(sigma_x, memory_norm), EPS, None)[..., None]
            out = a_unnorm / norm
            return jnp.where(memory_norm.sum() < EPS, jnp.zeros_like(out), out)

        def _reference_tuple_inner(hidden_states, w_q, w_k, w_v, w_o, gate, memory, memory_norm):
            b, s, _ = hidden_states.shape
            q = jnp.einsum('bsh,dh->bsd', hidden_states, w_q)
            k = jnp.einsum('bsh,dh->bsd', hidden_states, w_k)
            v = jnp.einsum('bsh,dh->bsd', hidden_states, w_v)
            sigma_q = elu_plus_one(q)
            sigma_k = elu_plus_one(k)
            memory_output = _retrieve(sigma_q, memory, memory_norm)
            kv = jnp.einsum('bsd,bse->bsde', sigma_k, v)
            kv_cumsum = jnp.cumsum(kv, axis=1)
            k_cumsum = jnp.cumsum(sigma_k, axis=1)
            numerator = jnp.einsum('bsd,bsde->bse', sigma_q, kv_cumsum)
            denominator = jnp.clip(jnp.einsum('bsd,bsd->bs', sigma_q, k_cumsum), EPS, None)[..., None]
            local_output = numerator / denominator
            g = jax.nn.sigmoid(gate[0])
            combined = g * memory_output + (1.0 - g) * local_output
            output = jnp.einsum('bsd,hd->bsh', combined, w_o)
            retrieved_unnorm = jnp.matmul(sigma_k, memory)
            norm = jnp.clip(jnp.matmul(sigma_k, memory_norm), EPS, None)[..., None]
            delta_v = v - retrieved_unnorm / norm
            memory_update = jnp.einsum('bsd,bse->de', sigma_k, delta_v) / (b * s)
            new_memory = jax.lax.stop_gradient(memory + memory_update)
            z_update = sigma_k.sum(axis=(0, 1)) / b
            new_memory_norm = jax.lax.stop_gradient(memory_norm + z_update)
            return (output, new_memory, new_memory_norm)
        key = jax.random.key(seed)
        ks = jax.random.split(key, 8)
        hidden_states = jax.random.normal(ks[0], (BATCH, SEQ, HIDDEN), dtype=jnp.float32)
        s = 1.0 / np.sqrt(HIDDEN)
        w_q = jax.random.normal(ks[1], (D_MEM, HIDDEN), dtype=jnp.float32) * s
        w_k = jax.random.normal(ks[2], (D_MEM, HIDDEN), dtype=jnp.float32) * s
        w_v = jax.random.normal(ks[3], (D_MEM, HIDDEN), dtype=jnp.float32) * s
        w_o = jax.random.normal(ks[4], (HIDDEN, D_MEM), dtype=jnp.float32) * (1.0 / np.sqrt(D_MEM))
        gate = jnp.zeros((1,), dtype=jnp.float32)
        memory = jax.random.normal(ks[5], (D_MEM, D_MEM), dtype=jnp.float32) * 0.1
        memory_norm = jax.random.uniform(ks[6], (D_MEM,), dtype=jnp.float32) * 10.0 + 1.0
        return {'hidden_states': hidden_states, 'w_q': w_q, 'w_k': w_k, 'w_v': w_v, 'w_o': w_o, 'gate': gate, 'memory': memory, 'memory_norm': memory_norm}
    _L0_attn_in = _L0_attn_setup()

    def _L0_ffn_setup():
        import jax, jax.numpy as jnp
        import numpy as np
        D_MODEL = 256
        HIDDEN = 1024
        N_ROUTING = 2
        key = jax.random.key(seed)
        ks = jax.random.split(key, 10)
        s = 0.02
        x = jax.random.normal(ks[0], (4, 1024, D_MODEL), dtype=jnp.float32)
        gate_w = jax.random.normal(ks[1], (N_ROUTING, D_MODEL), dtype=jnp.float32) * s
        w1 = jax.random.normal(ks[2], (N_ROUTING, D_MODEL, HIDDEN), dtype=jnp.float32) * s
        b1 = jax.random.normal(ks[3], (N_ROUTING, HIDDEN), dtype=jnp.float32) * s
        w2 = jax.random.normal(ks[4], (N_ROUTING, HIDDEN, D_MODEL), dtype=jnp.float32) * s
        b2 = jax.random.normal(ks[5], (N_ROUTING, D_MODEL), dtype=jnp.float32) * s
        sw1 = jax.random.normal(ks[6], (D_MODEL, HIDDEN), dtype=jnp.float32) * s
        sb1 = jax.random.normal(ks[7], (HIDDEN,), dtype=jnp.float32) * s
        sw2 = jax.random.normal(ks[8], (HIDDEN, D_MODEL), dtype=jnp.float32) * s
        sb2 = jax.random.normal(ks[9], (D_MODEL,), dtype=jnp.float32) * s
        return {'x': x, 'gate_w': gate_w, 'w1': w1, 'b1': b1, 'w2': w2, 'b2': b2, 'sw1': sw1, 'sb1': sb1, 'sw2': sw2, 'sb2': sb2}
    _L0_ffn_in = _L0_ffn_setup()
    _L0_c = _w((lambda *s: np.random.randn(*s).astype(np.float32) * 0.05)(4, 256))
    _L0_wmod = _w((lambda *s: np.random.randn(*s).astype(np.float32) * 0.05)(256, 6 * 256) * 256 ** (-0.5))

    def _L1_attn_setup():
        import jax, jax.numpy as jnp
        import numpy as np
        EMBED = 256
        HEADS = 16
        HEAD_DIM = EMBED // HEADS
        WIN = 64
        key = jax.random.key(seed)
        k0, k1, k2 = jax.random.split(key, 3)
        s = 0.02
        return {'x': jax.random.normal(k0, (4, 1024, EMBED), dtype=jnp.float32), 'W_qkv': jax.random.normal(k1, (EMBED, 3 * EMBED), dtype=jnp.float32) * s, 'b_qkv': jnp.zeros((3 * EMBED,), dtype=jnp.float32), 'W_out': jax.random.normal(k2, (EMBED, EMBED), dtype=jnp.float32) * s, 'b_out': jnp.zeros((EMBED,), dtype=jnp.float32)}
    _L1_attn_in = _L1_attn_setup()

    def _L1_ffn_setup():
        import jax, jax.numpy as jnp
        import numpy as np
        B, S, D = (1, 512, 256)
        F = 352
        E = 16
        K = 2
        CAP_FACTOR = 1.25

        def _mlp(h, wg, wu, wd):
            return jax.nn.silu(h @ wg) * (h @ wu) @ wd
        key = jax.random.key(seed)
        ks = jax.random.split(key, 10)
        sd = 0.02
        return {'x': jax.random.normal(ks[0], (B, S, D), jnp.float32), 'router_w': jax.random.normal(ks[1], (D, E), jnp.float32) * sd, 'router_b': jnp.zeros((E,), jnp.float32), 'w_gate': jax.random.normal(ks[2], (E, D, F), jnp.float32) * sd, 'w_up': jax.random.normal(ks[3], (E, D, F), jnp.float32) * sd, 'w_down': jax.random.normal(ks[4], (E, F, D), jnp.float32) * sd, 'sw_gate': jax.random.normal(ks[5], (D, F), jnp.float32) * sd, 'sw_up': jax.random.normal(ks[6], (D, F), jnp.float32) * sd, 'sw_down': jax.random.normal(ks[7], (F, D), jnp.float32) * sd}
    _L1_ffn_in = _L1_ffn_setup()
    _L1_c = _w((lambda *s: np.random.randn(*s).astype(np.float32) * 0.05)(4, 256))
    _L1_wmod = _w((lambda *s: np.random.randn(*s).astype(np.float32) * 0.05)(256, 6 * 256) * 256 ** (-0.5))
    _d = {'L0_attn_hidden_states': _L0_attn_in['hidden_states'], 'L0_attn_w_q': _L0_attn_in['w_q'], 'L0_attn_w_k': _L0_attn_in['w_k'], 'L0_attn_w_v': _L0_attn_in['w_v'], 'L0_attn_w_o': _L0_attn_in['w_o'], 'L0_attn_gate': _L0_attn_in['gate'], 'L0_attn_memory': _L0_attn_in['memory'], 'L0_attn_memory_norm': _L0_attn_in['memory_norm'], 'L0_ffn_gate_w': _L0_ffn_in['gate_w'], 'L0_ffn_w1': _L0_ffn_in['w1'], 'L0_ffn_b1': _L0_ffn_in['b1'], 'L0_ffn_w2': _L0_ffn_in['w2'], 'L0_ffn_b2': _L0_ffn_in['b2'], 'L0_ffn_sw1': _L0_ffn_in['sw1'], 'L0_ffn_sb1': _L0_ffn_in['sb1'], 'L0_ffn_sw2': _L0_ffn_in['sw2'], 'L0_ffn_sb2': _L0_ffn_in['sb2'], 'L0_c': _L0_c, 'L0_wmod': _L0_wmod, 'L1_attn_W_qkv': _L1_attn_in['W_qkv'], 'L1_attn_b_qkv': _L1_attn_in['b_qkv'], 'L1_attn_W_out': _L1_attn_in['W_out'], 'L1_attn_b_out': _L1_attn_in['b_out'], 'L1_ffn_router_w': _L1_ffn_in['router_w'], 'L1_ffn_router_b': _L1_ffn_in['router_b'], 'L1_ffn_w_gate': _L1_ffn_in['w_gate'], 'L1_ffn_w_up': _L1_ffn_in['w_up'], 'L1_ffn_w_down': _L1_ffn_in['w_down'], 'L1_ffn_sw_gate': _L1_ffn_in['sw_gate'], 'L1_ffn_sw_up': _L1_ffn_in['sw_up'], 'L1_ffn_sw_down': _L1_ffn_in['sw_down'], 'L1_c': _L1_c, 'L1_wmod': _L1_wmod}
    _x0 = _d['L0_attn_hidden_states']
    _d['L0_attn_hidden_states'] = jax.random.normal(jax.random.fold_in(jax.random.key(seed), 1), (4, 1024, 256), dtype=_x0.dtype)
    del _x0
    return _d

def reference(L0_attn_hidden_states, L0_attn_w_q, L0_attn_w_k, L0_attn_w_v, L0_attn_w_o, L0_attn_gate, L0_attn_memory, L0_attn_memory_norm, L0_ffn_gate_w, L0_ffn_w1, L0_ffn_b1, L0_ffn_w2, L0_ffn_b2, L0_ffn_sw1, L0_ffn_sb1, L0_ffn_sw2, L0_ffn_sb2, L0_c, L0_wmod, L1_attn_W_qkv, L1_attn_b_qkv, L1_attn_W_out, L1_attn_b_out, L1_ffn_router_w, L1_ffn_router_b, L1_ffn_w_gate, L1_ffn_w_up, L1_ffn_w_down, L1_ffn_sw_gate, L1_ffn_sw_up, L1_ffn_sw_down, L1_c, L1_wmod):

    def _L0_attn_ref(hidden_states, w_q, w_k, w_v, w_o, gate, memory, memory_norm):
        import jax, jax.numpy as jnp
        import numpy as np
        HIDDEN = 256
        D_MEM = 64
        BATCH = 4
        SEQ = 256
        EPS = 1e-06

        def elu_plus_one(x):
            return jnp.where(x > 0, x + 1.0, jnp.exp(x))

        def _retrieve(sigma_x, memory, memory_norm):
            a_unnorm = jnp.matmul(sigma_x, memory)
            norm = jnp.clip(jnp.matmul(sigma_x, memory_norm), EPS, None)[..., None]
            out = a_unnorm / norm
            return jnp.where(memory_norm.sum() < EPS, jnp.zeros_like(out), out)

        def _reference_tuple_inner(hidden_states, w_q, w_k, w_v, w_o, gate, memory, memory_norm):
            b, s, _ = hidden_states.shape
            q = jnp.einsum('bsh,dh->bsd', hidden_states, w_q)
            k = jnp.einsum('bsh,dh->bsd', hidden_states, w_k)
            v = jnp.einsum('bsh,dh->bsd', hidden_states, w_v)
            sigma_q = elu_plus_one(q)
            sigma_k = elu_plus_one(k)
            memory_output = _retrieve(sigma_q, memory, memory_norm)
            kv = jnp.einsum('bsd,bse->bsde', sigma_k, v)
            kv_cumsum = jnp.cumsum(kv, axis=1)
            k_cumsum = jnp.cumsum(sigma_k, axis=1)
            numerator = jnp.einsum('bsd,bsde->bse', sigma_q, kv_cumsum)
            denominator = jnp.clip(jnp.einsum('bsd,bsd->bs', sigma_q, k_cumsum), EPS, None)[..., None]
            local_output = numerator / denominator
            g = jax.nn.sigmoid(gate[0])
            combined = g * memory_output + (1.0 - g) * local_output
            output = jnp.einsum('bsd,hd->bsh', combined, w_o)
            retrieved_unnorm = jnp.matmul(sigma_k, memory)
            norm = jnp.clip(jnp.matmul(sigma_k, memory_norm), EPS, None)[..., None]
            delta_v = v - retrieved_unnorm / norm
            memory_update = jnp.einsum('bsd,bse->de', sigma_k, delta_v) / (b * s)
            new_memory = jax.lax.stop_gradient(memory + memory_update)
            z_update = sigma_k.sum(axis=(0, 1)) / b
            new_memory_norm = jax.lax.stop_gradient(memory_norm + z_update)
            return (output, new_memory, new_memory_norm)
        return _reference_tuple_inner(hidden_states, w_q, w_k, w_v, w_o, gate, memory, memory_norm)[0]

    def _L0_ffn_ref(x, gate_w, w1, b1, w2, b2, sw1, sb1, sw2, sb2):
        import jax, jax.numpy as jnp
        import numpy as np
        D_MODEL = 256
        HIDDEN = 1024
        N_ROUTING = 2
        B, S, D = x.shape
        xf = x.reshape(-1, D)
        gate_scores = xf @ gate_w.T
        gate_probs = jax.nn.softmax(gate_scores, axis=-1)
        top1 = jnp.argmax(gate_probs, axis=-1)
        one_hot = jax.nn.one_hot(top1, N_ROUTING, dtype=xf.dtype)
        masked = xf[None, :, :] * one_hot.T[:, :, None]
        h = jax.nn.relu(jnp.einsum('end,edh->enh', masked, w1) + b1[:, None, :])
        expert_out = jnp.einsum('enh,ehd->end', h, w2) + b2[:, None, :]
        routing_output = expert_out.sum(axis=0)
        shared = jax.nn.relu(xf @ sw1 + sb1) @ sw2 + sb2
        return (routing_output + shared).reshape(B, S, D)

    def _L1_attn_ref(x, W_qkv, b_qkv, W_out, b_out):
        import jax, jax.numpy as jnp
        import numpy as np
        EMBED = 256
        HEADS = 16
        HEAD_DIM = EMBED // HEADS
        WIN = 64
        B, L, C = x.shape
        pad_l = -L % WIN
        xp = jnp.pad(x, ((0, 0), (0, pad_l), (0, 0)))
        Lp = L + pad_l
        qkv = (xp @ W_qkv + b_qkv).reshape(B, Lp, 3, HEADS, HEAD_DIM)
        qkv = qkv.transpose(2, 0, 3, 1, 4)
        q, k, v = (qkv[0], qkv[1], qkv[2])
        step = WIN // 2
        Nw = (Lp - WIN) // step + 1
        win_idx = jnp.arange(Nw)[:, None] * step + jnp.arange(WIN)[None, :]

        def unfold(a):
            return a[:, :, win_idx, :].transpose(0, 1, 2, 4, 3)
        qw, kw, vw = (unfold(q), unfold(k), unfold(v))
        attn = jnp.einsum('bhndw,bhnew->bhnde', qw, kw) * HEAD_DIM ** (-0.5)
        attn = jax.nn.softmax(attn, axis=-1)
        o = jnp.einsum('bhnde,bhnew->bhndw', attn, vw)
        o = o.reshape(B, HEADS, -1, HEAD_DIM)
        o = o.transpose(0, 2, 1, 3).reshape(B, -1, C)
        o = o[:, :L]
        return o @ W_out + b_out

    def _L1_ffn_ref(x, router_w, router_b, w_gate, w_up, w_down, sw_gate, sw_up, sw_down):
        import jax, jax.numpy as jnp
        import numpy as np
        B, S, D = (1, 512, 256)
        F = 352
        E = 16
        K = 2
        CAP_FACTOR = 1.25

        def _mlp(h, wg, wu, wd):
            return jax.nn.silu(h @ wg) * (h @ wu) @ wd
        b, s, d = x.shape
        N = b * s
        NK = N * K
        C = int(np.ceil(CAP_FACTOR * NK / E))
        x_tokens = x.reshape(N, d)
        logits = x_tokens @ router_w + router_b
        probs = jax.nn.softmax(logits, axis=-1)
        vals, idx = jax.lax.top_k(probs, K)
        vals = vals / (jnp.sum(vals, axis=-1, keepdims=True) + 1e-09)
        idx_flat = idx.reshape(NK)
        vals_flat = vals.reshape(NK)
        oh_e = jax.nn.one_hot(idx_flat, E, dtype=x.dtype)
        pos = (jnp.cumsum(oh_e, axis=0) * oh_e).sum(axis=1) - 1
        within = (pos < C).astype(x.dtype)
        pos_c = jnp.clip(pos, 0, C - 1).astype(jnp.int32)
        token_ids = jnp.arange(NK) // K
        x_pair = x_tokens[token_ids] * within[:, None]
        expert_inputs = jnp.zeros((E, C, d), x.dtype).at[idx_flat, pos_c].add(x_pair)
        expert_outputs = jax.vmap(_mlp)(expert_inputs, w_gate, w_up, w_down)
        gathered = expert_outputs[idx_flat, pos_c] * (vals_flat * within)[:, None]
        output_tokens = gathered.reshape(N, K, d).sum(axis=1)
        return x + _mlp(x, sw_gate, sw_up, sw_down) + output_tokens.reshape(b, s, d)
    x = L0_attn_hidden_states
    mod = (_silu(L0_c) @ L0_wmod).reshape(L0_c.shape[0], 6, 1, -1)
    sa, ca, ga, sb, cb, gb = (mod[:, 0], mod[:, 1], mod[:, 2], mod[:, 3], mod[:, 4], mod[:, 5])
    ga = (2 * (ga >= 0) - 1) * jnp.maximum(jnp.abs(ga), 0.25)
    gb = (2 * (gb >= 0) - 1) * jnp.maximum(jnp.abs(gb), 0.25)
    h = _layernorm(x, axis=-1) * (1 + ca) + sa
    x = x + ga * _L0_attn_ref(h, L0_attn_w_q, L0_attn_w_k, L0_attn_w_v, L0_attn_w_o, L0_attn_gate, L0_attn_memory, L0_attn_memory_norm)
    h = _layernorm(x, axis=-1) * (1 + cb) + sb
    x = x + gb * _L0_ffn_ref(h, L0_ffn_gate_w, L0_ffn_w1, L0_ffn_b1, L0_ffn_w2, L0_ffn_b2, L0_ffn_sw1, L0_ffn_sb1, L0_ffn_sw2, L0_ffn_sb2)
    mod = (_silu(L1_c) @ L1_wmod).reshape(L1_c.shape[0], 6, 1, -1)
    sa, ca, ga, sb, cb, gb = (mod[:, 0], mod[:, 1], mod[:, 2], mod[:, 3], mod[:, 4], mod[:, 5])
    ga = (2 * (ga >= 0) - 1) * jnp.maximum(jnp.abs(ga), 0.25)
    gb = (2 * (gb >= 0) - 1) * jnp.maximum(jnp.abs(gb), 0.25)
    h = _layernorm(x, axis=-1) * (1 + ca) + sa
    x = x + ga * _L1_attn_ref(h, L1_attn_W_qkv, L1_attn_b_qkv, L1_attn_W_out, L1_attn_b_out)
    h = _layernorm(x, axis=-1) * (1 + cb) + sb
    x = x + gb * _L1_ffn_ref(h, L1_ffn_router_w, L1_ffn_router_b, L1_ffn_w_gate, L1_ffn_w_up, L1_ffn_w_down, L1_ffn_sw_gate, L1_ffn_sw_up, L1_ffn_sw_down)
    return x

_drawn_inputs = setup_inputs


def setup_inputs(seed=0):
    import zlib

    import numpy as np

    out = dict(_drawn_inputs(seed))
    spreads = {'L1_attn_b_qkv': (0.0, 0.8), 'L1_attn_b_out': (0.0, 0.324), 'L1_ffn_router_b': (0.0, 0.8)}
    factors = {'L0_attn_w_q': 8.0,
     'L0_attn_w_k': 8.0,
     'L0_attn_w_v': 4.854,
     'L0_attn_w_o': 4.929,
     'L0_attn_memory': 8.0,
     'L0_attn_memory_norm': 8.0,
     'L0_ffn_b1': 8.0,
     'L0_ffn_b2': 8.0,
     'L0_ffn_sb1': 8.0,
     'L0_ffn_sb2': 8.0,
     'L1_attn_W_qkv': 8.0,
     'L1_attn_W_out': 8.0,
     'L1_ffn_router_w': 8.0,
     'L1_ffn_w_gate': 8.0,
     'L1_ffn_w_up': 8.0,
     'L1_ffn_w_down': 8.0,
     'L1_ffn_sw_gate': 8.0,
     'L1_ffn_sw_up': 8.0,
     'L1_ffn_sw_down': 8.0}
    for name, (base, spread) in spreads.items():
        noise = np.random.default_rng([zlib.crc32(name.encode()), seed]).standard_normal(out[name].shape)
        drawn = base * np.exp(spread * noise) if base else spread * noise
        out[name] = jnp.asarray(drawn.astype(out[name].dtype))
    for name, factor in factors.items():
        out[name] = (out[name] * factor).astype(out[name].dtype)
    return out
```

```python
from contextlib import ExitStack

import concourse.bass as bass
from concourse import mybir

F32 = mybir.dt.float32
F32R = mybir.dt.float32r
BF16 = mybir.dt.bfloat16
U32 = mybir.dt.uint32
ALU = mybir.AluOpType
ACT = mybir.ActivationFunctionType
AX = mybir.AxisListType

P = 128
B, S, D = 4, 1024, 256
T2 = D // P
NC = S // P
TOK = B * P
NT = B * NC
DM = 64
H0 = 1024
HT0 = H0 // P
NSTEP = 3 * HT0
HEADS, HD = 16, 16
WIN, STEP = 64, 32
WT = WIN + STEP
HC = 5
E1, F1 = 16, 352
CAP = 640
SLOTS = E1 * CAP
ROW = D + 2
LN_EPS = 1e-5
MEM_EPS = 1e-6
FT = [(0, 128), (128, 128), (256, F1 - 256)]


class Steps:

    def __init__(self, names):
        self.names = names if isinstance(names, list) else names.split()

    def __call__(self, c, name):
        return c * len(self.names) + self.names.index(name) + 1


def reach(eng, sem, count):
    if not isinstance(count, int) or count > 0:
        eng.wait_ge(sem, count)


def apart(eng, sem, count, seen):
    if isinstance(count, int):
        reach(eng, sem, count)
    else:
        eng.wait_ge(sem, count)
        eng.sem_inc(seen, 1)


def build(nc, a, out, stop=9):
    ctx = ExitStack()
    with ctx:
        def sb(name, shape, dt=F32, c=None):
            return (c or ctx).enter_context(nc.sbuf_tensor(name, shape, dt))

        def sem(name, c=None):
            return (c or ctx).enter_context(nc.semaphore(name))

        X = ctx.enter_context(nc.psum_tensor("X", [P, 4, 512], F32))
        Y = ctx.enter_context(nc.psum_tensor("Y", [P, 4, 512], F32))
        dram = {
            "rows": nc.dram_tensor("expert_rows", [SLOTS, ROW], F32).ap(),
            "moe": nc.dram_tensor("moe_sum", [B * S, D], F32).ap(),
            "xres": nc.dram_tensor("x_residual", [B * S, D], F32).ap(),
        }

        k = {}
        k["x"] = sb("x", [P, B, NC, ROW])
        k["ident"] = sb("ident", [P, P])
        k["ones"] = sb("ones", [P, P])
        k["mod"] = sb("mod", [P, 2, 6, T2, B])
        k["gbb"] = sb("gbb", [P, T2, B])
        k["scb"] = sb("scb", [P, 2, B, T2])
        k["mhalf"] = sb("mhalf", [P, B])

        with ExitStack() as s:
            w = layer0_weights(nc, sb, s)
            setup(nc, sb, sem, a, k, w, X, Y, dram)
            layer0(nc, sb, sem, k, w, X, Y)
        if stop == 0:
            dump_x(nc, sem, k, out)
            return
        k["logits"] = sb("logits", [P, B, NC, E1])
        k["top"] = sb("top", [P, B, NC, 2])
        k["topi"] = sb("topi", [P, B, NC, 2])
        k["gbrow"] = sb("gbrow", [P, B, D])
        with ExitStack() as s:
            w = layer1_weights(nc, sb, s)
            setup1(nc, sb, sem, a, k, w, X, Y)
            layer1_attention(nc, sb, sem, k, w, X, Y, dram)
        if stop == 1:
            dump_res(nc, sem, dram, out)
            return
        shared_and_routing(nc, sb, sem, a, k, X, Y, dram)
        experts(nc, sb, sem, a, k, X, Y, dram)
        final(nc, sb, sem, k, dram, out)


def dump_x(nc, sem, k, out):
    with ExitStack() as s:
        d = sem("dumped", s)
        block = s.enter_context(nc.Block())

        @block.sync
        def _(sp):
            for b in range(B):
                sp.dma_start(out[b].rearrange("(c p) d -> p c d", p=P), k["x"][:, b, :, 0:D]).then_inc(d, 16)
            sp.wait_ge(d, 16 * B)


def dump_res(nc, sem, dram, out):
    with ExitStack() as s:
        d = sem("dumped", s)
        block = s.enter_context(nc.Block())

        @block.sync
        def _(sp):
            sp.dma_start(out.rearrange("b s d -> (b s) d"), dram["xres"]).then_inc(d, 16)
            sp.wait_ge(d, 16)


def layer0_weights(nc, sb, s):
    w = {}
    for n, shape in (("w1h", [P, 3, T2, H0]), ("w1l", [P, 3, T2, H0]), ("w2h", [P, 3, HT0, D]), ("w2l", [P, 3, HT0, D])):
        w[n] = sb(n, shape, F32R, s)
    w["b1"] = sb("b1", [P, 3, HT0], F32, s)
    w["gwd"] = sb("gwd", [P, T2, P], F32, s)
    w["wqkT"] = sb("wqkT", [P, T2, P], F32, s)
    w["wvT"] = sb("wvT", [P, T2, DM], F32, s)
    w["wog"] = sb("wog", [DM, B, D], F32, s)
    w["maug"] = sb("maug", [DM, DM + 1], F32, s)
    w["coef"] = sb("coef", [P, 2, B], F32, s)
    w["causal"] = sb("causal", [P, P], F32, s)
    return w


def setup(nc, sb, sem, a, k, w, X, Y, dram):
    with ExitStack() as s:
        t = lambda n, shape, dt=F32: sb(n, shape, dt, s)
        zeros = t("zeros", [P, CAP * ROW // P])
        vrows = t("vrows", [VROWS, P])
        wm = t("wm", [P, 2, T2, 6 * D])
        qk_raw, v_raw, o_raw, woT = t("qk_raw", [P, D]), t("v_raw", [DM, D]), t("o_raw", [P, T2, DM]), t("woT", [DM, D])
        gw, gwd1 = t("gw", [P, 2, T2]), t("gwd1", [P, T2])
        b2, b2s = t("b2", [P, 3, T2]), t("b2s", [P, T2])
        gcol, mn, gv = t("gcol", [P, 1]), t("mn", [P, DM]), t("gv", [P, 4])
        sign = t("sign", [P, B * D])
        garow = t("garow", [DM, B, D])
        raw = t("raw", [P, 2, 2048])

        x_in, small_in, wm_in = (sem(n, s) for n in ("x_in", "small_in", "wm_in"))
        raw_in = [sem(f"raw_in{i}", s) for i in range(2)]
        zero_out = sem("zero_out", s)
        pool_did, act_did, vec_did, pe_did = (sem(n, s) for n in ("setup_pool", "setup_act", "setup_vec", "setup_pe"))
        V = Steps(["ones", "zeros", "gwdiff", "gwd", "b2a", "b2b", "scale1", "gbge", "gbsign", "gbabs", "gb", "gbb",
                   "nsum", "flag", "den", "g", "gflag", "omg", "coef",
                   "gage", "gasign", "gaabs", "ga", "wog"] + [f"lo{i}" for i in range(6)])
        A = Steps(["silu", "b1", "b2", "gw", "eg", "qkT", "vT", "woT", "mod"] + [f"hi{i}" for i in range(6)])
        G = Steps("mhalf ident0 ident causal0 causal")
        T = Steps("wT mod garow")
        block = s.enter_context(nc.Block())

        srcs = []
        for e in range(3):
            w1 = a["L0_ffn_sw1"] if e == 0 else a["L0_ffn_w1"][e - 1]
            w2 = a["L0_ffn_sw2"] if e == 0 else a["L0_ffn_w2"][e - 1]
            srcs.append((w1.rearrange("(t p) n -> p t n", p=P), w["w1h"][:, e], w["w1l"][:, e], H0))
            srcs.append((w2.rearrange("(h p) n -> p h n", p=P), w["w2h"][:, e], w["w2l"][:, e], D))
        raws = [raw[:, i % 2, :].rearrange("p (t n) -> p t n", n=srcs[i][3]) for i in range(6)]

        @block.sync
        def _(sp):
            for l in range(2):
                sp.dma_start(wm[:, l], a[f"L{l}_wmod"].rearrange("(t p) n -> p t n", p=P)).then_inc(wm_in, 16)
            for c in range(NC):
                sp.dma_start(k["x"][:, :, c, 0:D],
                             a["L0_attn_hidden_states"].rearrange("b (c p) d -> p b c d", p=P)[:, :, c, :]).then_inc(x_in, 16)
            for i, (src, _, _, n) in enumerate(srcs):
                if i >= 2:
                    sp.wait_ge(vec_did, V(0, f"lo{i - 2}"))
                sp.dma_start(raws[i], src).then_inc(raw_in[i % 2], 16)
            sp.wait_ge(x_in, 16 * NC)

        @block.gpsimd
        def _(pool):
            pool.memset(k["mhalf"][:], -0.5).then_inc(pool_did, 1)
            pool.memset(k["ident"][:], 0.0).then_inc(pool_did, 1)
            pool.wait_ge(pool_did, G(0, "ident0"))
            pool.affine_select(out=k["ident"][:], in_=k["ident"][:], compare_op=ALU.not_equal, fill=1.0,
                               base=0, pattern=[[-1, P]], channel_multiplier=1).then_inc(pool_did, 1)
            pool.memset(w["causal"][:], 1.0).then_inc(pool_did, 1)
            pool.wait_ge(pool_did, G(0, "causal0"))
            pool.affine_select(out=w["causal"][:], in_=w["causal"][:], compare_op=ALU.is_ge, fill=0.0,
                               base=0, pattern=[[1, P]], channel_multiplier=-1).then_inc(pool_did, 1)

        @block.scalar
        def _(act):
            n = 0
            for dst, src in (
                (qk_raw[0:DM, :], a["L0_attn_w_q"]), (qk_raw[DM:P, :], a["L0_attn_w_k"]), (v_raw[:], a["L0_attn_w_v"]),
                (o_raw[:], a["L0_attn_w_o"].rearrange("(t p) m -> p t m", p=P)),
                (w["maug"][:, 0:DM], a["L0_attn_memory"]),
                (w["maug"][:, DM:DM + 1], a["L0_attn_memory_norm"].rearrange("(p o) -> p o", o=1)),
                (mn[:], a["L0_attn_memory_norm"].partition_broadcast(P)),
                (gcol[:], a["L0_attn_gate"].partition_broadcast(P)),
                (vrows[0:8], a["L0_ffn_sb1"].rearrange("(h p) -> h p", p=P)),
                (vrows[8:24], a["L0_ffn_b1"].rearrange("e (h p) -> (e h) p", p=P)),
                (vrows[24:26], a["L0_ffn_sb2"].rearrange("(t p) -> t p", p=P)),
                (vrows[26:30], a["L0_ffn_b2"].rearrange("e (t p) -> (e t) p", p=P)),
                (vrows[30:38], a["L0_c"].rearrange("b (t p) -> (b t) p", p=P)),
                (vrows[38:46], a["L1_c"].rearrange("b (t p) -> (b t) p", p=P)),
                (vrows[46:50], a["L0_ffn_gate_w"].rearrange("e (t p) -> (e t) p", p=P)),
            ):
                act.dma_start(dst, src).then_inc(small_in, 16)
                n += 16
            assert n == SMALL_LOADS * 16
            act.wait_ge(vec_did, V(0, "zeros"))
            for e in range(E1):
                act.dma_start(dram["rows"][e * CAP:(e + 1) * CAP].rearrange("(p q) r -> p (q r)", p=P), zeros[:]).then_inc(zero_out, 16)
            act.wait_ge(pe_did, T(0, "wT"))
            nc.scalar.activation(k["scb"][:], X[:, 3, 30:46].rearrange("p (l b t) -> p l b t", l=2, b=B), ACT.Silu).then_inc(act_did, 1)
            nc.scalar.copy(w["b1"][:], X[:, 3, 0:24].rearrange("p (e h) -> p e h", e=3)).then_inc(act_did, 1)
            nc.scalar.copy(b2[:], X[:, 3, 24:30].rearrange("p (e t) -> p e t", e=3)).then_inc(act_did, 1)
            nc.scalar.copy(gw[:], X[:, 3, 46:50].rearrange("p (e t) -> p e t", e=2)).then_inc(act_did, 1)
            nc.scalar.activation(gv[:, 0:1], gcol[:], ACT.Exp, scale=-1.0).then_inc(act_did, 1)
            nc.scalar.copy(w["wqkT"][:], X[:, 0, 0:2 * P].rearrange("p (t n) -> p t n", t=T2)).then_inc(act_did, 1)
            nc.scalar.copy(w["wvT"][:], X[:, 1, 0:2 * DM].rearrange("p (t n) -> p t n", t=T2)).then_inc(act_did, 1)
            nc.scalar.copy(woT[:], X[0:DM, 2, 0:D]).then_inc(act_did, 1)
            act.wait_ge(pe_did, T(0, "mod"))
            nc.scalar.copy(k["mod"][:], X[:, 3, 64:160].rearrange("p (l j t b) -> p l j t b", l=2, j=6, t=T2)).then_inc(act_did, 1)
            for i, (_, hi, _, n) in enumerate(srcs):
                act.wait_ge(raw_in[i % 2], 16 * (i // 2 + 1))
                nc.scalar.copy(hi, raws[i]).then_inc(act_did, 1)
            act.wait_ge(zero_out, 16 * E1)

        @block.tensor
        def _(pe):
            pe.wait_ge(pool_did, G(0, "ident"))
            pe.wait_ge(small_in, 16 * SMALL_LOADS)
            pe.transpose(X[:, 3, 0:VROWS], vrows[:], k["ident"][0:VROWS, 0:VROWS])
            for t_ in range(T2):
                pe.transpose(X[:, 0, t_ * P:(t_ + 1) * P], qk_raw[:, t_ * P:(t_ + 1) * P], k["ident"][:])
                pe.transpose(X[:, 1, t_ * DM:(t_ + 1) * DM], v_raw[:, t_ * P:(t_ + 1) * P], k["ident"][0:DM, 0:DM])
                ins = pe.transpose(X[0:DM, 2, t_ * P:(t_ + 1) * P], o_raw[:, t_, :], k["ident"][:])
            ins.then_inc(pe_did, 1)
            pe.wait_ge(act_did, A(0, "gw"))
            pe.wait_ge(wm_in, 32)
            for l in range(2):
                for jt in range(12):
                    o = X[:, 3, 64 + 48 * l + 4 * jt:64 + 48 * l + 4 * jt + 4]
                    for t_ in range(T2):
                        ins = pe.matmul(o, wm[:, l, t_, jt * P:(jt + 1) * P], k["scb"][:, l, :, t_],
                                        start=t_ == 0, stop=t_ == T2 - 1)
            ins.then_inc(pe_did, 1)
            mod_rows(pe, Y, wm[:, 0], k["scb"][:, 0], 2, DM).then_inc(pe_did, 1)

        @block.vector
        def _(v):
            v.memset(k["ones"][:], 1.0).then_inc(vec_did, 1)
            v.memset(zeros[:], 0.0).then_inc(vec_did, 1)
            v.wait_ge(act_did, A(0, "gw"))
            v.tensor_tensor(gwd1[:], gw[:, 1, :], gw[:, 0, :], ALU.subtract).then_inc(vec_did, 1)
            v.wait_ge(vec_did, V(0, "gwdiff"))
            for t_ in range(T2):
                ins = v.tensor_scalar(w["gwd"][:, t_, :], k["ones"][:], gwd1[:, t_:t_ + 1], None, ALU.mult)
            ins.then_inc(vec_did, 1)
            v.tensor_tensor(b2s[:], b2[:, 1], b2[:, 2], ALU.add).then_inc(vec_did, 1)
            v.wait_ge(vec_did, V(0, "b2a"))
            v.tensor_tensor(b2s[:], b2s[:], b2[:, 0], ALU.add).then_inc(vec_did, 1)
            v.wait_ge(act_did, A(0, "mod"))
            mod = k["mod"]
            for l in range(2):
                ins = v.tensor_scalar(mod[:, l, 1:5:3], mod[:, l, 1:5:3], 1.0, None, ALU.add)
            ins.then_inc(vec_did, 1)
            gate(v, vec_did, V, ("gbge", "gbsign", "gbabs", "gb"), mod[:, 0, 5].rearrange("p t b -> p (t b)"),
                 mod[:, 0, 2].rearrange("p t b -> p (t b)"), sign[:, 0:8])
            v.wait_ge(vec_did, V(0, "gb"))
            v.tensor_tensor(k["gbb"][:], mod[:, 0, 2], b2s[:].unsqueeze(2).to_broadcast([P, T2, B]), ALU.mult).then_inc(vec_did, 1)
            v.wait_ge(small_in, 16 * SMALL_LOADS)
            v.reduce_sum(gv[:, 1:2], mn[:], AX.X).then_inc(vec_did, 1)
            v.wait_ge(vec_did, V(0, "nsum"))
            v.tensor_scalar(gv[:, 1:2], gv[:, 1:2], MEM_EPS, None, ALU.is_ge).then_inc(vec_did, 1)
            v.wait_ge(act_did, A(0, "eg"))
            v.tensor_scalar(gv[:, 2:3], gv[:, 0:1], 1.0, None, ALU.add).then_inc(vec_did, 1)
            v.wait_ge(vec_did, V(0, "den"))
            v.reciprocal(gv[:, 2:3], gv[:, 2:3]).then_inc(vec_did, 1)
            v.wait_ge(vec_did, V(0, "g"))
            v.tensor_tensor(gv[:, 1:2], gv[:, 1:2], gv[:, 2:3], ALU.mult).then_inc(vec_did, 1)
            v.tensor_scalar(gv[:, 3:4], gv[:, 2:3], -1.0, 1.0, ALU.mult, ALU.add).then_inc(vec_did, 1)
            v.wait_ge(vec_did, V(0, "omg"))
            v.tensor_scalar(w["coef"][:, 0, :], k["ones"][:, 0:B], gv[:, 1:2], None, ALU.mult)
            v.tensor_scalar(w["coef"][:, 1, :], k["ones"][:, 0:B], gv[:, 3:4], None, ALU.mult).then_inc(vec_did, 1)
            v.wait_ge(pe_did, T(0, "garow"))
            gate(v, vec_did, V, ("gage", "gasign", "gaabs", "ga"), Y[0:DM, 0:2].rearrange("p a n -> p (a n)"),
                 garow[:].rearrange("p b d -> p (b d)"), sign[0:DM, :])
            v.wait_ge(vec_did, V(0, "ga"))
            v.wait_ge(act_did, A(0, "woT"))
            v.tensor_tensor(w["wog"][:], garow[:], woT[:].unsqueeze(1).to_broadcast([DM, B, D]), ALU.mult).then_inc(vec_did, 1)
            for i, (_, hi, lo, n) in enumerate(srcs):
                v.wait_ge(act_did, A(0, f"hi{i}"))
                v.tensor_tensor(lo, raws[i], hi.bitcast(F32), ALU.subtract).then_inc(vec_did, 1)


SMALL_LOADS = 15
VROWS = 50


def mod_rows(pe, Y, wm, scb, j, m):
    for b in range(B):
        for t_ in range(T2):
            ins = pe.matmul(Y[0:m, b // 2, (b % 2) * D:(b % 2 + 1) * D], scb[:, b, t_:t_ + 1].to_broadcast([P, m]),
                            wm[:, t_, j * D:(j + 1) * D], start=t_ == 0, stop=t_ == T2 - 1)
    return ins


def gate(v, done, V, steps, src, dst, sign):
    v.tensor_scalar(sign, src, 0.0, None, ALU.is_ge).then_inc(done, 1)
    v.wait_ge(done, V(0, steps[0]))
    v.tensor_scalar(sign, sign, 2.0, -1.0, ALU.mult, ALU.add).then_inc(done, 1)
    v.wait_ge(done, V(0, steps[1]))
    v.tensor_tensor(dst, src, sign, ALU.mult).then_inc(done, 1)
    v.wait_ge(done, V(0, steps[2]))
    v.scalar_tensor_tensor(out=dst, in0=dst, scalar=0.25, in1=sign, op0=ALU.max, op1=ALU.mult).then_inc(done, 1)


LN_VEC = "stats aggr eps sq sqv half rstd xn".split()
LN_POOL = ["pow"]


class Norm:

    def __init__(self, sb, sem, s, name):
        self.st = sb(f"{name}_stats", [P, B, 6], F32, s)
        self.mv = sb(f"{name}_meanvar", [P, B, 2], F32, s)
        self.ve = sb(f"{name}_vareps", [P, B], F32, s)
        self.y = sb(f"{name}_y", [P, B], F32, s)
        self.q = sb(f"{name}_q", [P, B], F32, s)
        self.seen = sem(f"{name}_seen", s)


def norm_vector(v, ln, done, V, c, x, xn, pool, pow_count, free, free_count):
    apart(v, done, V(c - 1, "xn"), ln.seen)
    for b in range(B):
        ins = v.bn_stats(ln.st[:, b, :], x[:, b, c, 0:D])
    ins.then_inc(done, 1)
    apart(v, done, V(c, "stats"), ln.seen)
    for b in range(B):
        ins = v.bn_aggr(ln.mv[:, b, :], ln.st[:, b, :])
    ins.then_inc(done, 1)
    v.wait_ge(done, V(c, "aggr"))
    v.tensor_scalar(ln.ve[:], ln.mv[:, :, 1], LN_EPS, None, ALU.add).then_inc(done, 1)
    v.wait_ge(pool, pow_count)
    v.tensor_tensor(ln.q[:], ln.y[:], ln.y[:], ALU.mult).then_inc(done, 1)
    v.wait_ge(done, V(c, "sq"))
    v.tensor_tensor(ln.q[:], ln.q[:], ln.ve[:], ALU.mult).then_inc(done, 1)
    v.wait_ge(done, V(c, "sqv"))
    v.tensor_scalar(ln.q[:], ln.q[:], -0.5, 1.5, ALU.mult, ALU.add).then_inc(done, 1)
    v.wait_ge(done, V(c, "half"))
    v.tensor_tensor(ln.y[:], ln.y[:], ln.q[:], ALU.mult).then_inc(done, 1)
    v.wait_ge(done, V(c, "rstd"))
    reach(v, free, free_count)
    for b in range(B):
        ins = v.tensor_scalar(xn[:, b, :], x[:, b, c, 0:D], ln.mv[:, b, 0:1], ln.y[:, b:b + 1], ALU.subtract, ALU.mult)
    ins.then_inc(done, 1)


def norm_pool(pool, ln, done, mhalf, vec, vec_count):
    pool.wait_ge(vec, vec_count)
    pool.tensor_tensor(ln.y[:], ln.ve[:], mhalf[:], ALU.pow).then_inc(done, 1)


def transpose_chunk(pe, X, src, ident):
    for b in range(B):
        for t in range(T2):
            ins = pe.transpose(X[:, t, b * P:(b + 1) * P], src[:, b, t * P:(t + 1) * P], ident[:])
    return ins


def modulate(act, dst, X, mod, scale, shift):
    for b in range(B):
        for t in range(T2):
            ins = act.activation(dst[:, t, b * P:(b + 1) * P], X[:, t, b * P:(b + 1) * P], ACT.Identity,
                                 bias=mod[:, shift, t, b:b + 1], scale=mod[:, scale, t, b:b + 1])
    return ins


def product3(pe, out, wh, wl, xh, xl, start, stop):
    pe.matmul(out, wh, xh, start=start, stop=False)
    pe.matmul(out, wh, xl, start=False, stop=False)
    return pe.matmul(out, wl, xh, start=False, stop=stop)


def layer0(nc, sb, sem, k, w, X, Y):
    with ExitStack() as s:
        t = lambda n, shape, dt=F32: sb(n, shape, dt, s)
        x, mod, ident = k["x"], k["mod"][:, 0], k["ident"]
        lna, lnf = Norm(sb, sem, s, "lna"), Norm(sb, sem, s, "lnf")
        xn = t("xn", [P, B, D])
        hT = t("a_hT", [P, T2, TOK])
        ex, sg = t("a_exp", [DM, 2, TOK]), t("a_sigma", [DM, 2, TOK])
        vaug = t("a_v", [P, B, DM + 1])
        amask = t("a_scores", [P, B, P])
        ktok = t("a_ktok", [P, B, DM])
        state = t("a_state", [DM, B, DM + 1])
        rd = t("a_rden", [P, 2, B])
        memn, comb = t("a_mem", [P, B, DM]), t("a_comb", [P, B, DM])
        cT = t("a_combT", [DM, TOK])
        hF = t("f_h", [P, T2, TOK])
        hS = t("f_hS", [P, 2, T2, TOK], F32R)
        hE = t("f_hE", [P, 2, T2, TOK], F32R)
        masks = t("f_masks", [P, 2, TOK], BF16)
        hid = t("f_hid", [P, 2, TOK])
        hidh, hidl = t("f_hidh", [P, 3, TOK], F32R), t("f_hidl", [P, 3, TOK], F32R)
        y = t("f_y", [P, T2, TOK])

        av, ap, aa, at = (sem(n, s) for n in ("attn_vec", "attn_pool", "attn_act", "attn_pe"))
        fv, fp, fa, ft = (sem(n, s) for n in ("ffn_vec", "ffn_pool", "ffn_act", "ffn_pe"))
        AV = Steps(LN_VEC + "sigma masked ktok state den recip coef mem loc comb x".split())
        AP = Steps(LN_POOL)
        AA = Steps("h neg relu exp v combT")
        AT = Steps("xT qk v scores kT mem loc state combT out")
        FV = Steps(LN_VEC + ["hi", "lo", "mask0", "mask1"] + [f"lo{i}" for i in range(NSTEP)] + ["x"])
        FP = Steps(LN_POOL + ["e0h", "e0l", "e1h", "e1l"])
        FA = Steps(["h"] + [n for i in range(NSTEP) for n in (f"relu{i}", f"hi{i}")] + ["y"])
        names = ["xT", "gate"]
        for i in range(NSTEP + 2):
            names += [f"up{i}"] * (i < NSTEP) + [f"down{i - 2}"] * (i >= 2)
        FT_ = Steps(names + ["yT"])
        init, seen = sem("layer0_init", s), sem("attn_seen_pe", s)
        block = s.enter_context(nc.Block())
        X2 = X[:, 0:2].rearrange("p a n -> p (a n)")

        def chunks(eng, *stages):
            for f in stages:
                f(0)
            with eng.Fori(1, NC) as c:
                for f in stages:
                    f(c)

        @block.gpsimd
        def _(pool):
            def attention(c):
                norm_pool(pool, lna, ap, k["mhalf"], av, AV(c, "eps"))

            def ffn(c):
                norm_pool(pool, lnf, fp, k["mhalf"], fv, FV(c, "eps"))
                pool.wait_ge(fv, FV(c, "mask1"))
                reach(pool, ft, FT_(c - 1, f"up{2 * HT0 - 1}"))
                for i, name in ((0, "e0h"), (1, "e0l")):
                    pool.tensor_tensor(hE[:, i], hS[:, i].bitcast(F32), masks[:, 0:1].to_broadcast([P, T2, TOK]), ALU.mult).then_inc(fp, 1)
                pool.wait_ge(ft, FT_(c, f"up{HT0 - 1}"))
                pool.wait_ge(fp, FP(c, "e0l"))
                for i in (0, 1):
                    pool.tensor_tensor(hS[:, i], hS[:, i].bitcast(F32), masks[:, 1:2].to_broadcast([P, T2, TOK]), ALU.mult).then_inc(fp, 1)
            chunks(pool, attention, ffn)

        @block.scalar
        def _(act):
            def attention(c):
                act.wait_ge(at, AT(c, "xT"))
                modulate(act, hT, X, mod, 1, 0).then_inc(aa, 1)
                act.wait_ge(at, AT(c, "qk"))
                qk = X[0:DM, 2:4]
                act.activation(ex[:], qk, ACT.Relu, scale=-1.0).then_inc(aa, 1)
                act.activation(sg[:], qk, ACT.Relu).then_inc(aa, 1)
                act.wait_ge(aa, AA(c, "neg"))
                act.activation(ex[:], ex[:], ACT.Exp, scale=-1.0).then_inc(aa, 1)
                act.wait_ge(at, AT(c, "v"))
                act.wait_ge(init, 2)
                act.copy(vaug[:, :, 0:DM], X[:, 0, 0:B * DM].rearrange("p (b d) -> p b d", b=B)).then_inc(aa, 1)
                act.wait_ge(at, AT(c, "combT"))
                act.copy(cT[:], X[0:DM, 2]).then_inc(aa, 1)

            def ffn(c):
                act.wait_ge(ft, FT_(c, "xT"))
                modulate(act, hF, X, mod, 4, 3).then_inc(fa, 1)
                for i in range(NSTEP):
                    e, h = divmod(i, HT0)
                    act.wait_ge(ft, FT_(c, f"up{i}"))
                    if i >= 2:
                        act.wait_ge(fv, FV(c, f"lo{i - 2}"))
                    act.activation(hid[:, i % 2], Y[:, i % 2], ACT.Relu, bias=w["b1"][:, e, h:h + 1]).then_inc(fa, 1)
                    if i >= 3:
                        act.wait_ge(ft, FT_(c, f"down{i - 3}"))
                    act.wait_ge(fa, FA(c, f"relu{i}"))
                    act.copy(hidh[:, i % 3], hid[:, i % 2]).then_inc(fa, 1)
                act.wait_ge(ft, FT_(c, f"down{NSTEP - 1}"))
                for b in range(B):
                    for t_ in range(T2):
                        ins = act.activation(y[:, t_, b * P:(b + 1) * P], Y[:, 2 + t_, b * P:(b + 1) * P], ACT.Identity,
                                             bias=k["gbb"][:, t_, b:b + 1], scale=mod[:, 2, t_, b:b + 1])
                ins.then_inc(fa, 1)
            chunks(act, attention, ffn)

        @block.vector
        def _(v):
            v.memset(state[:], 0.0).then_inc(init, 1)
            v.memset(vaug[:, :, DM:DM + 1], 1.0).then_inc(init, 1)

            def attention(c):
                norm_vector(v, lna, av, AV, c, x, xn, ap, AP(c, "pow"), ft, FT_(c - 1, "xT"))
                v.wait_ge(aa, AA(c, "exp"))
                v.tensor_tensor(sg[:], ex[:], sg[:], ALU.add).then_inc(av, 1)
                v.wait_ge(at, AT(c, "scores"))
                v.tensor_tensor(amask[:], X[:, 1].rearrange("p (b q) -> p b q", b=B),
                                w["causal"][:].unsqueeze(1).to_broadcast([P, B, P]), ALU.mult).then_inc(av, 1)
                v.wait_ge(at, AT(c, "kT"))
                v.tensor_copy(ktok[:], X[:, 2, 0:B * DM].rearrange("p (b d) -> p b d", b=B)).then_inc(av, 1)
                v.wait_ge(at, AT(c, "state"))
                v.wait_ge(init, 2)
                v.tensor_tensor(state[:], state[:], X[0:DM, 1, 0:B * (DM + 1)].rearrange("p (b d) -> p b d", b=B), ALU.add).then_inc(av, 1)
                mem = X[:, 3, 0:B * (DM + 1)].rearrange("p (b d) -> p b d", b=B)
                loc = X[:, 0, 0:B * (DM + 1)].rearrange("p (b d) -> p b d", b=B)
                v.tensor_scalar(rd[:, 0, :], mem[:, :, DM], MEM_EPS, None, ALU.max)
                v.tensor_scalar(rd[:, 1, :], loc[:, :, DM], MEM_EPS, None, ALU.max).then_inc(av, 1)
                v.wait_ge(av, AV(c, "den"))
                v.reciprocal(rd[:], rd[:]).then_inc(av, 1)
                v.wait_ge(av, AV(c, "recip"))
                v.tensor_tensor(rd[:], rd[:], w["coef"][:], ALU.mult).then_inc(av, 1)
                v.wait_ge(av, AV(c, "coef"))
                v.tensor_tensor(memn[:], mem[:, :, 0:DM], rd[:, 0, :].unsqueeze(2).to_broadcast([P, B, DM]), ALU.mult).then_inc(av, 1)
                v.tensor_tensor(comb[:], loc[:, :, 0:DM], rd[:, 1, :].unsqueeze(2).to_broadcast([P, B, DM]), ALU.mult).then_inc(av, 1)
                v.wait_ge(av, AV(c, "loc"))
                v.tensor_tensor(comb[:], comb[:], memn[:], ALU.add).then_inc(av, 1)
                v.wait_ge(at, AT(c, "out"))
                v.tensor_tensor(x[:, :, c, 0:D], x[:, :, c, 0:D], X2.rearrange("p (b d) -> p b d", b=B), ALU.add).then_inc(av, 1)

            def ffn(c):
                apart(v, av, AV(c, "x"), lnf.seen)
                norm_vector(v, lnf, fv, FV, c, x, xn, fp, FP(c, "pow"), at, AT(c, "xT"))
                v.wait_ge(fa, FA(c, "h"))
                v.tensor_copy(hS[:, 0], hF[:]).then_inc(fv, 1)
                v.wait_ge(fv, FV(c, "hi"))
                v.tensor_tensor(hS[:, 1], hF[:], hS[:, 0].bitcast(F32), ALU.subtract).then_inc(fv, 1)
                v.wait_ge(ft, FT_(c, "gate"))
                v.tensor_scalar(masks[:, 0, :], X[:, 2], 0.0, None, ALU.is_le).then_inc(fv, 1)
                v.tensor_scalar(masks[:, 1, :], X[:, 2], 0.0, None, ALU.is_gt).then_inc(fv, 1)
                for i in range(NSTEP):
                    v.wait_ge(fa, FA(c, f"hi{i}"))
                    v.tensor_tensor(hidl[:, i % 3], hid[:, i % 2], hidh[:, i % 3].bitcast(F32), ALU.subtract).then_inc(fv, 1)
                v.wait_ge(ft, FT_(c, "yT"))
                v.tensor_tensor(x[:, :, c, 0:D], x[:, :, c, 0:D], X2.rearrange("p (b d) -> p b d", b=B), ALU.add).then_inc(fv, 1)
            chunks(v, attention, ffn)

        @block.tensor
        def _(pe):
            bs = [slice(b * P, (b + 1) * P) for b in range(B)]
            aug = [slice(b * (DM + 1), (b + 1) * (DM + 1)) for b in range(B)]
            dm = [slice(b * DM, (b + 1) * DM) for b in range(B)]

            def attention(c):
                pe.wait_ge(av, AV(c, "xn"))
                reach(pe, fv, FV(c - 1, "x"))
                transpose_chunk(pe, X, xn, ident).then_inc(at, 1)
                pe.wait_ge(aa, AA(c, "h"))
                for i in range(2):
                    for t_ in range(T2):
                        ins = pe.matmul(X[0:DM, 2 + i], w["wqkT"][:, t_, i * DM:(i + 1) * DM], hT[:, t_, :], start=t_ == 0, stop=t_ == T2 - 1)
                ins.then_inc(at, 1)
                for b in range(B):
                    for t_ in range(T2):
                        ins = pe.matmul(X[:, 0, dm[b]], hT[:, t_, bs[b]], w["wvT"][:, t_, :], start=t_ == 0, stop=t_ == T2 - 1)
                ins.then_inc(at, 1)
                pe.wait_ge(av, AV(c, "sigma"))
                for b in range(B):
                    ins = pe.matmul(X[:, 1, bs[b]], sg[:, 1, bs[b]], sg[:, 0, bs[b]], start=True, stop=True)
                ins.then_inc(at, 1)
                for b in range(B):
                    ins = pe.transpose(X[:, 2, dm[b]], sg[:, 1, bs[b]], ident[0:DM, 0:DM])
                ins.then_inc(at, 1)
                for b in range(B):
                    ins = pe.matmul(X[:, 3, aug[b]], sg[:, 0, bs[b]], w["maug"][:], start=True, stop=True)
                ins.then_inc(at, 1)
                pe.wait_ge(aa, AA(c, "v"))
                pe.wait_ge(av, AV(c, "masked"))
                for b in range(B):
                    pe.matmul(X[:, 0, aug[b]], amask[:, b, :], vaug[:, b, :], start=True, stop=False)
                    ins = pe.matmul(X[:, 0, aug[b]], sg[:, 0, bs[b]], state[:, b, :], start=False, stop=True)
                ins.then_inc(at, 1)
                pe.wait_ge(av, AV(c, "ktok"))
                for b in range(B):
                    ins = pe.matmul(X[0:DM, 1, aug[b]], ktok[:, b, :], vaug[:, b, :], start=True, stop=True)
                ins.then_inc(at, 1)
                apart(pe, av, AV(c, "comb"), seen)
                for b in range(B):
                    ins = pe.transpose(X[0:DM, 2, bs[b]], comb[:, b, :], ident[:])
                ins.then_inc(at, 1)
                pe.wait_ge(aa, AA(c, "combT"))
                for b in range(B):
                    ins = pe.matmul(X2[:, b * D:(b + 1) * D], cT[:, bs[b]], w["wog"][:, b, :], start=True, stop=True)
                ins.then_inc(at, 1)

            def up(c, i):
                e, h = divmod(i, HT0)
                hin = hE if e == 1 else hS
                if h == 0:
                    if e == 0:
                        pe.wait_ge(fv, FV(c, "lo"))
                    else:
                        pe.wait_ge(fp, FP(c, f"e{e - 1}l"))
                if i >= 2:
                    pe.wait_ge(fa, FA(c, f"relu{i - 2}"))
                for t_ in range(T2):
                    cols = slice(h * P, (h + 1) * P)
                    ins = product3(pe, Y[:, i % 2], w["w1h"][:, e, t_, cols], w["w1l"][:, e, t_, cols],
                                   hin[:, 0, t_, :], hin[:, 1, t_, :], t_ == 0, t_ == T2 - 1)
                ins.then_inc(ft, 1)

            def down(c, i):
                e, h = divmod(i, HT0)
                pe.wait_ge(fv, FV(c, f"lo{i}"))
                if i == 0:
                    reach(pe, fa, FA(c - 1, "y"))
                for t_ in range(T2):
                    cols = slice(t_ * P, (t_ + 1) * P)
                    ins = product3(pe, Y[:, 2 + t_], w["w2h"][:, e, h, cols], w["w2l"][:, e, h, cols],
                                   hidh[:, i % 3], hidl[:, i % 3], i == 0, i == NSTEP - 1)
                ins.then_inc(ft, 1)

            def ffn(c):
                pe.wait_ge(fv, FV(c, "xn"))
                pe.wait_ge(av, AV(c, "x"))
                transpose_chunk(pe, X, xn, ident).then_inc(ft, 1)
                pe.wait_ge(fa, FA(c, "h"))
                for t_ in range(T2):
                    ins = pe.matmul(X[:, 2], w["gwd"][:, t_, :], hF[:, t_, :], start=t_ == 0, stop=t_ == T2 - 1)
                ins.then_inc(ft, 1)
                for i in range(NSTEP + 2):
                    if i < NSTEP:
                        up(c, i)
                    if i >= 2:
                        down(c, i - 2)
                pe.wait_ge(fa, FA(c, "y"))
                for b in range(B):
                    for t_ in range(T2):
                        ins = pe.transpose(X2[:, b * D + t_ * P:b * D + (t_ + 1) * P], y[:, t_, bs[b]], ident[:])
                ins.then_inc(ft, 1)
            chunks(pe, attention, ffn)


def layer1_weights(nc, sb, s):
    w = {}
    w["qkvh"], w["qkvl"] = sb("qkvh", [P, T2, 3 * D], F32R, s), sb("qkvl", [P, T2, 3 * D], F32R, s)
    w["bqk"] = sb("bqk", [P, 2 * D], F32, s)
    w["bv"] = sb("bv", [P, T2], F32, s)
    w["wog"] = sb("wog1", [P, B, T2, D], F32, s)
    w["bog"] = sb("bog1", [P, B, D], F32, s)
    w["cb"], w["sb"] = sb("cbrow", [P, B, D], F32, s), sb("sbrow", [P, B, D], F32, s)
    w["rw"], w["rb"] = sb("rw", [P, T2, E1], F32, s), sb("rb", [P, E1], F32, s)
    w["hm"] = sb("headmask", [P, 8], F32, s)
    w["par"] = sb("parity", [P, 2], F32, s)
    return w


def setup1(nc, sb, sem, a, k, w, X, Y):
    with ExitStack() as s:
        t = lambda n, shape, dt=F32: sb(n, shape, dt, s)
        wm = t("wm1", [P, T2, 6 * D])
        qkv, wout, bout = t("qkv_raw", [P, T2, 3 * D]), t("wout_raw", [P, T2, D]), t("bout_raw", [P, D])
        sign, garow = t("sign1", [P, B * D]), t("garow1", [P, B, D])
        loads = sem("loads1", s)
        act_did, vec_did, pe_did = (sem(n, s) for n in ("setup1_act", "setup1_vec", "setup1_pe"))
        V = Steps("hm par0 par1 lo gage gasign gaabs ga wog bog gbge gbsign gbabs gb")
        A = Steps("hi sb cb")
        T = Steps("ga sb cb gb")
        N = 9 * 16
        block = s.enter_context(nc.Block())

        @block.sync
        def _(sp):
            for dst, src in (
                (wm[:], a["L1_wmod"].rearrange("(t p) n -> p t n", p=P)),
                (qkv[:], a["L1_attn_W_qkv"].rearrange("(t p) n -> p t n", p=P)),
                (w["bqk"][:], a["L1_attn_b_qkv"][0:2 * D].partition_broadcast(P)),
                (w["bv"][:, 0:1], a["L1_attn_b_qkv"][2 * D:2 * D + P].rearrange("(p o) -> p o", o=1)),
                (w["bv"][:, 1:2], a["L1_attn_b_qkv"][2 * D + P:3 * D].rearrange("(p o) -> p o", o=1)),
                (wout[:], a["L1_attn_W_out"].rearrange("(t p) n -> p t n", p=P)),
                (bout[:], a["L1_attn_b_out"].partition_broadcast(P)),
                (w["rw"][:], a["L1_ffn_router_w"].rearrange("(t p) n -> p t n", p=P)),
                (w["rb"][:], a["L1_ffn_router_b"].partition_broadcast(P)),
            ):
                sp.dma_start(dst, src).then_inc(loads, 16)
            sp.wait_ge(loads, N)

        @block.scalar
        def _(act):
            act.wait_ge(loads, N)
            act.copy(w["qkvh"][:], qkv[:]).then_inc(act_did, 1)
            act.wait_ge(pe_did, T(0, "sb"))
            act.copy(w["sb"][:].rearrange("p b d -> p (b d)"), X[:, 0:2].rearrange("p a n -> p (a n)")).then_inc(act_did, 1)
            act.wait_ge(pe_did, T(0, "cb"))
            act.add(w["cb"][:].rearrange("p b d -> p (b d)"), X[:, 2:4].rearrange("p a n -> p (a n)"), 1.0).then_inc(act_did, 1)

        @block.tensor
        def _(pe):
            pe.wait_ge(loads, N)
            scb = k["scb"][:, 1]
            mod_rows(pe, Y[:, 0:2], wm, scb, 2, P).then_inc(pe_did, 1)
            mod_rows(pe, X[:, 0:2], wm, scb, 3, P).then_inc(pe_did, 1)
            mod_rows(pe, X[:, 2:4], wm, scb, 4, P).then_inc(pe_did, 1)
            mod_rows(pe, Y[:, 2:4], wm, scb, 5, P).then_inc(pe_did, 1)

        @block.vector
        def _(v):
            v.reduce_sum(w["hm"][:], k["ident"][:].rearrange("p (h d) -> p h d", d=HD), AX.X).then_inc(vec_did, 1)
            pairs = w["hm"][:].rearrange("p (q r) -> p r q", r=2)
            v.wait_ge(vec_did, V(0, "hm"))
            for r in range(2):
                v.reduce_sum(w["par"][:, r:r + 1], pairs[:, r], AX.X).then_inc(vec_did, 1)
            v.wait_ge(act_did, A(0, "hi"))
            v.tensor_tensor(w["qkvl"][:], qkv[:], w["qkvh"][:].bitcast(F32), ALU.subtract).then_inc(vec_did, 1)
            v.wait_ge(pe_did, T(0, "ga"))
            flat = lambda ap: ap.rearrange("p b d -> p (b d)")
            gate(v, vec_did, V, ("gage", "gasign", "gaabs", "ga"), Y[:, 0:2].rearrange("p a n -> p (a n)"), flat(garow[:]), sign[:])
            v.wait_ge(vec_did, V(0, "ga"))
            for g in range(T2):
                ins = v.tensor_tensor(w["wog"][:, :, g, :], garow[:], wout[:, g:g + 1, :].to_broadcast([P, B, D]), ALU.mult)
            ins.then_inc(vec_did, 1)
            v.tensor_tensor(w["bog"][:], garow[:], bout[:].unsqueeze(1).to_broadcast([P, B, D]), ALU.mult).then_inc(vec_did, 1)
            v.wait_ge(pe_did, T(0, "gb"))
            gate(v, vec_did, V, ("gbge", "gbsign", "gbabs", "gb"), Y[:, 2:4].rearrange("p a n -> p (a n)"), flat(k["gbrow"][:]), sign[:])


def layer1_attention(nc, sb, sem, k, w, X, Y, dram):
    with ExitStack() as s:
        t = lambda n, shape, dt=F32: sb(n, shape, dt, s)
        x, mod, ident, hm, par = k["x"], k["mod"][:, 1], k["ident"], w["hm"], w["par"]
        lna, lnf = Norm(sb, sem, s, "ln1a"), Norm(sb, sem, s, "ln1f")
        R = 4 * B
        xn, xnf = t("xn1", [P, B, D]), t("xnf", [P, B, D])
        hT = t("b_hT", [P, T2, B, HC * P])
        win = t("b_win", [P, 2, T2, B, P], F32R)
        qk = t("b_qk", [P, B, 2 * D])
        raw = t("b_raw", [P, R, 2 * HD])
        sc, ex = t("b_scores", [P, R, HD]), t("b_exp", [P, R, HD])
        mx, sm = t("b_max", [P, R]), t("b_sum", [P, R])
        pr, prT = t("b_pairs", [P, R, 2, HD]), t("b_pairsT", [P, R, 2, HD])
        attT = t("b_attT", [P, R, HD])
        vT = t("b_vT", [P, T2, B * WT])
        vbd = t("b_vdiag", [P, T2, B * WT // HD, 8, HD])
        z = t("b_z", [P, B, T2, P])
        h, xp = t("c_h", [P, B, D]), t("c_x", [P, B, D])
        hfT = t("c_hT", [P, T2, TOK])
        lg, top, topi = t("c_logits", [P, B, E1]), t("c_top", [P, B, 8]), t("c_topi", [P, B, 8], U32)

        av, ap, aa, at = (sem(n, s) for n in ("win_vec", "win_pool", "win_act", "win_pe"))
        nv, np_, na, nt = (sem(n, s) for n in ("norm_vec", "norm_pool", "norm_act", "norm_pe"))
        fv, fp, fa, ft = (sem(n, s) for n in ("route_vec", "route_pool", "route_act", "route_pe"))
        stored = sem("stream_stored", s)
        seen_v, seen_p = (sem(f"win_seen_{e}", s) for e in ("vec", "pool"))
        NV, NP, NA, NT_ = Steps(LN_VEC), Steps(LN_POOL), Steps("h"), Steps("xT")
        AV = Steps("win0 win1 qk even scores max sub sum recip prob pair0 pair1 pairsT attT vdiag x")
        AP = Steps("vdiag x")
        AA = Steps("win0 win1 pairs vT exp z")
        AT = Steps("qk scores vT z out")
        FV = Steps(LN_VEC + "scale h logits top topi kept".split())
        FP = Steps(LN_POOL + ["gate", "x"])
        FA = Steps("keep hT")
        FT_ = Steps("hT logits")
        block = s.enter_context(nc.Block())
        X2 = X[:, 0:2].rearrange("p a n -> p (a n)")
        bd = lambda ap: ap.rearrange("p (b d) -> p b d", b=B)

        def norms(eng, f):
            f(0)
            with eng.Fori(1, HC) as c:
                f(c)

        def chunks(eng, *stages):
            for f in stages:
                f(0)
            with eng.Fori(1, NC) as c:
                for f in stages:
                    f(c)

        def diagonal(eng, g):
            n = B * WT // HD
            v4 = vT[:, g].rearrange("p (j o w) -> p j o w", o=1, w=HD).to_broadcast([P, n, 8, HD])
            return eng.tensor_tensor(vbd[:, g], v4, hm[:].unsqueeze(1).unsqueeze(3).to_broadcast([P, n, 8, HD]), ALU.mult)

        @block.sync
        def _(sp):
            def store(c):
                sp.wait_ge(fp, FP(c, "x"))
                sp.dma_start(dram["xres"].rearrange("(b c p) d -> p b c d", b=B, p=P)[:, :, c, :], xp[:]).then_inc(stored, 16)
            chunks(sp, store)
            sp.wait_ge(stored, 16 * NC)

        @block.gpsimd
        def _(pool):
            norms(pool, lambda c: norm_pool(pool, lna, np_, k["mhalf"], nv, NV(c, "eps")))

            def attention(c):
                pool.wait_ge(aa, AA(c, "vT"))
                reach(pool, at, AT(c - 1, "z"))
                diagonal(pool, 0).then_inc(ap, 1)
                apart(pool, av, AV(c, "x"), seen_p)
                pool.tensor_tensor(x[:, :, c, 0:D], x[:, :, c, 0:D], w["bog"][:], ALU.add).then_inc(ap, 1)

            def route(c):
                norm_pool(pool, lnf, fp, k["mhalf"], fv, FV(c, "eps"))
                pool.wait_ge(fv, FV(c, "h"))
                reach(pool, stored, 16 * c)
                pool.tensor_tensor(xp[:], h[:], k["gbrow"][:], ALU.mult).then_inc(fp, 1)
                apart(pool, fp, FP(c, "gate"), seen_p)
                pool.tensor_tensor(xp[:], xp[:], x[:, :, c, 0:D], ALU.add).then_inc(fp, 1)
            chunks(pool, attention, route)

        @block.scalar
        def _(act):
            def norm(c):
                act.wait_ge(nt, NT_(c, "xT"))
                for b in range(B):
                    for t_ in range(T2):
                        ins = act.activation(hT[:, t_, b, bass.ds(c * P, P)], Y[:, t_, b * P:(b + 1) * P], ACT.Identity,
                                             bias=mod[:, 0, t_, b:b + 1], scale=mod[:, 1, t_, b:b + 1])
                ins.then_inc(na, 1)
            norms(act, norm)
            act.wait_ge(na, NA(HC - 1, "h"))

            def attention(c):
                reach(act, at, AT(c - 1, "vT"))
                for i, first in ((0, STEP), (1, 0)):
                    act.copy(win[:, 0, :, :, i * WIN:(i + 1) * WIN].rearrange("p t b n -> p (t b) n"),
                             hT[:].rearrange("p t b n -> p (t b) n")[:, :, bass.ds(c * WIN + first, WIN)]).then_inc(aa, 1)
                act.wait_ge(at, AT(c, "scores"))
                for q in range(4):
                    part = slice(32 * q, 32 * q + 32)
                    ins = act.copy(raw[part], X[part].rearrange("p b (r n) -> p (b r) n", n=P)[:, :, part])
                ins.then_inc(aa, 1)
                act.wait_ge(at, AT(c, "vT"))
                for g in range(T2):
                    ins = act.activation(vT[:, g], X[:, g, 0:B * WT], ACT.Identity, bias=w["bv"][:, g:g + 1])
                ins.then_inc(aa, 1)
                act.wait_ge(av, AV(c, "sub"))
                act.activation(ex[:], sc[:], ACT.Exp, scale=HD ** -0.5).then_inc(aa, 1)
                act.wait_ge(at, AT(c, "z"))
                act.copy(z[:].rearrange("p b g (w d q) -> p (b g w) d q", w=2, d=HD),
                         X[:, 2:4].rearrange("p a (r q d) -> p (a r) d q", q=4, d=HD)).then_inc(aa, 1)

            def route(c):
                act.wait_ge(fp, FP(c, "x"))
                act.copy(x[:, :, c, 0:D], h[:]).then_inc(fa, 1)
                act.wait_ge(ft, FT_(c, "hT"))
                act.copy(hfT[:].rearrange("p t n -> p (t n)"), Y[:, 0:2].rearrange("p a n -> p (a n)")).then_inc(fa, 1)
            chunks(act, attention, route)

        @block.vector
        def _(v):
            norms(v, lambda c: norm_vector(v, lna, nv, NV, c, x, xn, np_, NP(c, "pow"), nt, NT_(c - 1, "xT")))
            v.wait_ge(na, NA(HC - 1, "h"))

            def attention(c):
                for i, first in ((0, STEP), (1, 0)):
                    v.wait_ge(aa, AA(c, f"win{i}"))
                    cols = slice(i * WIN, (i + 1) * WIN)
                    hi, lo = (win[:, j, :, :, cols].rearrange("p t b n -> p (t b) n") for j in range(2))
                    v.tensor_tensor(lo, hT[:].rearrange("p t b n -> p (t b) n")[:, :, bass.ds(c * WIN + first, WIN)],
                                    hi.bitcast(F32), ALU.subtract).then_inc(av, 1)
                v.wait_ge(at, AT(c, "qk"))
                v.tensor_tensor(qk[:], X[:], w["bqk"][:].unsqueeze(1).to_broadcast([P, B, 2 * D]), ALU.add).then_inc(av, 1)
                v.wait_ge(aa, AA(c, "pairs"))
                v.tensor_scalar(sc[:], raw[:, :, 0:HD], par[:, 0:1], None, ALU.mult).then_inc(av, 1)
                v.wait_ge(av, AV(c, "even"))
                v.scalar_tensor_tensor(out=sc[:], in0=raw[:, :, HD:2 * HD], scalar=par[:, 1:2], in1=sc[:], op0=ALU.mult, op1=ALU.add).then_inc(av, 1)
                v.wait_ge(av, AV(c, "scores"))
                v.reduce_max(mx[:], sc[:], AX.X).then_inc(av, 1)
                v.wait_ge(av, AV(c, "max"))
                v.tensor_tensor(sc[:], sc[:], mx[:].unsqueeze(2).to_broadcast([P, R, HD]), ALU.subtract).then_inc(av, 1)
                v.wait_ge(aa, AA(c, "exp"))
                v.reduce_sum(sm[:], ex[:], AX.X).then_inc(av, 1)
                v.wait_ge(av, AV(c, "sum"))
                v.reciprocal(sm[:], sm[:]).then_inc(av, 1)
                v.wait_ge(av, AV(c, "recip"))
                v.tensor_tensor(ex[:], ex[:], sm[:].unsqueeze(2).to_broadcast([P, R, HD]), ALU.mult).then_inc(av, 1)
                v.wait_ge(av, AV(c, "prob"))
                for i in range(2):
                    v.tensor_scalar(pr[:, :, i, :], ex[:], par[:, i:i + 1], None, ALU.mult).then_inc(av, 1)
                v.wait_ge(av, AV(c, "pair1"))
                v.transpose(prT[:].rearrange("p r i d -> p (r i d)"), pr[:].rearrange("p r i d -> p (r i d)")).then_inc(av, 1)
                v.wait_ge(av, AV(c, "pairsT"))
                v.tensor_tensor(attT[:], prT[:, :, 0, :], prT[:, :, 1, :], ALU.add).then_inc(av, 1)
                diagonal(v, 1).then_inc(av, 1)
                v.wait_ge(at, AT(c, "out"))
                v.tensor_tensor(x[:, :, c, 0:D], x[:, :, c, 0:D], bd(X2), ALU.add).then_inc(av, 1)

            def route(c):
                apart(v, ap, AP(c, "x"), lnf.seen)
                norm_vector(v, lnf, fv, FV, c, x, xnf, fp, FP(c, "pow"), fv, FV(c - 1, "scale"))
                v.wait_ge(fv, FV(c, "xn"))
                reach(v, fa, FA(c - 1, "keep"))
                v.tensor_tensor(h[:], xnf[:], w["cb"][:], ALU.mult).then_inc(fv, 1)
                v.wait_ge(fv, FV(c, "scale"))
                v.tensor_tensor(h[:], h[:], w["sb"][:], ALU.add).then_inc(fv, 1)
                v.wait_ge(ft, FT_(c, "logits"))
                reach(v, fv, FV(c - 1, "kept"))
                v.tensor_tensor(lg[:], Y[:, 2, 0:B * E1].rearrange("p (b e) -> p b e", b=B),
                                w["rb"][:].unsqueeze(1).to_broadcast([P, B, E1]), ALU.add).then_inc(fv, 1)
                apart(v, fv, FV(c, "logits"), seen_v)
                for b in range(B):
                    ins = v.max(top[:, b, :], lg[:, b, :])
                ins.then_inc(fv, 1)
                apart(v, fv, FV(c, "top"), seen_v)
                for b in range(B):
                    ins = v.max_index(topi[:, b, :], top[:, b, :], lg[:, b, :])
                ins.then_inc(fv, 1)
                v.tensor_copy(k["logits"][:, :, c, :], lg[:])
                v.tensor_copy(k["top"][:, :, c, :], top[:, :, 0:2])
                v.wait_ge(fv, FV(c, "topi"))
                v.tensor_copy(k["topi"][:, :, c, :], topi[:, :, 0:2]).then_inc(fv, 1)
            chunks(v, attention, route)

        @block.tensor
        def _(pe):
            bs = [slice(b * P, (b + 1) * P) for b in range(B)]

            def norm(c):
                pe.wait_ge(nv, NV(c, "xn"))
                reach(pe, na, NA(c - 1, "h"))
                transpose_chunk(pe, Y, xn, ident).then_inc(nt, 1)
            norms(pe, norm)

            def attention(c):
                pe.wait_ge(av, AV(c, "win1"))
                reach(pe, av, AV(c - 1, "x"))
                for b in range(B):
                    for t_ in range(T2):
                        ins = product3(pe, X[:, b], win[:, 0, t_, b, :], win[:, 1, t_, b, :],
                                       w["qkvh"][:, t_, 0:2 * D], w["qkvl"][:, t_, 0:2 * D], t_ == 0, t_ == T2 - 1)
                ins.then_inc(at, 1)
                pe.wait_ge(av, AV(c, "qk"))
                for b in range(B):
                    for wi in range(2):
                        part = slice(WIN * (1 - wi), WIN * (2 - wi))
                        for g in range(T2):
                            r = 2 * (b % 2) + g
                            ins = pe.matmul(X[:, 2 * wi + b // 2, r * P:(r + 1) * P], qk[part, b, g * P:(g + 1) * P],
                                            qk[part, b, D + g * P:D + (g + 1) * P], start=True, stop=True)
                ins.then_inc(at, 1)
                pe.wait_ge(aa, AA(c, "pairs"))
                for g in range(T2):
                    for t_ in range(T2):
                        cols = slice(2 * D + g * P, 2 * D + (g + 1) * P)
                        ins = product3(pe, X[:, g, 0:B * WT], w["qkvh"][:, t_, cols], w["qkvl"][:, t_, cols],
                                       win[:, 0, t_, :, 0:WT], win[:, 1, t_, :, 0:WT], t_ == 0, t_ == T2 - 1)
                ins.then_inc(at, 1)
                pe.wait_ge(av, AV(c, "vdiag"))
                pe.wait_ge(ap, AP(c, "vdiag"))
                for b in range(B):
                    for g in range(T2):
                        o = X[:, 2 + b // 2, (b % 2) * 2 * P + g * P:(b % 2) * 2 * P + (g + 1) * P].rearrange("p (q d) -> p q d", d=HD)
                        for j in range(WT // HD):
                            lhs = vbd[:, g, b * (WT // HD) + (j - 2) % (WT // HD)].rearrange("p h d -> p (h d)")
                            r0, r1 = 2 * b + g, 2 * (B + b) + g
                            if j < 2:
                                rhs, dst = attT[:, r0, :], o[:, j, :]
                            elif j < 4:
                                rhs, dst = attT[:, r0:r1 + 1:r1 - r0, :], o[:, j:j + 3:2, :]
                            else:
                                rhs, dst = attT[:, r1, :], o[:, j + 2, :]
                            ins = pe.matmul(dst, lhs, rhs, start=True, stop=True)
                ins.then_inc(at, 1)
                pe.wait_ge(aa, AA(c, "z"))
                for b in range(B):
                    for g in range(T2):
                        ins = pe.matmul(X2[:, b * D:(b + 1) * D], z[:, b, g, :], w["wog"][:, b, g, :], start=g == 0, stop=g == T2 - 1)
                ins.then_inc(at, 1)

            def route(c):
                pe.wait_ge(fv, FV(c, "h"))
                transpose_chunk(pe, Y, h, ident).then_inc(ft, 1)
                pe.wait_ge(fa, FA(c, "hT"))
                reach(pe, fv, FV(c - 1, "logits"))
                for b in range(B):
                    for t_ in range(T2):
                        ins = pe.matmul(Y[:, 2, b * E1:(b + 1) * E1], hfT[:, t_, bs[b]], w["rw"][:, t_, :], start=t_ == 0, stop=t_ == T2 - 1)
                ins.then_inc(ft, 1)
            chunks(pe, attention, route)


class Unit:

    def __init__(self, pair, q):
        self.pair, self.q = pair, q
        self.u = 2 * pair + q

    def next(self):
        return Unit(self.pair + self.q, 1 - self.q)

    def last(self):
        return Unit(self.pair - 1 + self.q, 1 - self.q)


class Swiglu:

    PRE_A, PRE_V, PRE_T = ["hin0", "hin1"], ["hin0", "hin1"], ["turn0", "turn1"]
    MAIN_A = [f"{n}{f}" for f in range(3) for n in ("silu", "hi")]
    MAIN_V = [f"{n}{f}" for f in range(3) for n in ("mul", "lo")]
    MAIN_T = [f"{n}{f}" for f in range(3) for n in ("gate", "up")]

    def __init__(self, nc, sb, sem, s, name, X, Y, ident, tiles, halves, units):
        self.X, self.Y, self.ident, self.tiles, self.halves, self.units = X, Y, ident, tiles, halves, units
        n = tiles * P
        t = lambda m, shape, dt=F32: sb(f"{name}_{m}", shape, dt, s)
        self.hin = t("hin", [P, 2, 2, T2, n], F32R)
        self.sil, self.act = t("silu", [P, 3, n]), t("act", [P, 3, n])
        self.acth, self.actl = t("acth", [P, 2, 3, n], F32R), t("actl", [P, 2, 3, n], F32R)
        self.out = t("out", [P, 2, tiles, D])
        self.pre_a, self.pre_v, self.pre_t = (sem(f"{name}_next_{e}", s) for e in ("act", "vec", "pe"))
        self.main_a, self.main_v, self.main_t = (sem(f"{name}_{e}", s) for e in ("act", "vec", "pe"))
        self.down_a, self.down_t = (sem(f"{name}_down_{e}", s) for e in ("act", "pe"))
        self.PA, self.PV, self.PT = Steps(self.PRE_A), Steps(self.PRE_V), Steps(self.PRE_T)
        self.MA, self.MV, self.MT = Steps(self.MAIN_A), Steps(self.MAIN_V), Steps(self.MAIN_T)
        self.DN = Steps([f"tile{j}" for j in range(tiles)])

    def run(self, turn, first, end):
        first(Unit(0, 0))
        turn(Unit(0, 0), True, False)
        turn(Unit(0, 1), True, True)
        with self.eng.Fori(1, self.units // 2 - 1) as i:
            turn(Unit(i, 0), True, True)
            turn(Unit(i, 1), True, True)
        turn(Unit(self.units // 2 - 1, 0), True, True)
        turn(Unit(self.units // 2 - 1, 1), False, True)
        end(Unit(self.units // 2 - 1, 1))

    def turn_in(self, pe, un, t, rows):
        if t == 0:
            reach(pe, self.pre_v, self.PV(un.u - 1, "hin1"))
        else:
            pe.wait_ge(self.pre_v, self.PV(un.u, "hin0"))
        Y2 = self.Y[:, 0:2].rearrange("p a n -> p (a n)")
        for j in range(self.tiles):
            ins = pe.transpose(Y2[:, j * P:(j + 1) * P], rows[:, j, t * P:(t + 1) * P], self.ident[:])
        ins.then_inc(self.pre_t, 1)

    def gate_up(self, pe, un, f, wg, wu):
        f0, m = FT[f]
        if f == 0:
            pe.wait_ge(self.pre_v, self.PV(un.u, "hin1"))
        for base, wt, name in ((0, wg, "gate"), (2, wu, "up")):
            if name == "gate":
                if f:
                    pe.wait_ge(self.main_a, self.MA(un.u, f"silu{f - 1}"))
                else:
                    reach(pe, self.main_a, self.MA(un.u - 1, "silu2"))
            elif f:
                pe.wait_ge(self.main_v, self.MV(un.u, f"mul{f - 1}"))
            else:
                reach(pe, self.main_v, self.MV(un.u - 1, "mul2"))
            for hf, (n0, n) in enumerate(self.halves):
                for t in range(T2):
                    ins = product3(pe, self.X[0:m, base + hf, 0:n], wt[0][:, t, f0:f0 + m], wt[1][:, t, f0:f0 + m],
                                   self.hin[:, un.q, 0, t, n0:n0 + n], self.hin[:, un.q, 1, t, n0:n0 + n], t == 0, t == T2 - 1)
            ins.then_inc(self.main_t, 1)

    def down(self, pe, un, wd):
        pe.wait_ge(self.main_v, self.MV(un.u, "lo2"))
        for j in range(self.tiles):
            if j >= 2:
                pe.wait_ge(self.down_a, self.DN(un.u, f"tile{j - 2}"))
            else:
                reach(pe, self.down_a, self.DN(un.u - 1, f"tile{self.tiles - 2 + (j + self.tiles) % 2}"))
            for f, (_, m) in enumerate(FT):
                rows = slice(j * P, (j + 1) * P)
                ins = product3(pe, self.Y[:, 2 + j % 2, 0:D], self.acth[0:m, un.q, f, rows], self.actl[0:m, un.q, f, rows],
                               wd[0][0:m, f, :], wd[1][0:m, f, :], f == 0, f == 2)
            ins.then_inc(self.down_t, 1)

    def hin_hi(self, act, un, t):
        act.wait_ge(self.pre_t, self.PT(un.u, f"turn{t}"))
        reach(act, self.main_t, self.MT(un.u - 2, "up2"))
        n = self.tiles * P
        act.copy(self.hin[:, un.q, 0, t, :], self.Y[:, 0:2].rearrange("p a n -> p (a n)")[:, 0:n]).then_inc(self.pre_a, 1)

    def psum(self, base, m):
        nh, n = len(self.halves), self.halves[0][1]
        return self.X[0:m, base:base + nh, 0:n]

    def split(self, ap):
        return ap.rearrange("p (h n) -> p h n", h=len(self.halves))

    def silu(self, act, un, f):
        m = FT[f][1]
        act.wait_ge(self.main_t, self.MT(un.u, f"gate{f}"))
        reach(act, self.main_v, self.MV(un.u - 1, f"mul{f}"))
        act.activation(self.split(self.sil[0:m, f, :]), self.psum(0, m), ACT.Silu).then_inc(self.main_a, 1)
        act.wait_ge(self.main_v, self.MV(un.u, f"mul{f}"))
        reach(act, self.down_t, self.DN(un.u - 2, f"tile{self.tiles - 1}"))
        act.copy(self.acth[0:m, un.q, f, :], self.act[0:m, f, :]).then_inc(self.main_a, 1)

    def take_down(self, act, un, scale=None, free=None):
        for j in range(self.tiles):
            act.wait_ge(self.down_t, self.DN(un.u, f"tile{j}"))
            if j == 0 and free is not None:
                reach(act, *free)
            if scale is None:
                ins = act.copy(self.out[:, un.q, j, :], self.Y[:, 2 + j % 2, 0:D])
            else:
                ins = act.mul(self.out[:, un.q, j, :], self.Y[:, 2 + j % 2, 0:D], scale[:, j:j + 1])
            ins.then_inc(self.down_a, 1)

    def hin_lo(self, v, un, t):
        v.wait_ge(self.pre_a, self.PA(un.u, f"hin{t}"))
        n = self.tiles * P
        v.tensor_tensor(self.hin[:, un.q, 1, t, :], self.Y[:, 0:2].rearrange("p a n -> p (a n)")[:, 0:n],
                        self.hin[:, un.q, 0, t, :].bitcast(F32), ALU.subtract).then_inc(self.pre_v, 1)

    def mul(self, v, un, f):
        m = FT[f][1]
        v.wait_ge(self.main_t, self.MT(un.u, f"up{f}"))
        v.wait_ge(self.main_a, self.MA(un.u, f"silu{f}"))
        v.tensor_tensor(self.split(self.act[0:m, f, :]), self.psum(2, m), self.split(self.sil[0:m, f, :]), ALU.mult).then_inc(self.main_v, 1)
        v.wait_ge(self.main_a, self.MA(un.u, f"hi{f}"))
        v.tensor_tensor(self.actl[0:m, un.q, f, :], self.act[0:m, f, :], self.acth[0:m, un.q, f, :].bitcast(F32),
                        ALU.subtract).then_inc(self.main_v, 1)


def shared_and_routing(nc, sb, sem, a, k, X, Y, dram):
    with ExitStack() as s:
        t = lambda n, shape, dt=F32: sb(n, shape, dt, s)
        x = k["x"]
        sw = Swiglu(nc, sb, sem, s, "shared", X, Y, k["ident"], 4, [(0, 4 * P)], 2 * B)
        raw = t("sw_raw", [P, 2, T2, F1])
        rawd = t("sw_rawd", [P, 3, D])
        wg = (t("sw_gh", [P, T2, F1], F32R), t("sw_gl", [P, T2, F1], F32R))
        wu = (t("sw_uh", [P, T2, F1], F32R), t("sw_ul", [P, T2, F1], F32R))
        wd = (t("sw_dh", [P, 3, D], F32R), t("sw_dl", [P, 3, D], F32R))
        rows = t("sw_rows", [P, 2, 4, D])
        NK = 2
        tri, onesb = t("tri", [P, P], BF16), t("onesb", [P, P], BF16)
        trif = t("trif", [P, P])
        ie, ief = t("ie", [P, E1], U32), t("ief", [P, E1])
        tok = t("tok", [P, NT], U32)
        ti = t("ti", [P, NK, NT])
        one_hot, prod = t("one_hot", [P, NK, NT, E1]), t("prod", [P, NK, NT, E1])
        lg, ex = t("lg", [P, NT, E1]), t("ex", [P, NT, E1])
        cnt = t("cnt", [P, NT * E1], BF16)
        keep, tot, incl = t("keep", [P, E1, NT]), t("tot", [P, E1, NT]), t("incl", [P, E1, NT])
        before = t("before", [P, NT, E1])
        z, e2, val, pos, inside = t("z", [P, NT]), t("e2", [P, NT]), t("val", [P, NK, NT]), t("pos", [P, NK, NT]), t("inside", [P, NK, NT])
        slotf, slot = t("slotf", [P, NK, NT]), t("slot", [P, NK, NT], U32)

        loads, rows_in = sem("sw_loads", s), [sem(f"sw_rows{q}", s) for q in range(2)]
        wts_a, wts_v, rt_v, rt_a, rt_t, rt_p = (sem(n, s) for n in ("sw_split_act", "sw_split_vec", "slots_vec", "slots_act", "slots_pe", "slots_pool"))
        sent = [sem(f"scattered{i}", s) for i in range(2)]
        stored = [sem(f"sw_stored{q}", s) for q in range(2)]
        RV = Steps("sub gap ti oh0 oh1 cnt keep1 keep0 tot scan excl before prod pos inside z rz p2 sum rs v1 v2 w slotf over slot tok w0 w1")
        RA = Steps("exp e2 tri ones")
        RT = Steps("count")
        RP = Steps("tri0 tri ie tok")
        block = s.enter_context(nc.Block())
        tiles = x[:].rearrange("p b c r -> p (b c) r")
        lgt = k["logits"][:].rearrange("p b c e -> p (b c) e")
        top = k["top"][:].rearrange("p b c e -> p (b c) e")
        topi = k["topi"][:].rearrange("p b c e -> p (b c) e")

        @block.sync
        def _(sp):
            sp.dma_start(raw[:, 0], a["L1_ffn_sw_gate"].rearrange("(t p) n -> p t n", p=P)).then_inc(loads, 16)
            sp.dma_start(raw[:, 1], a["L1_ffn_sw_up"].rearrange("(t p) n -> p t n", p=P)).then_inc(loads, 16)
            sp.dma_start(rawd[:, 0:2], a["L1_ffn_sw_down"][0:2 * P].rearrange("(t p) n -> p t n", p=P)).then_inc(loads, 16)
            sp.dma_start(rawd[0:F1 - 2 * P, 2], a["L1_ffn_sw_down"][2 * P:F1]).then_inc(loads, 16)

            def load(un):
                reach(sp, sw.pre_t, sw.PT(un.u - 2, "turn1"))
                sp.dma_start(rows[:, un.q], tiles[:, bass.ds(4 * un.u, 4), 0:D]).then_inc(rows_in[un.q], 16)

            def turn(un, after, before_):
                if after:
                    load(un.next())
                if before_:
                    store(un.last())

            def store(un):
                sp.wait_ge(sw.down_a, sw.DN(un.u, "tile3"))
                sp.dma_start(dram["moe"][bass.ds(un.u * 4 * P, 4 * P)].rearrange("(j p) d -> p j d", p=P), sw.out[:, un.q]).then_inc(stored[un.q], 16)
            sw.eng = sp
            sw.run(turn, load, store)
            for q in range(2):
                sp.wait_ge(stored[q], 16 * B)

        @block.gpsimd
        def _(pool):
            pool.memset(trif[:], 1.0).then_inc(rt_p, 1)
            pool.wait_ge(rt_p, RP(0, "tri0"))
            pool.affine_select(out=trif[:], in_=trif[:], compare_op=ALU.is_ge, fill=0.0, base=-1,
                               pattern=[[1, P]], channel_multiplier=-1).then_inc(rt_p, 1)
            pool.iota(ie[:], pattern=[[1, E1]], base=0, channel_multiplier=0).then_inc(rt_p, 1)
            pool.iota(tok[:], pattern=[[P, NT]], base=1, channel_multiplier=1).then_inc(rt_p, 1)
            for kk in range(NK):
                pool.wait_ge(rt_v, RV(0, f"w{kk}"))
                for tt in range(NT):
                    pool.indirect_dma_start(dram["rows"], bass.IndirectOffsetOnAxis(slot[:, kk, tt:tt + 1], 0), tiles[:, tt, :], None,
                                            bounds_check=SLOTS - 1, oob_is_err=False).then_inc(sent[kk], 16)
            for kk in range(NK):
                pool.wait_ge(sent[kk], 16 * NT)

        @block.scalar
        def _(act):
            act.wait_ge(loads, 16 * 4)
            for i, (dst, src) in enumerate(((wg[0][:], raw[:, 0]), (wu[0][:], raw[:, 1]), (wd[0][:, 0:2], rawd[:, 0:2]),
                                            (wd[0][0:F1 - 2 * P, 2], rawd[0:F1 - 2 * P, 2]))):
                act.copy(dst, src).then_inc(wts_a, 1)
            act.wait_ge(rt_v, RV(0, "gap"))
            act.activation(ex[:], lg[:], ACT.Exp).then_inc(rt_a, 1)
            act.activation(e2[:], e2[:], ACT.Exp).then_inc(rt_a, 1)
            act.wait_ge(rt_p, RP(0, "tri"))
            act.copy(tri[:], trif[:]).then_inc(rt_a, 1)
            act.copy(onesb[:], k["ones"][:]).then_inc(rt_a, 1)

            def first(un):
                for t_ in range(T2):
                    sw.hin_hi(act, un, t_)

            def turn(un, after, before_):
                sw.silu(act, un, 0)
                if before_:
                    down(un.last())
                sw.silu(act, un, 1)
                if after:
                    sw.hin_hi(act, un.next(), 0)
                sw.silu(act, un, 2)
                if after:
                    sw.hin_hi(act, un.next(), 1)

            def down(un):
                sw.take_down(act, un, free=(stored[un.q], 16 * un.pair))
            sw.eng = act
            sw.run(turn, first, down)

        def route(v):
            def did(ins):
                ins.then_inc(rt_v, 1)

            bc = lambda ap: ap.unsqueeze(2).to_broadcast([P, NT, E1])
            did(v.tensor_tensor(lg[:], lgt, top[:, :, 0:1].to_broadcast([P, NT, E1]), ALU.subtract))
            did(v.tensor_tensor(e2[:], top[:, :, 1], top[:, :, 0], ALU.subtract))
            did(v.tensor_copy(ti[:], topi[:, :, 0:NK].rearrange("p t k -> p k t")))
            v.wait_ge(rt_p, RP(0, "ie"))
            v.tensor_copy(ief[:], ie[:])
            v.wait_ge(rt_v, RV(0, "ti"))
            v.drain()
            for kk in range(NK):
                did(v.tensor_tensor(one_hot[:, kk], ief[:].unsqueeze(1).to_broadcast([P, NT, E1]), bc(ti[:, kk]), ALU.is_equal))
            v.wait_ge(rt_v, RV(0, "oh1"))
            did(v.tensor_tensor(cnt[:].rearrange("p (t e) -> p t e", e=E1), one_hot[:, 0], one_hot[:, 1], ALU.add))
            did(v.memset(keep[:], 1.0))
            v.wait_ge(rt_v, RV(0, "keep1"))
            did(v.memset(keep[:, :, 0:1], 0.0))
            v.wait_ge(rt_t, RT(0, "count"))
            did(v.tensor_copy(tot[:], X[:, 1, 0:NT * E1].rearrange("p (t e) -> p e t", e=E1)))
            v.wait_ge(rt_v, RV(0, "tot"))
            flat = lambda ap: ap.rearrange("p e t -> p (e t)")
            did(v.tensor_tensor_scan(flat(incl[:]), flat(keep[:]), flat(tot[:]), 0.0, ALU.mult, ALU.add))
            v.wait_ge(rt_v, RV(0, "scan"))
            did(v.tensor_tensor(incl[:], incl[:], tot[:], ALU.subtract))
            v.wait_ge(rt_v, RV(0, "excl"))
            did(v.tensor_tensor(before[:], X[:, 0, 0:NT * E1].rearrange("p (t e) -> p t e", e=E1), incl[:].rearrange("p e t -> p t e"), ALU.add))
            v.wait_ge(rt_v, RV(0, "before"))
            for kk in range(NK):
                ins = v.tensor_tensor(prod[:, kk], one_hot[:, kk], before[:], ALU.mult)
            did(ins)
            v.wait_ge(rt_v, RV(0, "prod"))
            did(v.reduce_sum(pos[:].rearrange("p k t -> p (k t)"), prod[:].rearrange("p k t e -> p (k t) e"), AX.X))
            v.wait_ge(rt_v, RV(0, "pos"))
            did(v.tensor_scalar(inside[:], pos[:], float(CAP), None, ALU.is_lt))
            v.wait_ge(rt_a, RA(0, "e2"))
            did(v.reduce_sum(z[:], ex[:], AX.X))
            v.wait_ge(rt_v, RV(0, "z"))
            did(v.reciprocal(z[:], z[:]))
            v.wait_ge(rt_v, RV(0, "rz"))
            did(v.tensor_tensor(e2[:], e2[:], z[:], ALU.mult))
            v.wait_ge(rt_v, RV(0, "p2"))
            did(v.scalar_tensor_tensor(out=val[:, 0], in0=z[:], scalar=1e-9, in1=e2[:], op0=ALU.add, op1=ALU.add))
            v.wait_ge(rt_v, RV(0, "sum"))
            did(v.reciprocal(val[:, 0], val[:, 0]))
            v.wait_ge(rt_v, RV(0, "rs"))
            did(v.tensor_tensor(val[:, 1], val[:, 0], e2[:], ALU.mult))
            v.wait_ge(rt_v, RV(0, "v1"))
            did(v.tensor_tensor(val[:, 0], val[:, 0], z[:], ALU.mult))
            v.wait_ge(rt_v, RV(0, "v2"))
            did(v.tensor_tensor(val[:], val[:], inside[:], ALU.mult))
            did(v.scalar_tensor_tensor(out=slotf[:], in0=ti[:], scalar=float(CAP), in1=pos[:], op0=ALU.mult, op1=ALU.add))
            v.wait_ge(rt_v, RV(0, "slotf"))
            did(v.tensor_scalar(pos[:], inside[:], -float(4 * SLOTS), float(4 * SLOTS), ALU.mult, ALU.add))
            v.wait_ge(rt_v, RV(0, "over"))
            did(v.tensor_tensor(slot[:], slotf[:], pos[:], ALU.add))
            v.wait_ge(rt_p, RP(0, "tok"))
            did(v.tensor_copy(tiles[:, :, D + 1], tok[:]))
            v.wait_ge(rt_v, RV(0, "w"))
            did(v.tensor_copy(tiles[:, :, D], val[:, 0, :]))

        @block.vector
        def _(v):
            for i, (lo, src, hi) in enumerate(((wg[1][:], raw[:, 0], wg[0][:]), (wu[1][:], raw[:, 1], wu[0][:]),
                                               (wd[1][:, 0:2], rawd[:, 0:2], wd[0][:, 0:2]),
                                               (wd[1][0:F1 - 2 * P, 2], rawd[0:F1 - 2 * P, 2], wd[0][0:F1 - 2 * P, 2]))):
                v.wait_ge(wts_a, i + 1)
                v.tensor_tensor(lo, src, hi.bitcast(F32), ALU.subtract).then_inc(wts_v, 1)
            route(v)
            def first(un):
                for t_ in range(T2):
                    sw.hin_lo(v, un, t_)

            def turn(un, after, before_):
                sw.mul(v, un, 0)
                sw.mul(v, un, 1)
                if after:
                    sw.hin_lo(v, un.next(), 0)
                sw.mul(v, un, 2)
                if after:
                    sw.hin_lo(v, un.next(), 1)
            sw.eng = v
            sw.run(turn, first, lambda un: None)
            v.wait_ge(sent[0], 16 * NT)
            v.tensor_copy(tiles[:, :, D], val[:, 1, :]).then_inc(rt_v, 1)

        @block.tensor
        def _(pe):
            pe.wait_ge(rt_v, RV(0, "cnt"))
            pe.wait_ge(rt_a, RA(0, "ones"))
            pe.matmul(X[:, 0], tri[:], cnt[:], start=True, stop=True)
            pe.matmul(X[:, 1], onesb[:], cnt[:], start=True, stop=True).then_inc(rt_t, 1)
            pe.wait_ge(wts_v, 4)
            pe.wait_ge(rt_v, RV(0, "before"))

            def turn_in(un, t_):
                pe.wait_ge(rows_in[un.q], 16 * (un.pair + 1))
                sw.turn_in(pe, un, t_, rows[:, un.q])

            def first(un):
                for t_ in range(T2):
                    turn_in(un, t_)

            def turn(un, after, before_):
                sw.gate_up(pe, un, 0, wg, wu)
                if before_:
                    sw.down(pe, un.last(), wd)
                sw.gate_up(pe, un, 1, wg, wu)
                if after:
                    turn_in(un.next(), 0)
                sw.gate_up(pe, un, 2, wg, wu)
                if after:
                    turn_in(un.next(), 1)
            sw.eng = pe
            sw.run(turn, first, lambda un: sw.down(pe, un, wd))


def experts(nc, sb, sem, a, k, X, Y, dram):
    with ExitStack() as s:
        t = lambda n, shape, dt=F32: sb(n, shape, dt, s)
        NTE = CAP // P
        sw = Swiglu(nc, sb, sem, s, "expert", X, Y, k["ident"], NTE, [(0, CAP // 2), (CAP // 2, CAP // 2)], E1)
        raw = t("ew_raw", [P, 2, 2, T2, F1])
        rawd = t("ew_rawd", [P, 2, 3, D])
        wgu = [t(f"ew_{n}", [P, 2, 2, T2, F1], F32R) for n in ("h", "l")]
        wdn = [t(f"ew_d{n}", [P, 2, 3, D], F32R) for n in ("h", "l")]
        rows = t("ew_rows", [P, 2, NTE, ROW])
        wt = t("ew_weight", [P, 2, NTE])
        none = t("ew_none", [P, 2, NTE])
        idx = t("ew_idx", [P, 2, NTE], U32)
        weights_in = [sem(f"ew_weights{q}", s) for q in range(2)]
        rows_in = [sem(f"ew_rows{q}", s) for q in range(2)]
        added = [sem(f"ew_added{q}", s) for q in range(2)]
        x_in, seen = sem("x_back", s), sem("ew_seen", s)
        split_a, split_v, meta = sem("ew_split_act", s), sem("ew_split_vec", s), sem("ew_meta", s)
        SA, SV, ME = Steps("gu d01 d2"), Steps("gu d01 d2"), Steps("weight none idx")
        M2 = F1 - 2 * P
        block = s.enter_context(nc.Block())

        @block.sync
        def _(sp):
            e_of = lambda name, un: a[name][bass.ds(un.u, 1)].rearrange("o k n -> (o k) n")

            def load(un):
                q = un.q
                reach(sp, split_v, SV(un.u - 2, "d2"))
                sp.dma_start(raw[:, q, 0], e_of("L1_ffn_w_gate", un).rearrange("(t p) n -> p t n", p=P)).then_inc(weights_in[q], 16)
                sp.dma_start(raw[:, q, 1], e_of("L1_ffn_w_up", un).rearrange("(t p) n -> p t n", p=P)).then_inc(weights_in[q], 16)
                wd = e_of("L1_ffn_w_down", un)
                sp.dma_start(rawd[:, q, 0:2], wd[0:2 * P].rearrange("(t p) n -> p t n", p=P)).then_inc(weights_in[q], 16)
                sp.dma_start(rawd[0:M2, q, 2], wd[2 * P:F1]).then_inc(weights_in[q], 16)
                reach(sp, sw.pre_t, sw.PT(un.u - 2, "turn1"))
                reach(sp, meta, ME(un.u - 2, "idx"))
                sp.dma_start(rows[:, q], dram["rows"][bass.ds(un.u * CAP, CAP)].rearrange("(j p) r -> p j r", p=P)).then_inc(rows_in[q], 16)

            def turn(un, after, before):
                if after:
                    load(un.next())
            sw.eng = sp
            sw.run(turn, load, lambda un: None)
            sp.dma_start(k["x"][:, :, :, 0:D].rearrange("p b c d -> p (b c) d"),
                         dram["xres"].rearrange("(j p) d -> p j d", p=P)).then_inc(x_in, 16)
            sp.wait_ge(x_in, 16)

        @block.gpsimd
        def _(pool):
            def add(un):
                reach(pool, added[1 - un.q], 16 * NTE * (un.pair + un.q))
                pool.wait_ge(meta, ME(un.u, "idx"))
                for j in range(NTE):
                    apart(pool, sw.down_a, sw.DN(un.u, f"tile{j}"), seen)
                    pool.indirect_dma_start(dram["moe"], bass.IndirectOffsetOnAxis(idx[:, un.q, j:j + 1], 0), sw.out[:, un.q, j, :], None,
                                            compute_op=ALU.add,
                                            bounds_check=B * S - 1, oob_is_err=False).then_inc(added[un.q], 16)

            def turn(un, after, before):
                if before:
                    add(un.last())
            sw.eng = pool
            sw.run(turn, lambda un: None, add)
            for q in range(2):
                pool.wait_ge(added[q], 16 * NTE * E1 // 2)

        @block.scalar
        def _(act):
            def split(un):
                q = un.q
                act.wait_ge(weights_in[q], 64 * (un.pair + 1))
                reach(act, sw.down_t, sw.DN(un.u - 2, f"tile{NTE - 1}"))
                act.copy(wgu[0][:, q], raw[:, q]).then_inc(split_a, 1)
                act.copy(wdn[0][:, q, 0:2], rawd[:, q, 0:2]).then_inc(split_a, 1)
                act.copy(wdn[0][0:M2, q, 2], rawd[0:M2, q, 2]).then_inc(split_a, 1)

            def first(un):
                split(un)
                for t_ in range(T2):
                    sw.hin_hi(act, un, t_)

            def turn(un, after, before):
                sw.silu(act, un, 0)
                if before:
                    down(un.last())
                sw.silu(act, un, 1)
                if after:
                    split(un.next())
                    sw.hin_hi(act, un.next(), 0)
                sw.silu(act, un, 2)
                if after:
                    sw.hin_hi(act, un.next(), 1)

            def down(un):
                sw.take_down(act, un, wt[:, un.q], (added[un.q], 16 * NTE * un.pair))
            sw.eng = act
            sw.run(turn, first, down)

        @block.vector
        def _(v):
            def split(un):
                q = un.q
                for i, (hi, lo, r) in enumerate(((wgu[0][:, q], wgu[1][:, q], raw[:, q]), (wdn[0][:, q, 0:2], wdn[1][:, q, 0:2], rawd[:, q, 0:2]),
                                                 (wdn[0][0:M2, q, 2], wdn[1][0:M2, q, 2], rawd[0:M2, q, 2]))):
                    v.wait_ge(split_a, SA(un.u, ("gu", "d01", "d2")[i]))
                    v.tensor_tensor(lo, r, hi.bitcast(F32), ALU.subtract).then_inc(split_v, 1)

            def tokens(un):
                q = un.q
                v.wait_ge(rows_in[q], 16 * (un.pair + 1))
                reach(v, sw.down_a, sw.DN(un.u - 2, f"tile{NTE - 1}"))
                v.tensor_copy(wt[:, q], rows[:, q, :, D]).then_inc(meta, 1)
                v.tensor_scalar(none[:, q], rows[:, q, :, D + 1], 0.0, float(4 * SLOTS), ALU.is_equal, ALU.mult).then_inc(meta, 1)
                v.wait_ge(meta, ME(un.u, "none"))
                reach(v, added[q], 16 * NTE * un.pair)
                v.scalar_tensor_tensor(out=idx[:, q], in0=rows[:, q, :, D + 1], scalar=-1.0, in1=none[:, q], op0=ALU.add, op1=ALU.add).then_inc(meta, 1)

            def first(un):
                tokens(un)
                split(un)
                for t_ in range(T2):
                    sw.hin_lo(v, un, t_)

            def turn(un, after, before):
                sw.mul(v, un, 0)
                sw.mul(v, un, 1)
                if after:
                    split(un.next())
                    sw.hin_lo(v, un.next(), 0)
                sw.mul(v, un, 2)
                if after:
                    sw.hin_lo(v, un.next(), 1)
                    tokens(un.next())
            sw.eng = v
            sw.run(turn, first, lambda un: None)

        @block.tensor
        def _(pe):
            wd = lambda q: (wdn[0][:, q], wdn[1][:, q])
            wg = lambda q: (wgu[0][:, q, 0], wgu[1][:, q, 0])
            wu = lambda q: (wgu[0][:, q, 1], wgu[1][:, q, 1])

            def turn_in(un, t_):
                pe.wait_ge(rows_in[un.q], 16 * (un.pair + 1))
                sw.turn_in(pe, un, t_, rows[:, un.q])

            def first(un):
                for t_ in range(T2):
                    turn_in(un, t_)

            def turn(un, after, before):
                pe.wait_ge(split_v, SV(un.u, "d2"))
                sw.gate_up(pe, un, 0, wg(un.q), wu(un.q))
                if before:
                    sw.down(pe, un.last(), wd(1 - un.q))
                sw.gate_up(pe, un, 1, wg(un.q), wu(un.q))
                if after:
                    turn_in(un.next(), 0)
                sw.gate_up(pe, un, 2, wg(un.q), wu(un.q))
                if after:
                    turn_in(un.next(), 1)
            sw.eng = pe
            sw.run(turn, first, lambda un: sw.down(pe, un, wd(un.q)))


def final(nc, sb, sem, k, dram, out):
    with ExitStack() as s:
        G = 4
        x = k["x"]
        m = sb("fin_moe", [P, 2, G, D], F32, s)
        o = sb("fin_out", [P, 2, G, D], F32, s)
        loaded = [sem(f"fin_loaded{i}", s) for i in range(2)]
        stored = [sem(f"fin_stored{i}", s) for i in range(2)]
        vec = sem("fin_vec", s)
        block = s.enter_context(nc.Block())
        n = NT // G
        dst = out.rearrange("b (c p) d -> p b c d", p=P)

        @block.sync
        def _(sp):
            for i in range(n):
                if i >= 2:
                    sp.wait_ge(vec, 2 * (i - 2) + 1)
                sp.dma_start(m[:, i % 2], dram["moe"][i * G * P:(i + 1) * G * P].rearrange("(j p) d -> p j d", p=P)).then_inc(loaded[i % 2], 16)

        @block.scalar
        def _(act):
            for i in range(n):
                act.wait_ge(vec, 2 * i + 2)
                b, c = divmod(i * G, NC)
                act.dma_start(dst[:, b, c:c + G, :], o[:, i % 2]).then_inc(stored[i % 2], 16)
            for q in range(2):
                act.wait_ge(stored[q], 16 * (n // 2))

        @block.vector
        def _(v):
            for i in range(n):
                b, c = divmod(i * G, NC)
                v.wait_ge(loaded[i % 2], 16 * (i // 2 + 1))
                if i >= 2:
                    v.wait_ge(stored[i % 2], 16 * (i // 2))
                v.tensor_tensor(o[:, i % 2], m[:, i % 2], k["gbrow"][:, b:b + 1, :].to_broadcast([P, G, D]), ALU.mult).then_inc(vec, 1)
                v.wait_ge(vec, 2 * i + 1)
                v.tensor_tensor(o[:, i % 2], o[:, i % 2], x[:, b, c:c + G, 0:D], ALU.add).then_inc(vec, 1)


_INS = ["L0_attn_hidden_states", "L0_attn_w_q", "L0_attn_w_k", "L0_attn_w_v", "L0_attn_w_o", "L0_attn_gate",
        "L0_attn_memory", "L0_attn_memory_norm", "L0_ffn_gate_w", "L0_ffn_w1", "L0_ffn_b1", "L0_ffn_w2", "L0_ffn_b2",
        "L0_ffn_sw1", "L0_ffn_sb1", "L0_ffn_sw2", "L0_ffn_sb2", "L0_c", "L0_wmod", "L1_attn_W_qkv", "L1_attn_b_qkv",
        "L1_attn_W_out", "L1_attn_b_out", "L1_ffn_router_w", "L1_ffn_router_b", "L1_ffn_w_gate", "L1_ffn_w_up",
        "L1_ffn_w_down", "L1_ffn_sw_gate", "L1_ffn_sw_up", "L1_ffn_sw_down", "L1_c", "L1_wmod"]


def kernel(**inputs):
    import numpy as np
    import concourse.bacc as bacc
    from concourse.bass_utils import run_bass_kernel_spmd

    nc = bacc.Bacc("TRN2", target_bir_lowering=False, num_devices=1)
    arrays, aps = {}, {}
    for name in _INS:
        arr = np.ascontiguousarray(inputs[name])
        arrays[f"in_{name}"] = arr
        aps[name] = nc.dram_tensor(f"in_{name}", arr.shape, mybir.dt.from_np(arr.dtype), kind="ExternalInput").ap()
    out = nc.dram_tensor("out_0", (B, S, D), F32, kind="ExternalOutput").ap()
    build(nc, aps, out)
    r = run_bass_kernel_spmd(nc, [arrays], core_ids=[0])
    return r.results[0]["out_0"]
```

```python
from contextlib import ExitStack

import concourse.bass as bass
from concourse import mybir

F32 = mybir.dt.float32
F32R = mybir.dt.float32r
BF16 = mybir.dt.bfloat16
U32 = mybir.dt.uint32
ALU = mybir.AluOpType
ACT = mybir.ActivationFunctionType
AX = mybir.AxisListType

P = 128
B, S, D = 4, 1024, 256
T2 = D // P
NC = S // P
TOK = B * P
NT = B * NC
DM = 64
H0 = 1024
HT0 = H0 // P
NSTEP = 3 * HT0
HEADS, HD = 16, 16
WIN, STEP = 64, 32
WT = WIN + STEP
HC = 5
E1, F1 = 16, 352
CAP = 640
SLOTS = E1 * CAP
ROW = D + 2
LN_EPS = 1e-5
MEM_EPS = 1e-6
FT = [(0, 128), (128, 128), (256, F1 - 256)]


class Steps:

    def __init__(self, names):
        self.names = names if isinstance(names, list) else names.split()

    def __call__(self, c, name):
        return c * len(self.names) + self.names.index(name) + 1


def reach(eng, sem, count):
    if not isinstance(count, int) or count > 0:
        eng.wait_ge(sem, count)


def apart(eng, sem, count, seen):
    if isinstance(count, int):
        reach(eng, sem, count)
    else:
        eng.wait_ge(sem, count)
        eng.sem_inc(seen, 1)


def build(nc, a, out, stop=9):
    ctx = ExitStack()
    with ctx:
        def sb(name, shape, dt=F32, c=None):
            return (c or ctx).enter_context(nc.sbuf_tensor(name, shape, dt))

        def sem(name, c=None):
            return (c or ctx).enter_context(nc.semaphore(name))

        X = ctx.enter_context(nc.psum_tensor("X", [P, 4, 512], F32))
        Y = ctx.enter_context(nc.psum_tensor("Y", [P, 4, 512], F32))
        dram = {
            "rows": nc.dram_tensor("expert_rows", [SLOTS, ROW], F32).ap(),
            "moe": nc.dram_tensor("moe_sum", [B * S, D], F32).ap(),
            "xres": nc.dram_tensor("x_residual", [B * S, D], F32).ap(),
        }

        k = {}
        k["x"] = sb("x", [P, B, NC, ROW])
        k["ident"] = sb("ident", [P, P])
        k["ones"] = sb("ones", [P, P])
        k["mod"] = sb("mod", [P, 2, 6, T2, B])
        k["gbb"] = sb("gbb", [P, T2, B])
        k["scb"] = sb("scb", [P, 2, B, T2])
        k["mhalf"] = sb("mhalf", [P, B])

        with ExitStack() as s:
            w = layer0_weights(nc, sb, s)
            setup(nc, sb, sem, a, k, w, X, Y, dram)
            layer0(nc, sb, sem, k, w, X, Y)
        if stop == 0:
            dump_x(nc, sem, k, out)
            return
        k["logits"] = sb("logits", [P, B, NC, E1])
        k["top"] = sb("top", [P, B, NC, 2])
        k["topi"] = sb("topi", [P, B, NC, 2])
        k["gbrow"] = sb("gbrow", [P, B, D])
        with ExitStack() as s:
            w = layer1_weights(nc, sb, s)
            setup1(nc, sb, sem, a, k, w, X, Y)
            layer1_attention(nc, sb, sem, k, w, X, Y, dram)
        if stop == 1:
            dump_res(nc, sem, dram, out)
            return
        shared_and_routing(nc, sb, sem, a, k, X, Y, dram)
        experts(nc, sb, sem, a, k, X, Y, dram)
        final(nc, sb, sem, k, dram, out)


def dump_x(nc, sem, k, out):
    with ExitStack() as s:
        d = sem("dumped", s)
        block = s.enter_context(nc.Block())

        @block.sync
        def _(sp):
            for b in range(B):
                sp.dma_start(out[b].rearrange("(c p) d -> p c d", p=P), k["x"][:, b, :, 0:D]).then_inc(d, 16)
            sp.wait_ge(d, 16 * B)


def dump_res(nc, sem, dram, out):
    with ExitStack() as s:
        d = sem("dumped", s)
        block = s.enter_context(nc.Block())

        @block.sync
        def _(sp):
            sp.dma_start(out.rearrange("b s d -> (b s) d"), dram["xres"]).then_inc(d, 16)
            sp.wait_ge(d, 16)


def layer0_weights(nc, sb, s):
    w = {}
    for n, shape in (("w1h", [P, 3, T2, H0]), ("w1l", [P, 3, T2, H0]), ("w2h", [P, 3, HT0, D]), ("w2l", [P, 3, HT0, D])):
        w[n] = sb(n, shape, F32R, s)
    w["b1"] = sb("b1", [P, 3, HT0], F32, s)
    w["gwd"] = sb("gwd", [P, T2, P], F32, s)
    w["wqkT"] = sb("wqkT", [P, T2, P], F32, s)
    w["wvT"] = sb("wvT", [P, T2, DM], F32, s)
    w["wog"] = sb("wog", [DM, B, D], F32, s)
    w["maug"] = sb("maug", [DM, DM + 1], F32, s)
    w["coef"] = sb("coef", [P, 2, B], F32, s)
    w["causal"] = sb("causal", [P, P], F32, s)
    return w


def setup(nc, sb, sem, a, k, w, X, Y, dram):
    with ExitStack() as s:
        t = lambda n, shape, dt=F32: sb(n, shape, dt, s)
        zeros = t("zeros", [P, CAP * ROW // P])
        vrows = t("vrows", [VROWS, P])
        wm = t("wm", [P, 2, T2, 6 * D])
        qk_raw, v_raw, o_raw, woT = t("qk_raw", [P, D]), t("v_raw", [DM, D]), t("o_raw", [P, T2, DM]), t("woT", [DM, D])
        gw, gwd1 = t("gw", [P, 2, T2]), t("gwd1", [P, T2])
        b2, b2s = t("b2", [P, 3, T2]), t("b2s", [P, T2])
        gcol, mn, gv = t("gcol", [P, 1]), t("mn", [P, DM]), t("gv", [P, 4])
        sign = t("sign", [P, B * D])
        garow = t("garow", [DM, B, D])
        raw = t("raw", [P, 2, 2048])

        x_in, small_in, wm_in = (sem(n, s) for n in ("x_in", "small_in", "wm_in"))
        raw_in = [sem(f"raw_in{i}", s) for i in range(2)]
        zero_out = sem("zero_out", s)
        pool_did, act_did, vec_did, pe_did = (sem(n, s) for n in ("setup_pool", "setup_act", "setup_vec", "setup_pe"))
        V = Steps(["ones", "zeros", "gwdiff", "gwd", "b2a", "b2b", "scale1", "gbge", "gbsign", "gbabs", "gb", "gbb",
                   "nsum", "flag", "den", "g", "gflag", "omg", "coef",
                   "gage", "gasign", "gaabs", "ga", "wog"] + [f"lo{i}" for i in range(6)])
        A = Steps(["silu", "b1", "b2", "gw", "eg", "qkT", "vT", "woT", "mod"] + [f"hi{i}" for i in range(6)])
        G = Steps("mhalf ident0 ident causal0 causal")
        T = Steps("wT mod garow")
        block = s.enter_context(nc.Block())

        srcs = []
        for e in range(3):
            w1 = a["L0_ffn_sw1"] if e == 0 else a["L0_ffn_w1"][e - 1]
            w2 = a["L0_ffn_sw2"] if e == 0 else a["L0_ffn_w2"][e - 1]
            srcs.append((w1.rearrange("(t p) n -> p t n", p=P), w["w1h"][:, e], w["w1l"][:, e], H0))
            srcs.append((w2.rearrange("(h p) n -> p h n", p=P), w["w2h"][:, e], w["w2l"][:, e], D))
        raws = [raw[:, i % 2, :].rearrange("p (t n) -> p t n", n=srcs[i][3]) for i in range(6)]

        @block.sync
        def _(sp):
            for l in range(2):
                sp.dma_start(wm[:, l], a[f"L{l}_wmod"].rearrange("(t p) n -> p t n", p=P)).then_inc(wm_in, 16)
            for c in range(NC):
                sp.dma_start(k["x"][:, :, c, 0:D],
                             a["L0_attn_hidden_states"].rearrange("b (c p) d -> p b c d", p=P)[:, :, c, :]).then_inc(x_in, 16)
            for i, (src, _, _, n) in enumerate(srcs):
                if i >= 2:
                    sp.wait_ge(vec_did, V(0, f"lo{i - 2}"))
                sp.dma_start(raws[i], src).then_inc(raw_in[i % 2], 16)
            sp.wait_ge(x_in, 16 * NC)

        @block.gpsimd
        def _(pool):
            pool.memset(k["mhalf"][:], -0.5).then_inc(pool_did, 1)
            pool.memset(k["ident"][:], 0.0).then_inc(pool_did, 1)
            pool.wait_ge(pool_did, G(0, "ident0"))
            pool.affine_select(out=k["ident"][:], in_=k["ident"][:], compare_op=ALU.not_equal, fill=1.0,
                               base=0, pattern=[[-1, P]], channel_multiplier=1).then_inc(pool_did, 1)
            pool.memset(w["causal"][:], 1.0).then_inc(pool_did, 1)
            pool.wait_ge(pool_did, G(0, "causal0"))
            pool.affine_select(out=w["causal"][:], in_=w["causal"][:], compare_op=ALU.is_ge, fill=0.0,
                               base=0, pattern=[[1, P]], channel_multiplier=-1).then_inc(pool_did, 1)

        @block.scalar
        def _(act):
            n = 0
            for dst, src in (
                (qk_raw[0:DM, :], a["L0_attn_w_q"]), (qk_raw[DM:P, :], a["L0_attn_w_k"]), (v_raw[:], a["L0_attn_w_v"]),
                (o_raw[:], a["L0_attn_w_o"].rearrange("(t p) m -> p t m", p=P)),
                (w["maug"][:, 0:DM], a["L0_attn_memory"]),
                (w["maug"][:, DM:DM + 1], a["L0_attn_memory_norm"].rearrange("(p o) -> p o", o=1)),
                (mn[:], a["L0_attn_memory_norm"].partition_broadcast(P)),
                (gcol[:], a["L0_attn_gate"].partition_broadcast(P)),
                (vrows[0:8], a["L0_ffn_sb1"].rearrange("(h p) -> h p", p=P)),
                (vrows[8:24], a["L0_ffn_b1"].rearrange("e (h p) -> (e h) p", p=P)),
                (vrows[24:26], a["L0_ffn_sb2"].rearrange("(t p) -> t p", p=P)),
                (vrows[26:30], a["L0_ffn_b2"].rearrange("e (t p) -> (e t) p", p=P)),
                (vrows[30:38], a["L0_c"].rearrange("b (t p) -> (b t) p", p=P)),
                (vrows[38:46], a["L1_c"].rearrange("b (t p) -> (b t) p", p=P)),
                (vrows[46:50], a["L0_ffn_gate_w"].rearrange("e (t p) -> (e t) p", p=P)),
            ):
                act.dma_start(dst, src).then_inc(small_in, 16)
                n += 16
            assert n == SMALL_LOADS * 16
            act.wait_ge(vec_did, V(0, "zeros"))
            for e in range(E1):
                act.dma_start(dram["rows"][e * CAP:(e + 1) * CAP].rearrange("(p q) r -> p (q r)", p=P), zeros[:]).then_inc(zero_out, 16)
            act.wait_ge(pe_did, T(0, "wT"))
            nc.scalar.activation(k["scb"][:], X[:, 3, 30:46].rearrange("p (l b t) -> p l b t", l=2, b=B), ACT.Silu).then_inc(act_did, 1)
            nc.scalar.copy(w["b1"][:], X[:, 3, 0:24].rearrange("p (e h) -> p e h", e=3)).then_inc(act_did, 1)
            nc.scalar.copy(b2[:], X[:, 3, 24:30].rearrange("p (e t) -> p e t", e=3)).then_inc(act_did, 1)
            nc.scalar.copy(gw[:], X[:, 3, 46:50].rearrange("p (e t) -> p e t", e=2)).then_inc(act_did, 1)
            nc.scalar.activation(gv[:, 0:1], gcol[:], ACT.Exp, scale=-1.0).then_inc(act_did, 1)
            nc.scalar.copy(w["wqkT"][:], X[:, 0, 0:2 * P].rearrange("p (t n) -> p t n", t=T2)).then_inc(act_did, 1)
            nc.scalar.copy(w["wvT"][:], X[:, 1, 0:2 * DM].rearrange("p (t n) -> p t n", t=T2)).then_inc(act_did, 1)
            nc.scalar.copy(woT[:], X[0:DM, 2, 0:D]).then_inc(act_did, 1)
            act.wait_ge(pe_did, T(0, "mod"))
            nc.scalar.copy(k["mod"][:], X[:, 3, 64:160].rearrange("p (l j t b) -> p l j t b", l=2, j=6, t=T2)).then_inc(act_did, 1)
            for i, (_, hi, _, n) in enumerate(srcs):
                act.wait_ge(raw_in[i % 2], 16 * (i // 2 + 1))
                nc.scalar.copy(hi, raws[i]).then_inc(act_did, 1)
            act.wait_ge(zero_out, 16 * E1)

        @block.tensor
        def _(pe):
            pe.wait_ge(pool_did, G(0, "ident"))
            pe.wait_ge(small_in, 16 * SMALL_LOADS)
            pe.transpose(X[:, 3, 0:VROWS], vrows[:], k["ident"][0:VROWS, 0:VROWS])
            for t_ in range(T2):
                pe.transpose(X[:, 0, t_ * P:(t_ + 1) * P], qk_raw[:, t_ * P:(t_ + 1) * P], k["ident"][:])
                pe.transpose(X[:, 1, t_ * DM:(t_ + 1) * DM], v_raw[:, t_ * P:(t_ + 1) * P], k["ident"][0:DM, 0:DM])
                ins = pe.transpose(X[0:DM, 2, t_ * P:(t_ + 1) * P], o_raw[:, t_, :], k["ident"][:])
            ins.then_inc(pe_did, 1)
            pe.wait_ge(act_did, A(0, "gw"))
            pe.wait_ge(wm_in, 32)
            for l in range(2):
                for jt in range(12):
                    o = X[:, 3, 64 + 48 * l + 4 * jt:64 + 48 * l + 4 * jt + 4]
                    for t_ in range(T2):
                        ins = pe.matmul(o, wm[:, l, t_, jt * P:(jt + 1) * P], k["scb"][:, l, :, t_],
                                        start=t_ == 0, stop=t_ == T2 - 1)
            ins.then_inc(pe_did, 1)
            mod_rows(pe, Y, wm[:, 0], k["scb"][:, 0], 2, DM).then_inc(pe_did, 1)

        @block.vector
        def _(v):
            v.memset(k["ones"][:], 1.0).then_inc(vec_did, 1)
            v.memset(zeros[:], 0.0).then_inc(vec_did, 1)
            v.wait_ge(act_did, A(0, "gw"))
            v.tensor_tensor(gwd1[:], gw[:, 1, :], gw[:, 0, :], ALU.subtract).then_inc(vec_did, 1)
            v.wait_ge(vec_did, V(0, "gwdiff"))
            for t_ in range(T2):
                ins = v.tensor_scalar(w["gwd"][:, t_, :], k["ones"][:], gwd1[:, t_:t_ + 1], None, ALU.mult)
            ins.then_inc(vec_did, 1)
            v.tensor_tensor(b2s[:], b2[:, 1], b2[:, 2], ALU.add).then_inc(vec_did, 1)
            v.wait_ge(vec_did, V(0, "b2a"))
            v.tensor_tensor(b2s[:], b2s[:], b2[:, 0], ALU.add).then_inc(vec_did, 1)
            v.wait_ge(act_did, A(0, "mod"))
            mod = k["mod"]
            for l in range(2):
                ins = v.tensor_scalar(mod[:, l, 1:5:3], mod[:, l, 1:5:3], 1.0, None, ALU.add)
            ins.then_inc(vec_did, 1)
            gate(v, vec_did, V, ("gbge", "gbsign", "gbabs", "gb"), mod[:, 0, 5].rearrange("p t b -> p (t b)"),
                 mod[:, 0, 2].rearrange("p t b -> p (t b)"), sign[:, 0:8])
            v.wait_ge(vec_did, V(0, "gb"))
            v.tensor_tensor(k["gbb"][:], mod[:, 0, 2], b2s[:].unsqueeze(2).to_broadcast([P, T2, B]), ALU.mult).then_inc(vec_did, 1)
            v.wait_ge(small_in, 16 * SMALL_LOADS)
            v.reduce_sum(gv[:, 1:2], mn[:], AX.X).then_inc(vec_did, 1)
            v.wait_ge(vec_did, V(0, "nsum"))
            v.tensor_scalar(gv[:, 1:2], gv[:, 1:2], MEM_EPS, None, ALU.is_ge).then_inc(vec_did, 1)
            v.wait_ge(act_did, A(0, "eg"))
            v.tensor_scalar(gv[:, 2:3], gv[:, 0:1], 1.0, None, ALU.add).then_inc(vec_did, 1)
            v.wait_ge(vec_did, V(0, "den"))
            v.reciprocal(gv[:, 2:3], gv[:, 2:3]).then_inc(vec_did, 1)
            v.wait_ge(vec_did, V(0, "g"))
            v.tensor_tensor(gv[:, 1:2], gv[:, 1:2], gv[:, 2:3], ALU.mult).then_inc(vec_did, 1)
            v.tensor_scalar(gv[:, 3:4], gv[:, 2:3], -1.0, 1.0, ALU.mult, ALU.add).then_inc(vec_did, 1)
            v.wait_ge(vec_did, V(0, "omg"))
            v.tensor_scalar(w["coef"][:, 0, :], k["ones"][:, 0:B], gv[:, 1:2], None, ALU.mult)
            v.tensor_scalar(w["coef"][:, 1, :], k["ones"][:, 0:B], gv[:, 3:4], None, ALU.mult).then_inc(vec_did, 1)
            v.wait_ge(pe_did, T(0, "garow"))
            gate(v, vec_did, V, ("gage", "gasign", "gaabs", "ga"), Y[0:DM, 0:2].rearrange("p a n -> p (a n)"),
                 garow[:].rearrange("p b d -> p (b d)"), sign[0:DM, :])
            v.wait_ge(vec_did, V(0, "ga"))
            v.wait_ge(act_did, A(0, "woT"))
            v.tensor_tensor(w["wog"][:], garow[:], woT[:].unsqueeze(1).to_broadcast([DM, B, D]), ALU.mult).then_inc(vec_did, 1)
            for i, (_, hi, lo, n) in enumerate(srcs):
                v.wait_ge(act_did, A(0, f"hi{i}"))
                v.tensor_tensor(lo, raws[i], hi.bitcast(F32), ALU.subtract).then_inc(vec_did, 1)


SMALL_LOADS = 15
VROWS = 50


def mod_rows(pe, Y, wm, scb, j, m):
    for b in range(B):
        for t_ in range(T2):
            ins = pe.matmul(Y[0:m, b // 2, (b % 2) * D:(b % 2 + 1) * D], scb[:, b, t_:t_ + 1].to_broadcast([P, m]),
                            wm[:, t_, j * D:(j + 1) * D], start=t_ == 0, stop=t_ == T2 - 1)
    return ins


def gate(v, done, V, steps, src, dst, sign):
    v.tensor_scalar(sign, src, 0.0, None, ALU.is_ge).then_inc(done, 1)
    v.wait_ge(done, V(0, steps[0]))
    v.tensor_scalar(sign, sign, 2.0, -1.0, ALU.mult, ALU.add).then_inc(done, 1)
    v.wait_ge(done, V(0, steps[1]))
    v.tensor_tensor(dst, src, sign, ALU.mult).then_inc(done, 1)
    v.wait_ge(done, V(0, steps[2]))
    v.scalar_tensor_tensor(out=dst, in0=dst, scalar=0.25, in1=sign, op0=ALU.max, op1=ALU.mult).then_inc(done, 1)


LN_VEC = "stats aggr eps sq sqv half rstd xn".split()
LN_POOL = ["pow"]


class Norm:

    def __init__(self, sb, sem, s, name):
        self.st = sb(f"{name}_stats", [P, B, 6], F32, s)
        self.mv = sb(f"{name}_meanvar", [P, B, 2], F32, s)
        self.ve = sb(f"{name}_vareps", [P, B], F32, s)
        self.y = sb(f"{name}_y", [P, B], F32, s)
        self.q = sb(f"{name}_q", [P, B], F32, s)
        self.seen = sem(f"{name}_seen", s)


def norm_stats(v, ln, done, V, c, x):
    apart(v, done, V(c - 1, "xn"), ln.seen)
    for b in range(B):
        ins = v.bn_stats(ln.st[:, b, :], x[:, b, c, 0:D])
    ins.then_inc(done, 1)
    apart(v, done, V(c, "stats"), ln.seen)
    for b in range(B):
        ins = v.bn_aggr(ln.mv[:, b, :], ln.st[:, b, :])
    ins.then_inc(done, 1)
    v.wait_ge(done, V(c, "aggr"))
    v.tensor_scalar(ln.ve[:], ln.mv[:, :, 1], LN_EPS, None, ALU.add).then_inc(done, 1)


def norm_vector(v, ln, done, V, c, x, xn, pool, pow_count, free, free_count):
    v.wait_ge(pool, pow_count)
    v.tensor_tensor(ln.q[:], ln.y[:], ln.y[:], ALU.mult).then_inc(done, 1)
    v.wait_ge(done, V(c, "sq"))
    v.tensor_tensor(ln.q[:], ln.q[:], ln.ve[:], ALU.mult).then_inc(done, 1)
    v.wait_ge(done, V(c, "sqv"))
    v.tensor_scalar(ln.q[:], ln.q[:], -0.5, 1.5, ALU.mult, ALU.add).then_inc(done, 1)
    v.wait_ge(done, V(c, "half"))
    v.tensor_tensor(ln.y[:], ln.y[:], ln.q[:], ALU.mult).then_inc(done, 1)
    v.wait_ge(done, V(c, "rstd"))
    reach(v, free, free_count)
    for b in range(B):
        ins = v.tensor_scalar(xn[:, b, :], x[:, b, c, 0:D], ln.mv[:, b, 0:1], ln.y[:, b:b + 1], ALU.subtract, ALU.mult)
    ins.then_inc(done, 1)


def norm_pool(pool, ln, done, mhalf, vec, vec_count):
    pool.wait_ge(vec, vec_count)
    pool.tensor_tensor(ln.y[:], ln.ve[:], mhalf[:], ALU.pow).then_inc(done, 1)


def transpose_chunk(pe, X, src, ident):
    for b in range(B):
        for t in range(T2):
            ins = pe.transpose(X[:, t, b * P:(b + 1) * P], src[:, b, t * P:(t + 1) * P], ident[:])
    return ins


def modulate(act, dst, X, mod, scale, shift):
    for b in range(B):
        for t in range(T2):
            ins = act.activation(dst[:, t, b * P:(b + 1) * P], X[:, t, b * P:(b + 1) * P], ACT.Identity,
                                 bias=mod[:, shift, t, b:b + 1], scale=mod[:, scale, t, b:b + 1])
    return ins


def product3(pe, out, wh, wl, xh, xl, start, stop):
    pe.matmul(out, wh, xh, start=start, stop=False)
    pe.matmul(out, wh, xl, start=False, stop=False)
    return pe.matmul(out, wl, xh, start=False, stop=stop)


def layer0(nc, sb, sem, k, w, X, Y):
    with ExitStack() as s:
        t = lambda n, shape, dt=F32: sb(n, shape, dt, s)
        x, mod, ident = k["x"], k["mod"][:, 0], k["ident"]
        lna, lnf = Norm(sb, sem, s, "lna"), Norm(sb, sem, s, "lnf")
        xn = t("xn", [P, B, D])
        hT = t("a_hT", [P, T2, TOK])
        ex, sg = t("a_exp", [DM, 2, TOK]), t("a_sigma", [DM, 2, TOK])
        vaug = t("a_v", [P, B, DM + 1])
        amask = t("a_scores", [P, B, P])
        ktok = t("a_ktok", [P, B, DM])
        state = t("a_state", [DM, B, DM + 1])
        rd = t("a_rden", [P, 2, B])
        memn, comb = t("a_mem", [P, B, DM]), t("a_comb", [P, B, DM])
        cT = t("a_combT", [DM, TOK])
        hF = t("f_h", [P, T2, TOK])
        hS = t("f_hS", [P, 2, T2, TOK], F32R)
        hE = t("f_hE", [P, 2, T2, TOK], F32R)
        masks = t("f_masks", [P, 2, TOK], BF16)
        hid = t("f_hid", [P, 2, TOK])
        hidh, hidl = t("f_hidh", [P, 3, TOK], F32R), t("f_hidl", [P, 3, TOK], F32R)
        y = t("f_y", [P, T2, TOK])

        av, ap, aa, at = (sem(n, s) for n in ("attn_vec", "attn_pool", "attn_act", "attn_pe"))
        iv, ip, ia, it = (sem(n, s) for n in ("input_vec", "input_pool", "input_act", "input_pe"))
        low, masked, fa, ups, downs = (sem(n, s) for n in ("ffn_low_parts", "ffn_masked_inputs", "ffn_act", "ffn_ups", "ffn_downs"))
        rv, ra, rt = (sem(n, s) for n in ("result_vec", "result_act", "result_pe"))
        AV = Steps(LN_VEC + "sigma masked ktok state den recip coef mem loc comb x".split())
        AP, IP = Steps(LN_POOL), Steps(LN_POOL)
        AA = Steps("h neg relu exp v combT")
        AT = Steps("xT qk v scores kT mem loc state combT out")
        IV, IA, IT = Steps(LN_VEC + "mask0 mask1 hi lo".split()), Steps("h"), Steps("xT gate")
        MK = Steps("e0h e0l e1h e1l")
        STEP = Steps([f"{i}" for i in range(NSTEP)])
        FA = Steps([n for i in range(NSTEP) for n in (f"relu{i}", f"hi{i}")])
        RES = Steps("done")
        init, seen = sem("layer0_init", s), sem("attn_seen_pe", s)
        block = s.enter_context(nc.Block())
        X2 = X[:, 0:2].rearrange("p a n -> p (a n)")

        def step(c, i):
            return STEP(c, "0") + i

        def pipeline(eng, start, turn, end):
            start()
            turn(0, True, False)
            with eng.Fori(1, NC - 1) as c:
                turn(c, True, True)
            turn(NC - 1, False, True)
            end()

        @block.gpsimd
        def _(pool):
            def mask(c):
                pool.wait_ge(iv, IV(c, "lo"))
                reach(pool, ups, step(c, -HT0 - 1))
                for i in (0, 1):
                    pool.tensor_tensor(hE[:, i], hS[:, i].bitcast(F32), masks[:, 0:1].to_broadcast([P, T2, TOK]), ALU.mult).then_inc(masked, 1)

            def mask_rest(c):
                pool.wait_ge(ups, step(c, HT0 - 1))
                pool.wait_ge(masked, MK(c, "e0l"))
                for i in (0, 1):
                    pool.tensor_tensor(hS[:, i], hS[:, i].bitcast(F32), masks[:, 1:2].to_broadcast([P, T2, TOK]), ALU.mult).then_inc(masked, 1)

            def start():
                norm_pool(pool, lna, ap, k["mhalf"], av, AV(0, "eps"))
                norm_pool(pool, lnf, ip, k["mhalf"], iv, IV(0, "eps"))

            def turn(c, ahead, behind):
                mask(c)
                if ahead:
                    norm_pool(pool, lna, ap, k["mhalf"], av, AV(c + 1, "eps"))
                mask_rest(c)
                if ahead:
                    norm_pool(pool, lnf, ip, k["mhalf"], iv, IV(c + 1, "eps"))
            pipeline(pool, start, turn, lambda: None)

        @block.scalar
        def _(act):
            def attn_h(c):
                act.wait_ge(at, AT(c, "xT"))
                modulate(act, hT, X, mod, 1, 0).then_inc(aa, 1)

            def attn_sigma(c):
                act.wait_ge(at, AT(c, "qk"))
                qk = X[0:DM, 2:4]
                act.activation(ex[:], qk, ACT.Relu, scale=-1.0).then_inc(aa, 1)
                act.activation(sg[:], qk, ACT.Relu).then_inc(aa, 1)
                act.wait_ge(aa, AA(c, "neg"))
                act.activation(ex[:], ex[:], ACT.Exp, scale=-1.0).then_inc(aa, 1)
                act.wait_ge(at, AT(c, "v"))
                act.wait_ge(init, 2)
                act.copy(vaug[:, :, 0:DM], X[:, 0, 0:B * DM].rearrange("p (b d) -> p b d", b=B)).then_inc(aa, 1)

            def attn_comb(c):
                act.wait_ge(at, AT(c, "combT"))
                act.copy(cT[:], X[0:DM, 2]).then_inc(aa, 1)

            def inputs(c):
                act.wait_ge(it, IT(c, "xT"))
                modulate(act, hF, X, mod, 4, 3).then_inc(ia, 1)

            def hidden(c, i):
                e, h = divmod(i, HT0)
                act.wait_ge(ups, step(c, i))
                reach(act, low, step(c, i - 2))
                act.activation(hid[:, i % 2], Y[:, i % 2], ACT.Relu, bias=w["b1"][:, e, h:h + 1]).then_inc(fa, 1)
                reach(act, downs, step(c, i - 3))
                act.wait_ge(fa, FA(c, f"relu{i}"))
                act.copy(hidh[:, i % 3], hid[:, i % 2]).then_inc(fa, 1)

            def result(c):
                act.wait_ge(downs, step(c, NSTEP - 1))
                for b in range(B):
                    for t_ in range(T2):
                        ins = act.activation(y[:, t_, b * P:(b + 1) * P], Y[:, 2 + t_, b * P:(b + 1) * P], ACT.Identity,
                                             bias=k["gbb"][:, t_, b:b + 1], scale=mod[:, 2, t_, b:b + 1])
                ins.then_inc(ra, 1)

            def start():
                attn_h(0)
                attn_sigma(0)
                attn_comb(0)
                inputs(0)

            def turn(c, ahead, behind):
                for i in range(NSTEP):
                    hidden(c, i)
                    if behind and i == 1:
                        result(c - 1)
                    if ahead and i == 4:
                        attn_h(c + 1)
                    if ahead and i == 6:
                        attn_sigma(c + 1)
                    if ahead and i == 14:
                        attn_comb(c + 1)
                    if ahead and i == 19:
                        inputs(c + 1)
            pipeline(act, start, turn, lambda: result(NC - 1))

        @block.vector
        def _(v):
            v.memset(state[:], 0.0).then_inc(init, 1)
            v.memset(vaug[:, :, DM:DM + 1], 1.0).then_inc(init, 1)
            mem = X[:, 3, 0:B * (DM + 1)].rearrange("p (b d) -> p b d", b=B)
            loc = X[:, 0, 0:B * (DM + 1)].rearrange("p (b d) -> p b d", b=B)

            def attn_stats(c):
                norm_stats(v, lna, av, AV, c, x)

            def attn_norm(c):
                norm_vector(v, lna, av, AV, c, x, xn, ap, AP(c, "pow"), it, IT(c - 1, "xT"))

            def attn_sigma(c):
                v.wait_ge(aa, AA(c, "exp"))
                v.tensor_tensor(sg[:], ex[:], sg[:], ALU.add).then_inc(av, 1)

            def attn_scores(c):
                v.wait_ge(at, AT(c, "scores"))
                v.tensor_tensor(amask[:], X[:, 1].rearrange("p (b q) -> p b q", b=B),
                                w["causal"][:].unsqueeze(1).to_broadcast([P, B, P]), ALU.mult).then_inc(av, 1)
                v.wait_ge(at, AT(c, "kT"))
                v.tensor_copy(ktok[:], X[:, 2, 0:B * DM].rearrange("p (b d) -> p b d", b=B)).then_inc(av, 1)

            def attn_weights(c):
                v.wait_ge(at, AT(c, "state"))
                v.wait_ge(init, 2)
                v.tensor_tensor(state[:], state[:], X[0:DM, 1, 0:B * (DM + 1)].rearrange("p (b d) -> p b d", b=B), ALU.add).then_inc(av, 1)
                v.tensor_scalar(rd[:, 0, :], mem[:, :, DM], MEM_EPS, None, ALU.max)
                v.tensor_scalar(rd[:, 1, :], loc[:, :, DM], MEM_EPS, None, ALU.max).then_inc(av, 1)
                v.wait_ge(av, AV(c, "den"))
                v.reciprocal(rd[:], rd[:]).then_inc(av, 1)
                v.wait_ge(av, AV(c, "recip"))
                v.tensor_tensor(rd[:], rd[:], w["coef"][:], ALU.mult).then_inc(av, 1)

            def attn_combine(c):
                v.wait_ge(av, AV(c, "coef"))
                v.tensor_tensor(memn[:], mem[:, :, 0:DM], rd[:, 0, :].unsqueeze(2).to_broadcast([P, B, DM]), ALU.mult).then_inc(av, 1)
                v.tensor_tensor(comb[:], loc[:, :, 0:DM], rd[:, 1, :].unsqueeze(2).to_broadcast([P, B, DM]), ALU.mult).then_inc(av, 1)
                v.wait_ge(av, AV(c, "loc"))
                v.tensor_tensor(comb[:], comb[:], memn[:], ALU.add).then_inc(av, 1)

            def attn_add(c):
                v.wait_ge(at, AT(c, "out"))
                v.tensor_tensor(x[:, :, c, 0:D], x[:, :, c, 0:D], X2.rearrange("p (b d) -> p b d", b=B), ALU.add).then_inc(av, 1)

            def input_stats(c):
                apart(v, av, AV(c, "x"), lnf.seen)
                norm_stats(v, lnf, iv, IV, c, x)

            def input_norm(c):
                norm_vector(v, lnf, iv, IV, c, x, xn, ip, IP(c, "pow"), at, AT(c, "xT"))

            def input_masks(c):
                v.wait_ge(it, IT(c, "gate"))
                reach(v, masked, MK(c - 1, "e1l"))
                v.tensor_scalar(masks[:, 0, :], X[:, 2], 0.0, None, ALU.is_le).then_inc(iv, 1)
                v.tensor_scalar(masks[:, 1, :], X[:, 2], 0.0, None, ALU.is_gt).then_inc(iv, 1)

            def inputs(c):
                v.wait_ge(ia, IA(c, "h"))
                reach(v, ups, step(c, -1))
                v.tensor_copy(hS[:, 0], hF[:]).then_inc(iv, 1)
                v.wait_ge(iv, IV(c, "hi"))
                v.tensor_tensor(hS[:, 1], hF[:], hS[:, 0].bitcast(F32), ALU.subtract).then_inc(iv, 1)

            def hidden(c, i):
                v.wait_ge(fa, FA(c, f"hi{i}"))
                v.tensor_tensor(hidl[:, i % 3], hid[:, i % 2], hidh[:, i % 3].bitcast(F32), ALU.subtract).then_inc(low, 1)

            def result(c):
                v.wait_ge(rt, RES(c, "done"))
                v.tensor_tensor(x[:, :, c, 0:D], x[:, :, c, 0:D], X2.rearrange("p (b d) -> p b d", b=B), ALU.add).then_inc(rv, 1)

            def start():
                for part in (attn_stats, attn_norm, attn_sigma, attn_scores, attn_weights, attn_combine, attn_add,
                             input_stats, input_norm, input_masks, inputs):
                    part(0)

            def turn(c, ahead, behind):
                for i in range(NSTEP):
                    if ahead and i == NSTEP - 1:
                        inputs(c + 1)
                    hidden(c, i)
                    if ahead and i == 1:
                        attn_stats(c + 1)
                    if ahead and i == 2:
                        attn_norm(c + 1)
                    if behind and i == 3:
                        result(c - 1)
                    if ahead and i == 7:
                        attn_sigma(c + 1)
                    if ahead and i == 9:
                        attn_scores(c + 1)
                    if ahead and i == 11:
                        attn_weights(c + 1)
                    if ahead and i == 12:
                        attn_combine(c + 1)
                    if ahead and i == 16:
                        attn_add(c + 1)
                        input_stats(c + 1)
                    if ahead and i == 17:
                        input_norm(c + 1)
                    if ahead and i == 21:
                        input_masks(c + 1)
            pipeline(v, start, turn, lambda: result(NC - 1))

        @block.tensor
        def _(pe):
            bs = [slice(b * P, (b + 1) * P) for b in range(B)]
            aug = [slice(b * (DM + 1), (b + 1) * (DM + 1)) for b in range(B)]
            dm = [slice(b * DM, (b + 1) * DM) for b in range(B)]

            def attn_in(c):
                pe.wait_ge(av, AV(c, "xn"))
                reach(pe, rv, RES(c - 2, "done"))
                transpose_chunk(pe, X, xn, ident).then_inc(at, 1)

            def attn_qkv(c):
                pe.wait_ge(aa, AA(c, "h"))
                for i in range(2):
                    for t_ in range(T2):
                        ins = pe.matmul(X[0:DM, 2 + i], w["wqkT"][:, t_, i * DM:(i + 1) * DM], hT[:, t_, :], start=t_ == 0, stop=t_ == T2 - 1)
                ins.then_inc(at, 1)
                for b in range(B):
                    for t_ in range(T2):
                        ins = pe.matmul(X[:, 0, dm[b]], hT[:, t_, bs[b]], w["wvT"][:, t_, :], start=t_ == 0, stop=t_ == T2 - 1)
                ins.then_inc(at, 1)

            def attn_scores(c):
                pe.wait_ge(av, AV(c, "sigma"))
                for b in range(B):
                    ins = pe.matmul(X[:, 1, bs[b]], sg[:, 1, bs[b]], sg[:, 0, bs[b]], start=True, stop=True)
                ins.then_inc(at, 1)
                for b in range(B):
                    ins = pe.transpose(X[:, 2, dm[b]], sg[:, 1, bs[b]], ident[0:DM, 0:DM])
                ins.then_inc(at, 1)
                for b in range(B):
                    ins = pe.matmul(X[:, 3, aug[b]], sg[:, 0, bs[b]], w["maug"][:], start=True, stop=True)
                ins.then_inc(at, 1)

            def attn_values(c):
                pe.wait_ge(aa, AA(c, "v"))
                pe.wait_ge(av, AV(c, "masked"))
                for b in range(B):
                    pe.matmul(X[:, 0, aug[b]], amask[:, b, :], vaug[:, b, :], start=True, stop=False)
                    ins = pe.matmul(X[:, 0, aug[b]], sg[:, 0, bs[b]], state[:, b, :], start=False, stop=True)
                ins.then_inc(at, 1)
                pe.wait_ge(av, AV(c, "ktok"))
                for b in range(B):
                    ins = pe.matmul(X[0:DM, 1, aug[b]], ktok[:, b, :], vaug[:, b, :], start=True, stop=True)
                ins.then_inc(at, 1)

            def attn_turn(c):
                apart(pe, av, AV(c, "comb"), seen)
                for b in range(B):
                    ins = pe.transpose(X[0:DM, 2, bs[b]], comb[:, b, :], ident[:])
                ins.then_inc(at, 1)

            def attn_out(c):
                pe.wait_ge(aa, AA(c, "combT"))
                for b in range(B):
                    ins = pe.matmul(X2[:, b * D:(b + 1) * D], cT[:, bs[b]], w["wog"][:, b, :], start=True, stop=True)
                ins.then_inc(at, 1)

            def inputs_in(c):
                pe.wait_ge(iv, IV(c, "xn"))
                pe.wait_ge(av, AV(c, "x"))
                transpose_chunk(pe, X, xn, ident).then_inc(it, 1)

            def gate(c):
                pe.wait_ge(ia, IA(c, "h"))
                for t_ in range(T2):
                    ins = pe.matmul(X[:, 2], w["gwd"][:, t_, :], hF[:, t_, :], start=t_ == 0, stop=t_ == T2 - 1)
                ins.then_inc(it, 1)

            def up(c, i):
                e, h = divmod(i, HT0)
                hin = hE if e == 1 else hS
                if h == 0:
                    if e == 0:
                        pe.wait_ge(iv, IV(c, "lo"))
                    else:
                        pe.wait_ge(masked, MK(c, f"e{e - 1}l"))
                if i >= 2:
                    pe.wait_ge(fa, FA(c, f"relu{i - 2}"))
                else:
                    reach(pe, fa, FA(c - 1, f"relu{NSTEP + i - 2}"))
                for t_ in range(T2):
                    cols = slice(h * P, (h + 1) * P)
                    ins = product3(pe, Y[:, i % 2], w["w1h"][:, e, t_, cols], w["w1l"][:, e, t_, cols],
                                   hin[:, 0, t_, :], hin[:, 1, t_, :], t_ == 0, t_ == T2 - 1)
                ins.then_inc(ups, 1)

            def down(c, i):
                e, h = divmod(i, HT0)
                pe.wait_ge(low, step(c, i))
                if i == 0:
                    reach(pe, ra, RES(c - 1, "done"))
                for t_ in range(T2):
                    cols = slice(t_ * P, (t_ + 1) * P)
                    ins = product3(pe, Y[:, 2 + t_], w["w2h"][:, e, h, cols], w["w2l"][:, e, h, cols],
                                   hidh[:, i % 3], hidl[:, i % 3], i == 0, i == NSTEP - 1)
                ins.then_inc(downs, 1)

            def result(c):
                pe.wait_ge(ra, RES(c, "done"))
                for b in range(B):
                    for t_ in range(T2):
                        ins = pe.transpose(X2[:, b * D + t_ * P:b * D + (t_ + 1) * P], y[:, t_, bs[b]], ident[:])
                ins.then_inc(rt, 1)

            def start():
                for part in (attn_in, attn_qkv, attn_scores, attn_values, attn_turn, attn_out, inputs_in, gate):
                    part(0)

            def turn(c, ahead, behind):
                for i in range(NSTEP):
                    if behind and i == 0:
                        down(c - 1, NSTEP - 2)
                    up(c, i)
                    if behind and i == 1:
                        down(c - 1, NSTEP - 1)
                    if i >= 2:
                        down(c, i - 2)
                    if behind and i == 2:
                        result(c - 1)
                    if ahead and i == 4:
                        attn_in(c + 1)
                    if ahead and i == 6:
                        attn_qkv(c + 1)
                    if ahead and i == 9:
                        attn_scores(c + 1)
                    if ahead and i == 11:
                        attn_values(c + 1)
                    if ahead and i == 14:
                        attn_turn(c + 1)
                    if ahead and i == 16:
                        attn_out(c + 1)
                    if ahead and i == 19:
                        inputs_in(c + 1)
                    if ahead and i == 21:
                        gate(c + 1)

            def end():
                down(NC - 1, NSTEP - 2)
                down(NC - 1, NSTEP - 1)
                result(NC - 1)
            pipeline(pe, start, turn, end)


def layer1_weights(nc, sb, s):
    w = {}
    w["qkvh"], w["qkvl"] = sb("qkvh", [P, T2, 3 * D], F32R, s), sb("qkvl", [P, T2, 3 * D], F32R, s)
    w["bqk"] = sb("bqk", [P, 2 * D], F32, s)
    w["bv"] = sb("bv", [P, T2], F32, s)
    w["wog"] = sb("wog1", [P, B, T2, D], F32, s)
    w["bog"] = sb("bog1", [P, B, D], F32, s)
    w["cb"], w["sb"] = sb("cbrow", [P, B, D], F32, s), sb("sbrow", [P, B, D], F32, s)
    w["rw"], w["rb"] = sb("rw", [P, T2, E1], F32, s), sb("rb", [P, E1], F32, s)
    w["hm"] = sb("headmask", [P, 8], F32, s)
    w["par"] = sb("parity", [P, 2], F32, s)
    return w


def setup1(nc, sb, sem, a, k, w, X, Y):
    with ExitStack() as s:
        t = lambda n, shape, dt=F32: sb(n, shape, dt, s)
        wm = t("wm1", [P, T2, 6 * D])
        qkv, wout, bout = t("qkv_raw", [P, T2, 3 * D]), t("wout_raw", [P, T2, D]), t("bout_raw", [P, D])
        sign, garow = t("sign1", [P, B * D]), t("garow1", [P, B, D])
        loads = sem("loads1", s)
        act_did, vec_did, pe_did = (sem(n, s) for n in ("setup1_act", "setup1_vec", "setup1_pe"))
        V = Steps("hm par0 par1 lo gage gasign gaabs ga wog bog gbge gbsign gbabs gb")
        A = Steps("hi sb cb")
        T = Steps("ga sb cb gb")
        N = 9 * 16
        block = s.enter_context(nc.Block())

        @block.sync
        def _(sp):
            for dst, src in (
                (wm[:], a["L1_wmod"].rearrange("(t p) n -> p t n", p=P)),
                (qkv[:], a["L1_attn_W_qkv"].rearrange("(t p) n -> p t n", p=P)),
                (w["bqk"][:], a["L1_attn_b_qkv"][0:2 * D].partition_broadcast(P)),
                (w["bv"][:, 0:1], a["L1_attn_b_qkv"][2 * D:2 * D + P].rearrange("(p o) -> p o", o=1)),
                (w["bv"][:, 1:2], a["L1_attn_b_qkv"][2 * D + P:3 * D].rearrange("(p o) -> p o", o=1)),
                (wout[:], a["L1_attn_W_out"].rearrange("(t p) n -> p t n", p=P)),
                (bout[:], a["L1_attn_b_out"].partition_broadcast(P)),
                (w["rw"][:], a["L1_ffn_router_w"].rearrange("(t p) n -> p t n", p=P)),
                (w["rb"][:], a["L1_ffn_router_b"].partition_broadcast(P)),
            ):
                sp.dma_start(dst, src).then_inc(loads, 16)
            sp.wait_ge(loads, N)

        @block.scalar
        def _(act):
            act.wait_ge(loads, N)
            act.copy(w["qkvh"][:], qkv[:]).then_inc(act_did, 1)
            act.wait_ge(pe_did, T(0, "sb"))
            act.copy(w["sb"][:].rearrange("p b d -> p (b d)"), X[:, 0:2].rearrange("p a n -> p (a n)")).then_inc(act_did, 1)
            act.wait_ge(pe_did, T(0, "cb"))
            act.add(w["cb"][:].rearrange("p b d -> p (b d)"), X[:, 2:4].rearrange("p a n -> p (a n)"), 1.0).then_inc(act_did, 1)

        @block.tensor
        def _(pe):
            pe.wait_ge(loads, N)
            scb = k["scb"][:, 1]
            mod_rows(pe, Y[:, 0:2], wm, scb, 2, P).then_inc(pe_did, 1)
            mod_rows(pe, X[:, 0:2], wm, scb, 3, P).then_inc(pe_did, 1)
            mod_rows(pe, X[:, 2:4], wm, scb, 4, P).then_inc(pe_did, 1)
            mod_rows(pe, Y[:, 2:4], wm, scb, 5, P).then_inc(pe_did, 1)

        @block.vector
        def _(v):
            v.reduce_sum(w["hm"][:], k["ident"][:].rearrange("p (h d) -> p h d", d=HD), AX.X).then_inc(vec_did, 1)
            pairs = w["hm"][:].rearrange("p (q r) -> p r q", r=2)
            v.wait_ge(vec_did, V(0, "hm"))
            for r in range(2):
                v.reduce_sum(w["par"][:, r:r + 1], pairs[:, r], AX.X).then_inc(vec_did, 1)
            v.wait_ge(act_did, A(0, "hi"))
            v.tensor_tensor(w["qkvl"][:], qkv[:], w["qkvh"][:].bitcast(F32), ALU.subtract).then_inc(vec_did, 1)
            v.wait_ge(pe_did, T(0, "ga"))
            flat = lambda ap: ap.rearrange("p b d -> p (b d)")
            gate(v, vec_did, V, ("gage", "gasign", "gaabs", "ga"), Y[:, 0:2].rearrange("p a n -> p (a n)"), flat(garow[:]), sign[:])
            v.wait_ge(vec_did, V(0, "ga"))
            for g in range(T2):
                ins = v.tensor_tensor(w["wog"][:, :, g, :], garow[:], wout[:, g:g + 1, :].to_broadcast([P, B, D]), ALU.mult)
            ins.then_inc(vec_did, 1)
            v.tensor_tensor(w["bog"][:], garow[:], bout[:].unsqueeze(1).to_broadcast([P, B, D]), ALU.mult).then_inc(vec_did, 1)
            v.wait_ge(pe_did, T(0, "gb"))
            gate(v, vec_did, V, ("gbge", "gbsign", "gbabs", "gb"), Y[:, 2:4].rearrange("p a n -> p (a n)"), flat(k["gbrow"][:]), sign[:])


def layer1_attention(nc, sb, sem, k, w, X, Y, dram):
    with ExitStack() as s:
        t = lambda n, shape, dt=F32: sb(n, shape, dt, s)
        x, mod, ident, hm, par = k["x"], k["mod"][:, 1], k["ident"], w["hm"], w["par"]
        lna, lnf = Norm(sb, sem, s, "ln1a"), Norm(sb, sem, s, "ln1f")
        R = 4 * B
        xn, xnf = t("xn1", [P, B, D]), t("xnf", [P, B, D])
        hT = t("b_hT", [P, T2, B, HC * P])
        win = t("b_win", [P, 2, T2, B, P], F32R)
        qk = t("b_qk", [P, B, 2 * D])
        raw = t("b_raw", [P, R, 2 * HD])
        sc, ex = t("b_scores", [P, R, HD]), t("b_exp", [P, R, HD])
        mx, sm = t("b_max", [P, R]), t("b_sum", [P, R])
        pr, prT = t("b_pairs", [P, R, 2, HD]), t("b_pairsT", [P, R, 2, HD])
        attT = t("b_attT", [P, R, HD])
        vT = t("b_vT", [P, T2, B * WT])
        vbd = t("b_vdiag", [P, T2, B * WT // HD, 8, HD])
        z = t("b_z", [P, B, T2, P])
        h, xp = t("c_h", [P, B, D]), t("c_x", [P, B, D])
        hfT = t("c_hT", [P, T2, TOK])
        lg, top, topi = t("c_logits", [P, B, E1]), t("c_top", [P, B, 8]), t("c_topi", [P, B, 8], U32)

        sv, sp_, sa, st = (sem(n, s) for n in ("scores_vec", "scores_pool", "scores_act", "scores_pe"))
        ov, oa, ot = (sem(n, s) for n in ("output_vec", "output_act", "output_pe"))
        nv, np_, na, nt = (sem(n, s) for n in ("norm_vec", "norm_pool", "norm_act", "norm_pe"))
        fv, fp, fa, ft = (sem(n, s) for n in ("route_vec", "route_pool", "route_act", "route_pe"))
        stored = sem("stream_stored", s)
        seen_v, seen_p = (sem(f"win_seen_{e}", s) for e in ("vec", "pool"))
        NV, NP, NA, NT_ = Steps(LN_VEC), Steps(LN_POOL), Steps("h"), Steps("xT")
        SV, SP = Steps("win0 win1 qk vdiag"), Steps("bias vdiag")
        SA, ST = Steps("win0 win1 pairs vT"), Steps("qk scores vT")
        OV = Steps("even scores max sub sum recip prob pair0 pair1 pairsT attT x")
        OA, OT = Steps("exp z"), Steps("z out")
        FV = Steps(LN_VEC + "scale h logits top topi kept".split())
        FP = Steps(LN_POOL + ["gate", "x"])
        FA, FT_ = Steps("hT keep"), Steps("hT logits")
        block = s.enter_context(nc.Block())
        Y2 = Y[:, 0:2].rearrange("p a n -> p (a n)")
        bd = lambda ap: ap.rearrange("p (b d) -> p b d", b=B)

        def norms(eng, f):
            f(0)
            with eng.Fori(1, HC) as c:
                f(c)

        def pipeline(eng, turn):
            turn(0, True, False, False, True)
            turn(1, True, True, False, True)
            turn(2, True, True, True, True)
            with eng.Fori(3, NC - 1) as c:
                turn(c, True, True, True, True)
            turn(NC - 1, True, True, True, False)
            turn(NC, False, True, True, False)
            turn(NC + 1, False, False, True, False)

        def diagonal(eng, g):
            n = B * WT // HD
            v4 = vT[:, g].rearrange("p (j o w) -> p j o w", o=1, w=HD).to_broadcast([P, n, 8, HD])
            return eng.tensor_tensor(vbd[:, g], v4, hm[:].unsqueeze(1).unsqueeze(3).to_broadcast([P, n, 8, HD]), ALU.mult)

        @block.sync
        def _(sp):
            def store(c):
                sp.wait_ge(fp, FP(c, "x"))
                sp.dma_start(dram["xres"].rearrange("(b c p) d -> p b c d", b=B, p=P)[:, :, c, :], xp[:]).then_inc(stored, 16)
            store(0)
            with sp.Fori(1, NC) as c:
                store(c)
            sp.wait_ge(stored, 16 * NC)

        @block.gpsimd
        def _(pool):
            norms(pool, lambda c: norm_pool(pool, lna, np_, k["mhalf"], nv, NV(c, "eps")))

            pool.wait_ge(nv, NV(HC - 1, "xn"))

            def bias(c):
                pool.tensor_tensor(x[:, :, c, 0:D], x[:, :, c, 0:D], w["bog"][:], ALU.add).then_inc(sp_, 1)

            def values(c):
                pool.wait_ge(sa, SA(c, "vT"))
                reach(pool, ot, OT(c - 1, "z"))
                diagonal(pool, 0).then_inc(sp_, 1)

            def route(c):
                norm_pool(pool, lnf, fp, k["mhalf"], fv, FV(c, "eps"))
                pool.wait_ge(fv, FV(c, "h"))
                reach(pool, stored, 16 * c)
                pool.tensor_tensor(xp[:], h[:], k["gbrow"][:], ALU.mult).then_inc(fp, 1)
                apart(pool, fp, FP(c, "gate"), seen_p)
                pool.tensor_tensor(xp[:], xp[:], x[:, :, c, 0:D], ALU.add).then_inc(fp, 1)

            def turn(c, a, b, d, more):
                if a:
                    bias(c)
                if d:
                    route(c - 2)
                if a:
                    values(c)
            pipeline(pool, turn)

        @block.scalar
        def _(act):
            def norm(c):
                act.wait_ge(nt, NT_(c, "xT"))
                for b in range(B):
                    for t_ in range(T2):
                        ins = act.activation(hT[:, t_, b, bass.ds(c * P, P)], Y[:, t_, b * P:(b + 1) * P], ACT.Identity,
                                             bias=mod[:, 0, t_, b:b + 1], scale=mod[:, 1, t_, b:b + 1])
                ins.then_inc(na, 1)
            norms(act, norm)
            act.wait_ge(na, NA(HC - 1, "h"))

            def window(c):
                reach(act, st, ST(c - 1, "vT"))
                for i, first in ((0, STEP), (1, 0)):
                    act.copy(win[:, 0, :, :, i * WIN:(i + 1) * WIN].rearrange("p t b n -> p (t b) n"),
                             hT[:].rearrange("p t b n -> p (t b) n")[:, :, bass.ds(c * WIN + first, WIN)]).then_inc(sa, 1)

            def pairs(c):
                act.wait_ge(st, ST(c, "scores"))
                reach(act, ov, OV(c - 1, "scores"))
                for q in range(4):
                    part = slice(32 * q, 32 * q + 32)
                    ins = act.copy(raw[part], X[part].rearrange("p b (r n) -> p (b r) n", n=P)[:, :, part])
                ins.then_inc(sa, 1)

            def values(c):
                act.wait_ge(st, ST(c, "vT"))
                reach(act, sv, SV(c - 1, "vdiag"))
                reach(act, sp_, SP(c - 1, "vdiag"))
                for g in range(T2):
                    ins = act.activation(vT[:, g], X[:, g, 0:B * WT], ACT.Identity, bias=w["bv"][:, g:g + 1])
                ins.then_inc(sa, 1)

            def exp(c):
                act.wait_ge(ov, OV(c, "sub"))
                act.activation(ex[:], sc[:], ACT.Exp, scale=HD ** -0.5).then_inc(oa, 1)

            def turned(c):
                act.wait_ge(ot, OT(c, "z"))
                act.copy(z[:].rearrange("p b g (w d q) -> p (b g w) d q", w=2, d=HD),
                         Y[:, 2:4].rearrange("p a (r q d) -> p (a r) d q", q=4, d=HD)).then_inc(oa, 1)

            def keep(c):
                act.wait_ge(fp, FP(c, "x"))
                act.copy(x[:, :, c, 0:D], h[:]).then_inc(fa, 1)

            def routed(c):
                act.wait_ge(ft, FT_(c, "hT"))
                act.copy(hfT[:].rearrange("p t n -> p (t n)"), Y[:, 0:2].rearrange("p a n -> p (a n)")).then_inc(fa, 1)

            window(0)

            def turn(c, a, b, d, more):
                if b:
                    exp(c - 1)
                if d:
                    routed(c - 2)
                if b:
                    turned(c - 1)
                if a:
                    pairs(c)
                if d:
                    keep(c - 2)
                if a:
                    values(c)
                if more:
                    window(c + 1)
            pipeline(act, turn)

        @block.vector
        def _(v):
            def norm(c):
                norm_stats(v, lna, nv, NV, c, x)
                norm_vector(v, lna, nv, NV, c, x, xn, np_, NP(c, "pow"), nt, NT_(c - 1, "xT"))
            norms(v, norm)
            v.wait_ge(na, NA(HC - 1, "h"))

            def window(c):
                for i, first in ((0, STEP), (1, 0)):
                    v.wait_ge(sa, SA(c, f"win{i}"))
                    cols = slice(i * WIN, (i + 1) * WIN)
                    hi, lo = (win[:, j, :, :, cols].rearrange("p t b n -> p (t b) n") for j in range(2))
                    v.tensor_tensor(lo, hT[:].rearrange("p t b n -> p (t b) n")[:, :, bass.ds(c * WIN + first, WIN)],
                                    hi.bitcast(F32), ALU.subtract).then_inc(sv, 1)

            def projections(c):
                v.wait_ge(st, ST(c, "qk"))
                v.tensor_tensor(qk[:], X[:], w["bqk"][:].unsqueeze(1).to_broadcast([P, B, 2 * D]), ALU.add).then_inc(sv, 1)

            def values(c):
                v.wait_ge(sa, SA(c, "vT"))
                reach(v, ot, OT(c - 1, "z"))
                diagonal(v, 1).then_inc(sv, 1)

            def less_max(c):
                v.wait_ge(sa, SA(c, "pairs"))
                v.tensor_scalar(sc[:], raw[:, :, 0:HD], par[:, 0:1], None, ALU.mult).then_inc(ov, 1)
                v.wait_ge(ov, OV(c, "even"))
                v.scalar_tensor_tensor(out=sc[:], in0=raw[:, :, HD:2 * HD], scalar=par[:, 1:2], in1=sc[:], op0=ALU.mult, op1=ALU.add).then_inc(ov, 1)
                v.wait_ge(ov, OV(c, "scores"))
                v.reduce_max(mx[:], sc[:], AX.X).then_inc(ov, 1)
                v.wait_ge(ov, OV(c, "max"))
                v.tensor_tensor(sc[:], sc[:], mx[:].unsqueeze(2).to_broadcast([P, R, HD]), ALU.subtract).then_inc(ov, 1)

            def softmax(c):
                v.wait_ge(oa, OA(c, "exp"))
                v.reduce_sum(sm[:], ex[:], AX.X).then_inc(ov, 1)
                v.wait_ge(ov, OV(c, "sum"))
                v.reciprocal(sm[:], sm[:]).then_inc(ov, 1)
                v.wait_ge(ov, OV(c, "recip"))
                v.tensor_tensor(ex[:], ex[:], sm[:].unsqueeze(2).to_broadcast([P, R, HD]), ALU.mult).then_inc(ov, 1)
                v.wait_ge(ov, OV(c, "prob"))
                for i in range(2):
                    v.tensor_scalar(pr[:, :, i, :], ex[:], par[:, i:i + 1], None, ALU.mult).then_inc(ov, 1)
                v.wait_ge(ov, OV(c, "pair1"))
                v.transpose(prT[:].rearrange("p r i d -> p (r i d)"), pr[:].rearrange("p r i d -> p (r i d)")).then_inc(ov, 1)
                v.wait_ge(ov, OV(c, "pairsT"))
                reach(v, ot, OT(c - 1, "z"))
                v.tensor_tensor(attT[:], prT[:, :, 0, :], prT[:, :, 1, :], ALU.add).then_inc(ov, 1)

            def add(c):
                v.wait_ge(ot, OT(c, "out"))
                apart(v, sp_, SP(c, "bias"), seen_v)
                v.tensor_tensor(x[:, :, c, 0:D], x[:, :, c, 0:D], bd(Y2), ALU.add).then_inc(ov, 1)

            def stats(c):
                apart(v, ov, OV(c, "x"), lnf.seen)
                norm_stats(v, lnf, fv, FV, c, x)

            def normed(c):
                norm_vector(v, lnf, fv, FV, c, x, xnf, fp, FP(c, "pow"), fv, FV(c - 1, "scale"))
                v.wait_ge(fv, FV(c, "xn"))
                reach(v, fa, FA(c - 1, "keep"))
                v.tensor_tensor(h[:], xnf[:], w["cb"][:], ALU.mult).then_inc(fv, 1)
                v.wait_ge(fv, FV(c, "scale"))
                v.tensor_tensor(h[:], h[:], w["sb"][:], ALU.add).then_inc(fv, 1)

            def logits(c):
                v.wait_ge(ft, FT_(c, "logits"))
                reach(v, fv, FV(c - 1, "kept"))
                v.tensor_tensor(lg[:], Y[:, 0, 0:B * E1].rearrange("p (b e) -> p b e", b=B),
                                w["rb"][:].unsqueeze(1).to_broadcast([P, B, E1]), ALU.add).then_inc(fv, 1)

            def largest(c):
                apart(v, fv, FV(c, "logits"), seen_v)
                for b in range(B):
                    ins = v.max(top[:, b, :], lg[:, b, :])
                ins.then_inc(fv, 1)
                apart(v, fv, FV(c, "top"), seen_v)
                for b in range(B):
                    ins = v.max_index(topi[:, b, :], top[:, b, :], lg[:, b, :])
                ins.then_inc(fv, 1)
                v.tensor_copy(k["logits"][:, :, c, :], lg[:])
                v.tensor_copy(k["top"][:, :, c, :], top[:, :, 0:2])
                v.wait_ge(fv, FV(c, "topi"))
                v.tensor_copy(k["topi"][:, :, c, :], topi[:, :, 0:2]).then_inc(fv, 1)

            window(0)

            def turn(c, a, b, d, more):
                if d:
                    stats(c - 2)
                if b:
                    less_max(c - 1)
                if d:
                    normed(c - 2)
                if b:
                    softmax(c - 1)
                if d:
                    logits(c - 2)
                if a:
                    projections(c)
                if d:
                    largest(c - 2)
                if b:
                    add(c - 1)
                if a:
                    values(c)
                if more:
                    window(c + 1)
            pipeline(v, turn)

        @block.tensor
        def _(pe):
            bs = [slice(b * P, (b + 1) * P) for b in range(B)]

            def norm(c):
                pe.wait_ge(nv, NV(c, "xn"))
                reach(pe, na, NA(c - 1, "h"))
                transpose_chunk(pe, Y, xn, ident).then_inc(nt, 1)
            norms(pe, norm)

            def projections(c):
                pe.wait_ge(sv, SV(c, "win1"))
                reach(pe, sa, SA(c - 1, "vT"))
                for b in range(B):
                    for t_ in range(T2):
                        ins = product3(pe, X[:, b], win[:, 0, t_, b, :], win[:, 1, t_, b, :],
                                       w["qkvh"][:, t_, 0:2 * D], w["qkvl"][:, t_, 0:2 * D], t_ == 0, t_ == T2 - 1)
                ins.then_inc(st, 1)

            def scores(c):
                pe.wait_ge(sv, SV(c, "qk"))
                for b in range(B):
                    for wi in range(2):
                        part = slice(WIN * (1 - wi), WIN * (2 - wi))
                        for g in range(T2):
                            r = 2 * (b % 2) + g
                            ins = pe.matmul(X[:, 2 * wi + b // 2, r * P:(r + 1) * P], qk[part, b, g * P:(g + 1) * P],
                                            qk[part, b, D + g * P:D + (g + 1) * P], start=True, stop=True)
                ins.then_inc(st, 1)

            def values(c):
                pe.wait_ge(sa, SA(c, "pairs"))
                for g in range(T2):
                    for t_ in range(T2):
                        cols = slice(2 * D + g * P, 2 * D + (g + 1) * P)
                        ins = product3(pe, X[:, g, 0:B * WT], w["qkvh"][:, t_, cols], w["qkvl"][:, t_, cols],
                                       win[:, 0, t_, :, 0:WT], win[:, 1, t_, :, 0:WT], t_ == 0, t_ == T2 - 1)
                ins.then_inc(st, 1)

            def weigh(c):
                pe.wait_ge(sv, SV(c, "vdiag"))
                pe.wait_ge(sp_, SP(c, "vdiag"))
                pe.wait_ge(ov, OV(c, "attT"))
                for b in range(B):
                    for g in range(T2):
                        o = Y[:, 2 + b // 2, (b % 2) * 2 * P + g * P:(b % 2) * 2 * P + (g + 1) * P].rearrange("p (q d) -> p q d", d=HD)
                        for j in range(WT // HD):
                            lhs = vbd[:, g, b * (WT // HD) + (j - 2) % (WT // HD)].rearrange("p h d -> p (h d)")
                            r0, r1 = 2 * b + g, 2 * (B + b) + g
                            if j < 2:
                                rhs, dst = attT[:, r0, :], o[:, j, :]
                            elif j < 4:
                                rhs, dst = attT[:, r0:r1 + 1:r1 - r0, :], o[:, j:j + 3:2, :]
                            else:
                                rhs, dst = attT[:, r1, :], o[:, j + 2, :]
                            ins = pe.matmul(dst, lhs, rhs, start=True, stop=True)
                ins.then_inc(ot, 1)

            def out(c):
                pe.wait_ge(oa, OA(c, "z"))
                reach(pe, fv, FV(c - 1, "logits"))
                for b in range(B):
                    for g in range(T2):
                        ins = pe.matmul(Y2[:, b * D:(b + 1) * D], z[:, b, g, :], w["wog"][:, b, g, :], start=g == 0, stop=g == T2 - 1)
                ins.then_inc(ot, 1)

            def turn_in(c):
                pe.wait_ge(ov, OV(c, "x"))
                pe.wait_ge(fv, FV(c, "h"))
                transpose_chunk(pe, Y, h, ident).then_inc(ft, 1)

            def logits(c):
                pe.wait_ge(fa, FA(c, "hT"))
                for b in range(B):
                    for t_ in range(T2):
                        ins = pe.matmul(Y[:, 0, b * E1:(b + 1) * E1], hfT[:, t_, bs[b]], w["rw"][:, t_, :], start=t_ == 0, stop=t_ == T2 - 1)
                ins.then_inc(ft, 1)

            def turn(c, a, b, d, more):
                if a:
                    projections(c)
                if d:
                    turn_in(c - 2)
                    logits(c - 2)
                if b:
                    weigh(c - 1)
                if a:
                    scores(c)
                if b:
                    out(c - 1)
                if a:
                    values(c)
            pipeline(pe, turn)


class Unit:

    def __init__(self, pair, q):
        self.pair, self.q = pair, q
        self.u = 2 * pair + q

    def next(self):
        return Unit(self.pair + self.q, 1 - self.q)

    def last(self):
        return Unit(self.pair - 1 + self.q, 1 - self.q)


class Swiglu:

    PRE_A, PRE_V, PRE_T = ["hin0", "hin1"], ["hin0", "hin1"], ["turn0", "turn1"]
    MAIN_A = [f"{n}{f}" for f in range(3) for n in ("silu", "hi")]
    MAIN_V = [f"{n}{f}" for f in range(3) for n in ("mul", "lo")]
    MAIN_T = [f"{n}{f}" for f in range(3) for n in ("gate", "up")]

    def __init__(self, nc, sb, sem, s, name, X, Y, ident, tiles, halves, units):
        self.X, self.Y, self.ident, self.tiles, self.halves, self.units = X, Y, ident, tiles, halves, units
        n = tiles * P
        t = lambda m, shape, dt=F32: sb(f"{name}_{m}", shape, dt, s)
        self.hin = t("hin", [P, 2, 2, T2, n], F32R)
        self.sil, self.act = t("silu", [P, 3, n]), t("act", [P, 3, n])
        self.acth, self.actl = t("acth", [P, 2, 3, n], F32R), t("actl", [P, 2, 3, n], F32R)
        self.out = t("out", [P, 2, tiles, D])
        self.pre_a, self.pre_v, self.pre_t = (sem(f"{name}_next_{e}", s) for e in ("act", "vec", "pe"))
        self.main_a, self.main_v, self.main_t = (sem(f"{name}_{e}", s) for e in ("act", "vec", "pe"))
        self.down_a, self.down_t = (sem(f"{name}_down_{e}", s) for e in ("act", "pe"))
        self.PA, self.PV, self.PT = Steps(self.PRE_A), Steps(self.PRE_V), Steps(self.PRE_T)
        self.MA, self.MV, self.MT = Steps(self.MAIN_A), Steps(self.MAIN_V), Steps(self.MAIN_T)
        self.DN = Steps([f"tile{j}" for j in range(tiles)])

    def run(self, turn, first, end):
        first(Unit(0, 0))
        turn(Unit(0, 0), True, False)
        turn(Unit(0, 1), True, True)
        with self.eng.Fori(1, self.units // 2 - 1) as i:
            turn(Unit(i, 0), True, True)
            turn(Unit(i, 1), True, True)
        turn(Unit(self.units // 2 - 1, 0), True, True)
        turn(Unit(self.units // 2 - 1, 1), False, True)
        end(Unit(self.units // 2 - 1, 1))

    def turn_in(self, pe, un, t, rows):
        if t == 0:
            reach(pe, self.pre_v, self.PV(un.u - 1, "hin1"))
        else:
            pe.wait_ge(self.pre_v, self.PV(un.u, "hin0"))
        Y2 = self.Y[:, 0:2].rearrange("p a n -> p (a n)")
        for j in range(self.tiles):
            ins = pe.transpose(Y2[:, j * P:(j + 1) * P], rows[:, j, t * P:(t + 1) * P], self.ident[:])
        ins.then_inc(self.pre_t, 1)

    def gate_up(self, pe, un, f, wg, wu):
        f0, m = FT[f]
        if f == 0:
            pe.wait_ge(self.pre_v, self.PV(un.u, "hin1"))
        for base, wt, name in ((0, wg, "gate"), (2, wu, "up")):
            if name == "gate":
                if f:
                    pe.wait_ge(self.main_a, self.MA(un.u, f"silu{f - 1}"))
                else:
                    reach(pe, self.main_a, self.MA(un.u - 1, "silu2"))
            elif f:
                pe.wait_ge(self.main_v, self.MV(un.u, f"mul{f - 1}"))
            else:
                reach(pe, self.main_v, self.MV(un.u - 1, "mul2"))
            for hf, (n0, n) in enumerate(self.halves):
                for t in range(T2):
                    ins = product3(pe, self.X[0:m, base + hf, 0:n], wt[0][:, t, f0:f0 + m], wt[1][:, t, f0:f0 + m],
                                   self.hin[:, un.q, 0, t, n0:n0 + n], self.hin[:, un.q, 1, t, n0:n0 + n], t == 0, t == T2 - 1)
            ins.then_inc(self.main_t, 1)

    def down(self, pe, un, wd):
        pe.wait_ge(self.main_v, self.MV(un.u, "lo2"))
        for j in range(self.tiles):
            if j >= 2:
                pe.wait_ge(self.down_a, self.DN(un.u, f"tile{j - 2}"))
            else:
                reach(pe, self.down_a, self.DN(un.u - 1, f"tile{self.tiles - 2 + (j + self.tiles) % 2}"))
            for f, (_, m) in enumerate(FT):
                rows = slice(j * P, (j + 1) * P)
                ins = product3(pe, self.Y[:, 2 + j % 2, 0:D], self.acth[0:m, un.q, f, rows], self.actl[0:m, un.q, f, rows],
                               wd[0][0:m, f, :], wd[1][0:m, f, :], f == 0, f == 2)
            ins.then_inc(self.down_t, 1)

    def hin_hi(self, act, un, t):
        act.wait_ge(self.pre_t, self.PT(un.u, f"turn{t}"))
        reach(act, self.main_t, self.MT(un.u - 2, "up2"))
        n = self.tiles * P
        act.copy(self.hin[:, un.q, 0, t, :], self.Y[:, 0:2].rearrange("p a n -> p (a n)")[:, 0:n]).then_inc(self.pre_a, 1)

    def psum(self, base, m):
        nh, n = len(self.halves), self.halves[0][1]
        return self.X[0:m, base:base + nh, 0:n]

    def split(self, ap):
        return ap.rearrange("p (h n) -> p h n", h=len(self.halves))

    def silu(self, act, un, f):
        m = FT[f][1]
        act.wait_ge(self.main_t, self.MT(un.u, f"gate{f}"))
        reach(act, self.main_v, self.MV(un.u - 1, f"mul{f}"))
        act.activation(self.split(self.sil[0:m, f, :]), self.psum(0, m), ACT.Silu).then_inc(self.main_a, 1)
        act.wait_ge(self.main_v, self.MV(un.u, f"mul{f}"))
        reach(act, self.down_t, self.DN(un.u - 2, f"tile{self.tiles - 1}"))
        act.copy(self.acth[0:m, un.q, f, :], self.act[0:m, f, :]).then_inc(self.main_a, 1)

    def take_down(self, act, un, scale=None, free=None):
        for j in range(self.tiles):
            act.wait_ge(self.down_t, self.DN(un.u, f"tile{j}"))
            if j == 0 and free is not None:
                reach(act, *free)
            if scale is None:
                ins = act.copy(self.out[:, un.q, j, :], self.Y[:, 2 + j % 2, 0:D])
            else:
                ins = act.mul(self.out[:, un.q, j, :], self.Y[:, 2 + j % 2, 0:D], scale[:, j:j + 1])
            ins.then_inc(self.down_a, 1)

    def hin_lo(self, v, un, t):
        v.wait_ge(self.pre_a, self.PA(un.u, f"hin{t}"))
        n = self.tiles * P
        v.tensor_tensor(self.hin[:, un.q, 1, t, :], self.Y[:, 0:2].rearrange("p a n -> p (a n)")[:, 0:n],
                        self.hin[:, un.q, 0, t, :].bitcast(F32), ALU.subtract).then_inc(self.pre_v, 1)

    def mul(self, v, un, f):
        m = FT[f][1]
        v.wait_ge(self.main_t, self.MT(un.u, f"up{f}"))
        v.wait_ge(self.main_a, self.MA(un.u, f"silu{f}"))
        v.tensor_tensor(self.split(self.act[0:m, f, :]), self.psum(2, m), self.split(self.sil[0:m, f, :]), ALU.mult).then_inc(self.main_v, 1)
        v.wait_ge(self.main_a, self.MA(un.u, f"hi{f}"))
        v.tensor_tensor(self.actl[0:m, un.q, f, :], self.act[0:m, f, :], self.acth[0:m, un.q, f, :].bitcast(F32),
                        ALU.subtract).then_inc(self.main_v, 1)


def shared_and_routing(nc, sb, sem, a, k, X, Y, dram):
    with ExitStack() as s:
        t = lambda n, shape, dt=F32: sb(n, shape, dt, s)
        x = k["x"]
        sw = Swiglu(nc, sb, sem, s, "shared", X, Y, k["ident"], 4, [(0, 4 * P)], 2 * B)
        raw = t("sw_raw", [P, 2, T2, F1])
        rawd = t("sw_rawd", [P, 3, D])
        wg = (t("sw_gh", [P, T2, F1], F32R), t("sw_gl", [P, T2, F1], F32R))
        wu = (t("sw_uh", [P, T2, F1], F32R), t("sw_ul", [P, T2, F1], F32R))
        wd = (t("sw_dh", [P, 3, D], F32R), t("sw_dl", [P, 3, D], F32R))
        rows = t("sw_rows", [P, 2, 4, D])
        NK = 2
        tri, onesb = t("tri", [P, P], BF16), t("onesb", [P, P], BF16)
        trif = t("trif", [P, P])
        ie, ief = t("ie", [P, E1], U32), t("ief", [P, E1])
        tok = t("tok", [P, NT], U32)
        ti = t("ti", [P, NK, NT])
        one_hot, prod = t("one_hot", [P, NK, NT, E1]), t("prod", [P, NK, NT, E1])
        lg, ex = t("lg", [P, NT, E1]), t("ex", [P, NT, E1])
        cnt = t("cnt", [P, NT * E1], BF16)
        keep, tot, incl = t("keep", [P, E1, NT]), t("tot", [P, E1, NT]), t("incl", [P, E1, NT])
        before = t("before", [P, NT, E1])
        z, e2, val, pos, inside = t("z", [P, NT]), t("e2", [P, NT]), t("val", [P, NK, NT]), t("pos", [P, NK, NT]), t("inside", [P, NK, NT])
        slotf, slot = t("slotf", [P, NK, NT]), t("slot", [P, NK, NT], U32)

        loads, rows_in = sem("sw_loads", s), [sem(f"sw_rows{q}", s) for q in range(2)]
        wts_a, wts_v, rt_v, rt_a, rt_t, rt_p = (sem(n, s) for n in ("sw_split_act", "sw_split_vec", "slots_vec", "slots_act", "slots_pe", "slots_pool"))
        sent = [sem(f"scattered{i}", s) for i in range(2)]
        stored = [sem(f"sw_stored{q}", s) for q in range(2)]
        RV = Steps("sub gap ti oh0 oh1 cnt keep1 keep0 tot scan excl before prod pos inside z rz p2 sum rs v1 v2 w slotf over slot tok w0 w1")
        RA = Steps("exp e2 tri ones")
        RT = Steps("count")
        RP = Steps("tri0 tri ie tok")
        block = s.enter_context(nc.Block())
        tiles = x[:].rearrange("p b c r -> p (b c) r")
        lgt = k["logits"][:].rearrange("p b c e -> p (b c) e")
        top = k["top"][:].rearrange("p b c e -> p (b c) e")
        topi = k["topi"][:].rearrange("p b c e -> p (b c) e")

        @block.sync
        def _(sp):
            sp.dma_start(raw[:, 0], a["L1_ffn_sw_gate"].rearrange("(t p) n -> p t n", p=P)).then_inc(loads, 16)
            sp.dma_start(raw[:, 1], a["L1_ffn_sw_up"].rearrange("(t p) n -> p t n", p=P)).then_inc(loads, 16)
            sp.dma_start(rawd[:, 0:2], a["L1_ffn_sw_down"][0:2 * P].rearrange("(t p) n -> p t n", p=P)).then_inc(loads, 16)
            sp.dma_start(rawd[0:F1 - 2 * P, 2], a["L1_ffn_sw_down"][2 * P:F1]).then_inc(loads, 16)

            def load(un):
                reach(sp, sw.pre_t, sw.PT(un.u - 2, "turn1"))
                sp.dma_start(rows[:, un.q], tiles[:, bass.ds(4 * un.u, 4), 0:D]).then_inc(rows_in[un.q], 16)

            def turn(un, after, before_):
                if after:
                    load(un.next())
                if before_:
                    store(un.last())

            def store(un):
                sp.wait_ge(sw.down_a, sw.DN(un.u, "tile3"))
                sp.dma_start(dram["moe"][bass.ds(un.u * 4 * P, 4 * P)].rearrange("(j p) d -> p j d", p=P), sw.out[:, un.q]).then_inc(stored[un.q], 16)
            sw.eng = sp
            sw.run(turn, load, store)
            for q in range(2):
                sp.wait_ge(stored[q], 16 * B)

        @block.gpsimd
        def _(pool):
            pool.memset(trif[:], 1.0).then_inc(rt_p, 1)
            pool.wait_ge(rt_p, RP(0, "tri0"))
            pool.affine_select(out=trif[:], in_=trif[:], compare_op=ALU.is_ge, fill=0.0, base=-1,
                               pattern=[[1, P]], channel_multiplier=-1).then_inc(rt_p, 1)
            pool.iota(ie[:], pattern=[[1, E1]], base=0, channel_multiplier=0).then_inc(rt_p, 1)
            pool.iota(tok[:], pattern=[[P, NT]], base=1, channel_multiplier=1).then_inc(rt_p, 1)
            for kk in range(NK):
                pool.wait_ge(rt_v, RV(0, f"w{kk}"))
                for tt in range(NT):
                    pool.indirect_dma_start(dram["rows"], bass.IndirectOffsetOnAxis(slot[:, kk, tt:tt + 1], 0), tiles[:, tt, :], None,
                                            bounds_check=SLOTS - 1, oob_is_err=False).then_inc(sent[kk], 16)
            for kk in range(NK):
                pool.wait_ge(sent[kk], 16 * NT)

        @block.scalar
        def _(act):
            act.wait_ge(loads, 16 * 4)
            for i, (dst, src) in enumerate(((wg[0][:], raw[:, 0]), (wu[0][:], raw[:, 1]), (wd[0][:, 0:2], rawd[:, 0:2]),
                                            (wd[0][0:F1 - 2 * P, 2], rawd[0:F1 - 2 * P, 2]))):
                act.copy(dst, src).then_inc(wts_a, 1)
            act.wait_ge(rt_v, RV(0, "gap"))
            act.activation(ex[:], lg[:], ACT.Exp).then_inc(rt_a, 1)
            act.activation(e2[:], e2[:], ACT.Exp).then_inc(rt_a, 1)
            act.wait_ge(rt_p, RP(0, "tri"))
            act.copy(tri[:], trif[:]).then_inc(rt_a, 1)
            act.copy(onesb[:], k["ones"][:]).then_inc(rt_a, 1)

            def first(un):
                for t_ in range(T2):
                    sw.hin_hi(act, un, t_)

            def turn(un, after, before_):
                sw.silu(act, un, 0)
                if before_:
                    down(un.last())
                sw.silu(act, un, 1)
                if after:
                    sw.hin_hi(act, un.next(), 0)
                sw.silu(act, un, 2)
                if after:
                    sw.hin_hi(act, un.next(), 1)

            def down(un):
                sw.take_down(act, un, free=(stored[un.q], 16 * un.pair))
            sw.eng = act
            sw.run(turn, first, down)

        def route(v):
            def did(ins):
                ins.then_inc(rt_v, 1)

            bc = lambda ap: ap.unsqueeze(2).to_broadcast([P, NT, E1])
            did(v.tensor_tensor(lg[:], lgt, top[:, :, 0:1].to_broadcast([P, NT, E1]), ALU.subtract))
            did(v.tensor_tensor(e2[:], top[:, :, 1], top[:, :, 0], ALU.subtract))
            did(v.tensor_copy(ti[:], topi[:, :, 0:NK].rearrange("p t k -> p k t")))
            v.wait_ge(rt_p, RP(0, "ie"))
            v.tensor_copy(ief[:], ie[:])
            v.wait_ge(rt_v, RV(0, "ti"))
            v.drain()
            for kk in range(NK):
                did(v.tensor_tensor(one_hot[:, kk], ief[:].unsqueeze(1).to_broadcast([P, NT, E1]), bc(ti[:, kk]), ALU.is_equal))
            v.wait_ge(rt_v, RV(0, "oh1"))
            did(v.tensor_tensor(cnt[:].rearrange("p (t e) -> p t e", e=E1), one_hot[:, 0], one_hot[:, 1], ALU.add))
            did(v.memset(keep[:], 1.0))
            v.wait_ge(rt_v, RV(0, "keep1"))
            did(v.memset(keep[:, :, 0:1], 0.0))
            v.wait_ge(rt_t, RT(0, "count"))
            did(v.tensor_copy(tot[:], X[:, 1, 0:NT * E1].rearrange("p (t e) -> p e t", e=E1)))
            v.wait_ge(rt_v, RV(0, "tot"))
            flat = lambda ap: ap.rearrange("p e t -> p (e t)")
            did(v.tensor_tensor_scan(flat(incl[:]), flat(keep[:]), flat(tot[:]), 0.0, ALU.mult, ALU.add))
            v.wait_ge(rt_v, RV(0, "scan"))
            did(v.tensor_tensor(incl[:], incl[:], tot[:], ALU.subtract))
            v.wait_ge(rt_v, RV(0, "excl"))
            did(v.tensor_tensor(before[:], X[:, 0, 0:NT * E1].rearrange("p (t e) -> p t e", e=E1), incl[:].rearrange("p e t -> p t e"), ALU.add))
            v.wait_ge(rt_v, RV(0, "before"))
            for kk in range(NK):
                ins = v.tensor_tensor(prod[:, kk], one_hot[:, kk], before[:], ALU.mult)
            did(ins)
            v.wait_ge(rt_v, RV(0, "prod"))
            did(v.reduce_sum(pos[:].rearrange("p k t -> p (k t)"), prod[:].rearrange("p k t e -> p (k t) e"), AX.X))
            v.wait_ge(rt_v, RV(0, "pos"))
            did(v.tensor_scalar(inside[:], pos[:], float(CAP), None, ALU.is_lt))
            v.wait_ge(rt_a, RA(0, "e2"))
            did(v.reduce_sum(z[:], ex[:], AX.X))
            v.wait_ge(rt_v, RV(0, "z"))
            did(v.reciprocal(z[:], z[:]))
            v.wait_ge(rt_v, RV(0, "rz"))
            did(v.tensor_tensor(e2[:], e2[:], z[:], ALU.mult))
            v.wait_ge(rt_v, RV(0, "p2"))
            did(v.scalar_tensor_tensor(out=val[:, 0], in0=z[:], scalar=1e-9, in1=e2[:], op0=ALU.add, op1=ALU.add))
            v.wait_ge(rt_v, RV(0, "sum"))
            did(v.reciprocal(val[:, 0], val[:, 0]))
            v.wait_ge(rt_v, RV(0, "rs"))
            did(v.tensor_tensor(val[:, 1], val[:, 0], e2[:], ALU.mult))
            v.wait_ge(rt_v, RV(0, "v1"))
            did(v.tensor_tensor(val[:, 0], val[:, 0], z[:], ALU.mult))
            v.wait_ge(rt_v, RV(0, "v2"))
            did(v.tensor_tensor(val[:], val[:], inside[:], ALU.mult))
            did(v.scalar_tensor_tensor(out=slotf[:], in0=ti[:], scalar=float(CAP), in1=pos[:], op0=ALU.mult, op1=ALU.add))
            v.wait_ge(rt_v, RV(0, "slotf"))
            did(v.tensor_scalar(pos[:], inside[:], -float(4 * SLOTS), float(4 * SLOTS), ALU.mult, ALU.add))
            v.wait_ge(rt_v, RV(0, "over"))
            did(v.tensor_tensor(slot[:], slotf[:], pos[:], ALU.add))
            v.wait_ge(rt_p, RP(0, "tok"))
            did(v.tensor_copy(tiles[:, :, D + 1], tok[:]))
            v.wait_ge(rt_v, RV(0, "w"))
            did(v.tensor_copy(tiles[:, :, D], val[:, 0, :]))

        @block.vector
        def _(v):
            for i, (lo, src, hi) in enumerate(((wg[1][:], raw[:, 0], wg[0][:]), (wu[1][:], raw[:, 1], wu[0][:]),
                                               (wd[1][:, 0:2], rawd[:, 0:2], wd[0][:, 0:2]),
                                               (wd[1][0:F1 - 2 * P, 2], rawd[0:F1 - 2 * P, 2], wd[0][0:F1 - 2 * P, 2]))):
                v.wait_ge(wts_a, i + 1)
                v.tensor_tensor(lo, src, hi.bitcast(F32), ALU.subtract).then_inc(wts_v, 1)
            route(v)
            def first(un):
                for t_ in range(T2):
                    sw.hin_lo(v, un, t_)

            def turn(un, after, before_):
                sw.mul(v, un, 0)
                sw.mul(v, un, 1)
                if after:
                    sw.hin_lo(v, un.next(), 0)
                sw.mul(v, un, 2)
                if after:
                    sw.hin_lo(v, un.next(), 1)
            sw.eng = v
            sw.run(turn, first, lambda un: None)
            v.wait_ge(sent[0], 16 * NT)
            v.tensor_copy(tiles[:, :, D], val[:, 1, :]).then_inc(rt_v, 1)

        @block.tensor
        def _(pe):
            pe.wait_ge(rt_v, RV(0, "cnt"))
            pe.wait_ge(rt_a, RA(0, "ones"))
            pe.matmul(X[:, 0], tri[:], cnt[:], start=True, stop=True)
            pe.matmul(X[:, 1], onesb[:], cnt[:], start=True, stop=True).then_inc(rt_t, 1)
            pe.wait_ge(wts_v, 4)
            pe.wait_ge(rt_v, RV(0, "before"))

            def turn_in(un, t_):
                pe.wait_ge(rows_in[un.q], 16 * (un.pair + 1))
                sw.turn_in(pe, un, t_, rows[:, un.q])

            def first(un):
                for t_ in range(T2):
                    turn_in(un, t_)

            def turn(un, after, before_):
                sw.gate_up(pe, un, 0, wg, wu)
                if before_:
                    sw.down(pe, un.last(), wd)
                sw.gate_up(pe, un, 1, wg, wu)
                if after:
                    turn_in(un.next(), 0)
                sw.gate_up(pe, un, 2, wg, wu)
                if after:
                    turn_in(un.next(), 1)
            sw.eng = pe
            sw.run(turn, first, lambda un: sw.down(pe, un, wd))


def experts(nc, sb, sem, a, k, X, Y, dram):
    with ExitStack() as s:
        t = lambda n, shape, dt=F32: sb(n, shape, dt, s)
        NTE = CAP // P
        sw = Swiglu(nc, sb, sem, s, "expert", X, Y, k["ident"], NTE, [(0, CAP // 2), (CAP // 2, CAP // 2)], E1)
        raw = t("ew_raw", [P, 2, 2, T2, F1])
        rawd = t("ew_rawd", [P, 2, 3, D])
        wgu = [t(f"ew_{n}", [P, 2, 2, T2, F1], F32R) for n in ("h", "l")]
        wdn = [t(f"ew_d{n}", [P, 2, 3, D], F32R) for n in ("h", "l")]
        rows = t("ew_rows", [P, 2, NTE, ROW])
        wt = t("ew_weight", [P, 2, NTE])
        none = t("ew_none", [P, 2, NTE])
        idx = t("ew_idx", [P, 2, NTE], U32)
        weights_in = [sem(f"ew_weights{q}", s) for q in range(2)]
        rows_in = [sem(f"ew_rows{q}", s) for q in range(2)]
        added = [sem(f"ew_added{q}", s) for q in range(2)]
        x_in, seen = sem("x_back", s), sem("ew_seen", s)
        split_a, split_v, meta = sem("ew_split_act", s), sem("ew_split_vec", s), sem("ew_meta", s)
        SA, SV, ME = Steps("gu d01 d2"), Steps("gu d01 d2"), Steps("weight none idx")
        M2 = F1 - 2 * P
        block = s.enter_context(nc.Block())

        @block.sync
        def _(sp):
            e_of = lambda name, un: a[name][bass.ds(un.u, 1)].rearrange("o k n -> (o k) n")

            def load(un):
                q = un.q
                reach(sp, split_v, SV(un.u - 2, "d2"))
                sp.dma_start(raw[:, q, 0], e_of("L1_ffn_w_gate", un).rearrange("(t p) n -> p t n", p=P)).then_inc(weights_in[q], 16)
                sp.dma_start(raw[:, q, 1], e_of("L1_ffn_w_up", un).rearrange("(t p) n -> p t n", p=P)).then_inc(weights_in[q], 16)
                wd = e_of("L1_ffn_w_down", un)
                sp.dma_start(rawd[:, q, 0:2], wd[0:2 * P].rearrange("(t p) n -> p t n", p=P)).then_inc(weights_in[q], 16)
                sp.dma_start(rawd[0:M2, q, 2], wd[2 * P:F1]).then_inc(weights_in[q], 16)
                reach(sp, sw.pre_t, sw.PT(un.u - 2, "turn1"))
                reach(sp, meta, ME(un.u - 2, "idx"))
                sp.dma_start(rows[:, q], dram["rows"][bass.ds(un.u * CAP, CAP)].rearrange("(j p) r -> p j r", p=P)).then_inc(rows_in[q], 16)

            def turn(un, after, before):
                if after:
                    load(un.next())
            sw.eng = sp
            sw.run(turn, load, lambda un: None)
            sp.dma_start(k["x"][:, :, :, 0:D].rearrange("p b c d -> p (b c) d"),
                         dram["xres"].rearrange("(j p) d -> p j d", p=P)).then_inc(x_in, 16)
            sp.wait_ge(x_in, 16)

        @block.gpsimd
        def _(pool):
            def add(un):
                reach(pool, added[1 - un.q], 16 * NTE * (un.pair + un.q))
                pool.wait_ge(meta, ME(un.u, "idx"))
                for j in range(NTE):
                    apart(pool, sw.down_a, sw.DN(un.u, f"tile{j}"), seen)
                    pool.indirect_dma_start(dram["moe"], bass.IndirectOffsetOnAxis(idx[:, un.q, j:j + 1], 0), sw.out[:, un.q, j, :], None,
                                            compute_op=ALU.add,
                                            bounds_check=B * S - 1, oob_is_err=False).then_inc(added[un.q], 16)

            def turn(un, after, before):
                if before:
                    add(un.last())
            sw.eng = pool
            sw.run(turn, lambda un: None, add)
            for q in range(2):
                pool.wait_ge(added[q], 16 * NTE * E1 // 2)

        @block.scalar
        def _(act):
            def split(un):
                q = un.q
                act.wait_ge(weights_in[q], 64 * (un.pair + 1))
                reach(act, sw.down_t, sw.DN(un.u - 2, f"tile{NTE - 1}"))
                act.copy(wgu[0][:, q], raw[:, q]).then_inc(split_a, 1)
                act.copy(wdn[0][:, q, 0:2], rawd[:, q, 0:2]).then_inc(split_a, 1)
                act.copy(wdn[0][0:M2, q, 2], rawd[0:M2, q, 2]).then_inc(split_a, 1)

            def first(un):
                split(un)
                for t_ in range(T2):
                    sw.hin_hi(act, un, t_)

            def turn(un, after, before):
                sw.silu(act, un, 0)
                if before:
                    down(un.last())
                sw.silu(act, un, 1)
                if after:
                    split(un.next())
                    sw.hin_hi(act, un.next(), 0)
                sw.silu(act, un, 2)
                if after:
                    sw.hin_hi(act, un.next(), 1)

            def down(un):
                sw.take_down(act, un, wt[:, un.q], (added[un.q], 16 * NTE * un.pair))
            sw.eng = act
            sw.run(turn, first, down)

        @block.vector
        def _(v):
            def split(un):
                q = un.q
                for i, (hi, lo, r) in enumerate(((wgu[0][:, q], wgu[1][:, q], raw[:, q]), (wdn[0][:, q, 0:2], wdn[1][:, q, 0:2], rawd[:, q, 0:2]),
                                                 (wdn[0][0:M2, q, 2], wdn[1][0:M2, q, 2], rawd[0:M2, q, 2]))):
                    v.wait_ge(split_a, SA(un.u, ("gu", "d01", "d2")[i]))
                    v.tensor_tensor(lo, r, hi.bitcast(F32), ALU.subtract).then_inc(split_v, 1)

            def tokens(un):
                q = un.q
                v.wait_ge(rows_in[q], 16 * (un.pair + 1))
                reach(v, sw.down_a, sw.DN(un.u - 2, f"tile{NTE - 1}"))
                v.tensor_copy(wt[:, q], rows[:, q, :, D]).then_inc(meta, 1)
                v.tensor_scalar(none[:, q], rows[:, q, :, D + 1], 0.0, float(4 * SLOTS), ALU.is_equal, ALU.mult).then_inc(meta, 1)
                v.wait_ge(meta, ME(un.u, "none"))
                reach(v, added[q], 16 * NTE * un.pair)
                v.scalar_tensor_tensor(out=idx[:, q], in0=rows[:, q, :, D + 1], scalar=-1.0, in1=none[:, q], op0=ALU.add, op1=ALU.add).then_inc(meta, 1)

            def first(un):
                tokens(un)
                split(un)
                for t_ in range(T2):
                    sw.hin_lo(v, un, t_)

            def turn(un, after, before):
                sw.mul(v, un, 0)
                sw.mul(v, un, 1)
                if after:
                    split(un.next())
                    sw.hin_lo(v, un.next(), 0)
                sw.mul(v, un, 2)
                if after:
                    sw.hin_lo(v, un.next(), 1)
                    tokens(un.next())
            sw.eng = v
            sw.run(turn, first, lambda un: None)

        @block.tensor
        def _(pe):
            wd = lambda q: (wdn[0][:, q], wdn[1][:, q])
            wg = lambda q: (wgu[0][:, q, 0], wgu[1][:, q, 0])
            wu = lambda q: (wgu[0][:, q, 1], wgu[1][:, q, 1])

            def turn_in(un, t_):
                pe.wait_ge(rows_in[un.q], 16 * (un.pair + 1))
                sw.turn_in(pe, un, t_, rows[:, un.q])

            def first(un):
                for t_ in range(T2):
                    turn_in(un, t_)

            def turn(un, after, before):
                pe.wait_ge(split_v, SV(un.u, "d2"))
                sw.gate_up(pe, un, 0, wg(un.q), wu(un.q))
                if before:
                    sw.down(pe, un.last(), wd(1 - un.q))
                sw.gate_up(pe, un, 1, wg(un.q), wu(un.q))
                if after:
                    turn_in(un.next(), 0)
                sw.gate_up(pe, un, 2, wg(un.q), wu(un.q))
                if after:
                    turn_in(un.next(), 1)
            sw.eng = pe
            sw.run(turn, first, lambda un: sw.down(pe, un, wd(un.q)))


def final(nc, sb, sem, k, dram, out):
    with ExitStack() as s:
        G = 4
        x = k["x"]
        m = sb("fin_moe", [P, 2, G, D], F32, s)
        o = sb("fin_out", [P, 2, G, D], F32, s)
        loaded = [sem(f"fin_loaded{i}", s) for i in range(2)]
        stored = [sem(f"fin_stored{i}", s) for i in range(2)]
        vec = sem("fin_vec", s)
        block = s.enter_context(nc.Block())
        n = NT // G
        dst = out.rearrange("b (c p) d -> p b c d", p=P)

        @block.sync
        def _(sp):
            for i in range(n):
                if i >= 2:
                    sp.wait_ge(vec, 2 * (i - 2) + 1)
                sp.dma_start(m[:, i % 2], dram["moe"][i * G * P:(i + 1) * G * P].rearrange("(j p) d -> p j d", p=P)).then_inc(loaded[i % 2], 16)

        @block.scalar
        def _(act):
            for i in range(n):
                act.wait_ge(vec, 2 * i + 2)
                b, c = divmod(i * G, NC)
                act.dma_start(dst[:, b, c:c + G, :], o[:, i % 2]).then_inc(stored[i % 2], 16)
            for q in range(2):
                act.wait_ge(stored[q], 16 * (n // 2))

        @block.vector
        def _(v):
            for i in range(n):
                b, c = divmod(i * G, NC)
                v.wait_ge(loaded[i % 2], 16 * (i // 2 + 1))
                if i >= 2:
                    v.wait_ge(stored[i % 2], 16 * (i // 2))
                v.tensor_tensor(o[:, i % 2], m[:, i % 2], k["gbrow"][:, b:b + 1, :].to_broadcast([P, G, D]), ALU.mult).then_inc(vec, 1)
                v.wait_ge(vec, 2 * i + 1)
                v.tensor_tensor(o[:, i % 2], o[:, i % 2], x[:, b, c:c + G, 0:D], ALU.add).then_inc(vec, 1)


_INS = ["L0_attn_hidden_states", "L0_attn_w_q", "L0_attn_w_k", "L0_attn_w_v", "L0_attn_w_o", "L0_attn_gate",
        "L0_attn_memory", "L0_attn_memory_norm", "L0_ffn_gate_w", "L0_ffn_w1", "L0_ffn_b1", "L0_ffn_w2", "L0_ffn_b2",
        "L0_ffn_sw1", "L0_ffn_sb1", "L0_ffn_sw2", "L0_ffn_sb2", "L0_c", "L0_wmod", "L1_attn_W_qkv", "L1_attn_b_qkv",
        "L1_attn_W_out", "L1_attn_b_out", "L1_ffn_router_w", "L1_ffn_router_b", "L1_ffn_w_gate", "L1_ffn_w_up",
        "L1_ffn_w_down", "L1_ffn_sw_gate", "L1_ffn_sw_up", "L1_ffn_sw_down", "L1_c", "L1_wmod"]


def kernel(**inputs):
    import numpy as np
    import concourse.bacc as bacc
    from concourse.bass_utils import run_bass_kernel_spmd

    nc = bacc.Bacc("TRN2", target_bir_lowering=False, num_devices=1)
    arrays, aps = {}, {}
    for name in _INS:
        arr = np.ascontiguousarray(inputs[name])
        arrays[f"in_{name}"] = arr
        aps[name] = nc.dram_tensor(f"in_{name}", arr.shape, mybir.dt.from_np(arr.dtype), kind="ExternalInput").ap()
    out = nc.dram_tensor("out_0", (B, S, D), F32, kind="ExternalOutput").ap()
    build(nc, aps, out)
    r = run_bass_kernel_spmd(nc, [arrays], core_ids=[0])
    return r.results[0]["out_0"]
```

```python
from contextlib import ExitStack

import concourse.bass as bass
from concourse import mybir

F32 = mybir.dt.float32
F32R = mybir.dt.float32r
BF16 = mybir.dt.bfloat16
U32 = mybir.dt.uint32
ALU = mybir.AluOpType
ACT = mybir.ActivationFunctionType
AX = mybir.AxisListType

P = 128
B, S, D = 4, 1024, 256
T2 = D // P
NC = S // P
TOK = B * P
NT = B * NC
DM = 64
H0 = 1024
HT0 = H0 // P
NSTEP = 3 * HT0
HEADS, HD = 16, 16
WIN, STEP = 64, 32
WT = WIN + STEP
HC = 5
E1, F1 = 16, 352
CAP = 640
SLOTS = E1 * CAP
ROW = D + 2
LN_EPS = 1e-5
MEM_EPS = 1e-6
FT = [(0, 128), (128, 128), (256, F1 - 256)]


class Steps:

    def __init__(self, names):
        self.names = names if isinstance(names, list) else names.split()

    def __call__(self, c, name):
        return c * len(self.names) + self.names.index(name) + 1


def reach(eng, sem, count):
    if not isinstance(count, int) or count > 0:
        eng.wait_ge(sem, count)


def apart(eng, sem, count, seen):
    if isinstance(count, int):
        reach(eng, sem, count)
    else:
        eng.wait_ge(sem, count)
        eng.sem_inc(seen, 1)


def build(nc, a, out):
    ctx = ExitStack()
    with ctx:
        def sb(name, shape, dt=F32, c=None):
            return (c or ctx).enter_context(nc.sbuf_tensor(name, shape, dt))

        def sem(name, c=None):
            return (c or ctx).enter_context(nc.semaphore(name))

        X = ctx.enter_context(nc.psum_tensor("X", [P, 4, 512], F32))
        Y = ctx.enter_context(nc.psum_tensor("Y", [P, 4, 512], F32))
        dram = {
            "rows": nc.dram_tensor("expert_rows", [SLOTS, ROW], F32).ap(),
            "xres": nc.dram_tensor("x_residual", [B * S, D], F32).ap(),
        }

        dram["out"] = out.rearrange("b s d -> (b s) d")
        k = {}
        k["x"] = sb("x", [P, B, NC, ROW])
        k["ident"] = sb("ident", [P, P])
        k["mod"] = sb("mod", [P, 6, T2, B])
        k["mod1"] = sb("mod1", [P, 2, T2, B])
        k["gbb"] = sb("gbb", [P, T2, B])
        k["scb"] = sb("scb", [P, 2, B, T2])
        k["mhalf"] = sb("mhalf", [P, B])

        with ExitStack() as s:
            w = layer0_weights(nc, sb, s)
            setup(nc, sb, sem, a, k, w, X, Y, dram)
            layer0(nc, sb, sem, a, k, w, X, Y, dram)
        k["logits"] = sb("logits", [P, B, NC, E1])
        k["top"] = sb("top", [P, B, NC, 2])
        k["topi"] = sb("topi", [P, B, NC, 2])
        k["gbrow"] = sb("gbrow", [P, B, D])
        shared = {"raw": sb("sw_raw", [P, 2, T2, F1]), "rawd": sb("sw_rawd", [P, 3, D]), "loads": sem("sw_loads")}
        with ExitStack() as s:
            w = layer1_weights(nc, sb, s)
            layer1_attention(nc, sb, sem, a, k, w, X, Y, dram, shared)
        with ExitStack() as s:
            pre = expert_inputs(sb, sem, s)
            shared_and_routing(nc, sb, sem, a, k, X, Y, dram, shared, pre)
            experts(nc, sb, sem, a, k, X, Y, dram, pre)


def layer0_weights(nc, sb, s):
    w = {}
    for n, shape in (("w1h", [P, 3, T2, H0]), ("w1l", [P, 3, T2, H0]), ("w2h", [P, 3, HT0, D]), ("w2l", [P, 3, HT0, D])):
        w[n] = sb(n, shape, F32R, s)
    w["b1"] = sb("b1", [P, 3, HT0], F32, s)
    w["gwd"] = sb("gwd", [P, T2, P], F32, s)
    w["wqkT"] = sb("wqkT", [P, T2, P], F32, s)
    w["wvT"] = sb("wvT", [P, T2, DM], F32, s)
    w["wog"] = sb("wog", [DM, B, D], F32, s)
    w["maug"] = sb("maug", [DM, DM + 1], F32, s)
    w["coef"] = sb("coef", [P, 2, B], F32, s)
    w["causal"] = sb("causal", [P, P], F32, s)
    return w


def setup(nc, sb, sem, a, k, w, X, Y, dram):
    with ExitStack() as s:
        t = lambda n, shape, dt=F32: sb(n, shape, dt, s)
        ones = t("ones", [P, P])
        vrows = t("vrows", [VROWS, P])
        wm = t("wm", [P, T2, 6 * D])
        qk_raw, v_raw, o_raw, woT = t("qk_raw", [P, D]), t("v_raw", [DM, D]), t("o_raw", [P, T2, DM]), t("woT", [DM, D])
        gw, gwd1 = t("gw", [P, 2, T2]), t("gwd1", [P, T2])
        b2, b2s = t("b2", [P, 3, T2]), t("b2s", [P, T2])
        gcol, mn, gv = t("gcol", [P, 1]), t("mn", [P, DM]), t("gv", [P, 4])
        sign = t("sign", [P, B * D])
        garow = t("garow", [DM, B, D])

        x_in, small_in, wm_in = (sem(n, s) for n in ("x_in", "small_in", "wm_in"))
        pool_did, act_did, vec_did, pe_did = (sem(n, s) for n in ("setup_pool", "setup_act", "setup_vec", "setup_pe"))
        V = Steps(["ones", "gwdiff", "gwd", "b2a", "b2b", "scale1", "gbge", "gbsign", "gbabs", "gb", "gbb",
                   "nsum", "flag", "den", "g", "gflag", "omg", "coef",
                   "gage", "gasign", "gaabs", "ga", "wog"])
        A = Steps(["silu", "b1", "b2", "gw", "eg", "qkT", "vT", "woT", "mod"])
        G = Steps("mhalf ident0 ident causal0 causal")
        T = Steps("wT mod garow")
        block = s.enter_context(nc.Block())

        @block.sync
        def _(sp):
            sp.dma_start(wm[:], a["L0_wmod"].rearrange("(t p) n -> p t n", p=P)).then_inc(wm_in, 16)
            sp.dma_start(k["x"][:, :, 0, 0:D], x_of(a)[:, :, 0, :]).then_inc(x_in, 16)
            sp.wait_ge(x_in, 16)

        @block.gpsimd
        def _(pool):
            pool.memset(k["mhalf"][:], -0.5).then_inc(pool_did, 1)
            pool.memset(k["ident"][:], 0.0).then_inc(pool_did, 1)
            pool.wait_ge(pool_did, G(0, "ident0"))
            pool.affine_select(out=k["ident"][:], in_=k["ident"][:], compare_op=ALU.not_equal, fill=1.0,
                               base=0, pattern=[[-1, P]], channel_multiplier=1).then_inc(pool_did, 1)
            pool.memset(w["causal"][:], 1.0).then_inc(pool_did, 1)
            pool.wait_ge(pool_did, G(0, "causal0"))
            pool.affine_select(out=w["causal"][:], in_=w["causal"][:], compare_op=ALU.is_ge, fill=0.0,
                               base=0, pattern=[[1, P]], channel_multiplier=-1).then_inc(pool_did, 1)

        @block.scalar
        def _(act):
            n = 0
            for dst, src in (
                (qk_raw[0:DM, :], a["L0_attn_w_q"]), (qk_raw[DM:P, :], a["L0_attn_w_k"]), (v_raw[:], a["L0_attn_w_v"]),
                (o_raw[:], a["L0_attn_w_o"].rearrange("(t p) m -> p t m", p=P)),
                (w["maug"][:, 0:DM], a["L0_attn_memory"]),
                (w["maug"][:, DM:DM + 1], a["L0_attn_memory_norm"].rearrange("(p o) -> p o", o=1)),
                (mn[:], a["L0_attn_memory_norm"].partition_broadcast(P)),
                (gcol[:], a["L0_attn_gate"].partition_broadcast(P)),
                (vrows[0:8], a["L0_ffn_sb1"].rearrange("(h p) -> h p", p=P)),
                (vrows[8:24], a["L0_ffn_b1"].rearrange("e (h p) -> (e h) p", p=P)),
                (vrows[24:26], a["L0_ffn_sb2"].rearrange("(t p) -> t p", p=P)),
                (vrows[26:30], a["L0_ffn_b2"].rearrange("e (t p) -> (e t) p", p=P)),
                (vrows[30:38], a["L0_c"].rearrange("b (t p) -> (b t) p", p=P)),
                (vrows[38:46], a["L1_c"].rearrange("b (t p) -> (b t) p", p=P)),
                (vrows[46:50], a["L0_ffn_gate_w"].rearrange("e (t p) -> (e t) p", p=P)),
            ):
                act.dma_start(dst, src).then_inc(small_in, 16)
                n += 16
            assert n == SMALL_LOADS * 16
            act.wait_ge(pe_did, T(0, "wT"))
            nc.scalar.activation(k["scb"][:], X[:, 3, 30:46].rearrange("p (l b t) -> p l b t", l=2, b=B), ACT.Silu).then_inc(act_did, 1)
            nc.scalar.copy(w["b1"][:], X[:, 3, 0:24].rearrange("p (e h) -> p e h", e=3)).then_inc(act_did, 1)
            nc.scalar.copy(b2[:], X[:, 3, 24:30].rearrange("p (e t) -> p e t", e=3)).then_inc(act_did, 1)
            nc.scalar.copy(gw[:], X[:, 3, 46:50].rearrange("p (e t) -> p e t", e=2)).then_inc(act_did, 1)
            nc.scalar.activation(gv[:, 0:1], gcol[:], ACT.Exp, scale=-1.0).then_inc(act_did, 1)
            nc.scalar.copy(w["wqkT"][:], X[:, 0, 0:2 * P].rearrange("p (t n) -> p t n", t=T2)).then_inc(act_did, 1)
            nc.scalar.copy(w["wvT"][:], X[:, 1, 0:2 * DM].rearrange("p (t n) -> p t n", t=T2)).then_inc(act_did, 1)
            nc.scalar.copy(woT[:], X[0:DM, 2, 0:D]).then_inc(act_did, 1)
            act.wait_ge(pe_did, T(0, "mod"))
            nc.scalar.copy(k["mod"][:], X[:, 3, 64:112].rearrange("p (j t b) -> p j t b", j=6, t=T2)).then_inc(act_did, 1)

        @block.tensor
        def _(pe):
            pe.wait_ge(pool_did, G(0, "ident"))
            pe.wait_ge(small_in, 16 * SMALL_LOADS)
            pe.transpose(X[:, 3, 0:VROWS], vrows[:], k["ident"][0:VROWS, 0:VROWS])
            for t_ in range(T2):
                pe.transpose(X[:, 0, t_ * P:(t_ + 1) * P], qk_raw[:, t_ * P:(t_ + 1) * P], k["ident"][:])
                pe.transpose(X[:, 1, t_ * DM:(t_ + 1) * DM], v_raw[:, t_ * P:(t_ + 1) * P], k["ident"][0:DM, 0:DM])
                ins = pe.transpose(X[0:DM, 2, t_ * P:(t_ + 1) * P], o_raw[:, t_, :], k["ident"][:])
            ins.then_inc(pe_did, 1)
            pe.wait_ge(act_did, A(0, "gw"))
            pe.wait_ge(wm_in, 16)
            mod_columns(pe, X[:, 3, 64:112], wm, k["scb"][:, 0], range(12)).then_inc(pe_did, 1)
            mod_rows(pe, Y, wm, k["scb"][:, 0], 2, DM).then_inc(pe_did, 1)

        @block.vector
        def _(v):
            v.memset(ones[:], 1.0).then_inc(vec_did, 1)
            v.wait_ge(act_did, A(0, "gw"))
            v.tensor_tensor(gwd1[:], gw[:, 1, :], gw[:, 0, :], ALU.subtract).then_inc(vec_did, 1)
            v.wait_ge(vec_did, V(0, "gwdiff"))
            for t_ in range(T2):
                ins = v.tensor_scalar(w["gwd"][:, t_, :], ones[:], gwd1[:, t_:t_ + 1], None, ALU.mult)
            ins.then_inc(vec_did, 1)
            v.tensor_tensor(b2s[:], b2[:, 1], b2[:, 2], ALU.add).then_inc(vec_did, 1)
            v.wait_ge(vec_did, V(0, "b2a"))
            v.tensor_tensor(b2s[:], b2s[:], b2[:, 0], ALU.add).then_inc(vec_did, 1)
            v.wait_ge(act_did, A(0, "mod"))
            mod = k["mod"]
            v.tensor_scalar(mod[:, 1:5:3], mod[:, 1:5:3], 1.0, None, ALU.add).then_inc(vec_did, 1)
            gate(v, vec_did, V, ("gbge", "gbsign", "gbabs", "gb"), mod[:, 5].rearrange("p t b -> p (t b)"),
                 mod[:, 2].rearrange("p t b -> p (t b)"), sign[:, 0:8])
            v.wait_ge(vec_did, V(0, "gb"))
            v.tensor_tensor(k["gbb"][:], mod[:, 2], b2s[:].unsqueeze(2).to_broadcast([P, T2, B]), ALU.mult).then_inc(vec_did, 1)
            v.wait_ge(small_in, 16 * SMALL_LOADS)
            v.reduce_sum(gv[:, 1:2], mn[:], AX.X).then_inc(vec_did, 1)
            v.wait_ge(vec_did, V(0, "nsum"))
            v.tensor_scalar(gv[:, 1:2], gv[:, 1:2], MEM_EPS, None, ALU.is_ge).then_inc(vec_did, 1)
            v.wait_ge(act_did, A(0, "eg"))
            v.tensor_scalar(gv[:, 2:3], gv[:, 0:1], 1.0, None, ALU.add).then_inc(vec_did, 1)
            v.wait_ge(vec_did, V(0, "den"))
            v.reciprocal(gv[:, 2:3], gv[:, 2:3]).then_inc(vec_did, 1)
            v.wait_ge(vec_did, V(0, "g"))
            v.tensor_tensor(gv[:, 1:2], gv[:, 1:2], gv[:, 2:3], ALU.mult).then_inc(vec_did, 1)
            v.tensor_scalar(gv[:, 3:4], gv[:, 2:3], -1.0, 1.0, ALU.mult, ALU.add).then_inc(vec_did, 1)
            v.wait_ge(vec_did, V(0, "omg"))
            v.tensor_scalar(w["coef"][:, 0, :], ones[:, 0:B], gv[:, 1:2], None, ALU.mult)
            v.tensor_scalar(w["coef"][:, 1, :], ones[:, 0:B], gv[:, 3:4], None, ALU.mult).then_inc(vec_did, 1)
            v.wait_ge(pe_did, T(0, "garow"))
            gate(v, vec_did, V, ("gage", "gasign", "gaabs", "ga"), Y[0:DM, 0:2].rearrange("p a n -> p (a n)"),
                 garow[:].rearrange("p b d -> p (b d)"), sign[0:DM, :])
            v.wait_ge(vec_did, V(0, "ga"))
            v.wait_ge(act_did, A(0, "woT"))
            v.tensor_tensor(w["wog"][:], garow[:], woT[:].unsqueeze(1).to_broadcast([DM, B, D]), ALU.mult).then_inc(vec_did, 1)


SMALL_LOADS = 15
VROWS = 50


def x_of(a):
    return a["L0_attn_hidden_states"].rearrange("b (c p) d -> p b c d", p=P)


def mod_columns(pe, o, wm, scb, tiles):
    for i, jt in enumerate(tiles):
        for t_ in range(T2):
            ins = pe.matmul(o[:, i * B:(i + 1) * B], wm[:, t_, jt * P:(jt + 1) * P], scb[:, :, t_],
                            start=t_ == 0, stop=t_ == T2 - 1)
    return ins


def mod_rows(pe, Y, wm, scb, j, m):
    for b in range(B):
        for t_ in range(T2):
            ins = pe.matmul(Y[0:m, b // 2, (b % 2) * D:(b % 2 + 1) * D], scb[:, b, t_:t_ + 1].to_broadcast([P, m]),
                            wm[:, t_, j * D:(j + 1) * D], start=t_ == 0, stop=t_ == T2 - 1)
    return ins


def gate(v, done, V, steps, src, dst, sign):
    v.tensor_scalar(sign, src, 0.0, None, ALU.is_ge).then_inc(done, 1)
    v.wait_ge(done, V(0, steps[0]))
    v.tensor_scalar(sign, sign, 2.0, -1.0, ALU.mult, ALU.add).then_inc(done, 1)
    v.wait_ge(done, V(0, steps[1]))
    v.tensor_tensor(dst, src, sign, ALU.mult).then_inc(done, 1)
    v.wait_ge(done, V(0, steps[2]))
    v.scalar_tensor_tensor(out=dst, in0=dst, scalar=0.25, in1=sign, op0=ALU.max, op1=ALU.mult).then_inc(done, 1)


LN_VEC = "stats aggr eps sq sqv half rstd xn".split()
LN_POOL = ["pow"]


class Norm:

    def __init__(self, sb, sem, s, name):
        self.st = sb(f"{name}_stats", [P, B, 6], F32, s)
        self.mv = sb(f"{name}_meanvar", [P, B, 2], F32, s)
        self.ve = sb(f"{name}_vareps", [P, B], F32, s)
        self.y = sb(f"{name}_y", [P, B], F32, s)
        self.q = sb(f"{name}_q", [P, B], F32, s)
        self.seen = sem(f"{name}_seen", s)


def norm_stats(v, ln, done, V, c, x):
    apart(v, done, V(c - 1, "xn"), ln.seen)
    for b in range(B):
        ins = v.bn_stats(ln.st[:, b, :], x[:, b, c, 0:D])
    ins.then_inc(done, 1)
    apart(v, done, V(c, "stats"), ln.seen)
    for b in range(B):
        ins = v.bn_aggr(ln.mv[:, b, :], ln.st[:, b, :])
    ins.then_inc(done, 1)
    v.wait_ge(done, V(c, "aggr"))
    v.tensor_scalar(ln.ve[:], ln.mv[:, :, 1], LN_EPS, None, ALU.add).then_inc(done, 1)


def norm_vector(v, ln, done, V, c, x, xn, pool, pow_count, free, free_count):
    v.wait_ge(pool, pow_count)
    v.tensor_tensor(ln.q[:], ln.y[:], ln.y[:], ALU.mult).then_inc(done, 1)
    v.wait_ge(done, V(c, "sq"))
    v.tensor_tensor(ln.q[:], ln.q[:], ln.ve[:], ALU.mult).then_inc(done, 1)
    v.wait_ge(done, V(c, "sqv"))
    v.tensor_scalar(ln.q[:], ln.q[:], -0.5, 1.5, ALU.mult, ALU.add).then_inc(done, 1)
    v.wait_ge(done, V(c, "half"))
    v.tensor_tensor(ln.y[:], ln.y[:], ln.q[:], ALU.mult).then_inc(done, 1)
    v.wait_ge(done, V(c, "rstd"))
    reach(v, free, free_count)
    for b in range(B):
        ins = v.tensor_scalar(xn[:, b, :], x[:, b, c, 0:D], ln.mv[:, b, 0:1], ln.y[:, b:b + 1], ALU.subtract, ALU.mult)
    ins.then_inc(done, 1)


def norm_pool(pool, ln, done, mhalf, vec, vec_count):
    pool.wait_ge(vec, vec_count)
    pool.tensor_tensor(ln.y[:], ln.ve[:], mhalf[:], ALU.pow).then_inc(done, 1)


def transpose_chunk(pe, X, src, ident):
    for b in range(B):
        for t in range(T2):
            ins = pe.transpose(X[:, t, b * P:(b + 1) * P], src[:, b, t * P:(t + 1) * P], ident[:])
    return ins


def modulate(act, dst, X, mod, scale, shift):
    for b in range(B):
        for t in range(T2):
            ins = act.activation(dst[:, t, b * P:(b + 1) * P], X[:, t, b * P:(b + 1) * P], ACT.Identity,
                                 bias=mod[:, shift, t, b:b + 1], scale=mod[:, scale, t, b:b + 1])
    return ins


def product3(pe, out, wh, wl, xh, xl, start, stop):
    pe.matmul(out, wh, xh, start=start, stop=False)
    pe.matmul(out, wh, xl, start=False, stop=False)
    return pe.matmul(out, wl, xh, start=False, stop=stop)


def layer0(nc, sb, sem, a, k, w, X, Y, dram):
    with ExitStack() as s:
        t = lambda n, shape, dt=F32: sb(n, shape, dt, s)
        x, mod, ident = k["x"], k["mod"], k["ident"]
        lna, lnf = Norm(sb, sem, s, "lna"), Norm(sb, sem, s, "lnf")
        xn = t("xn", [P, B, D])
        hT = t("a_hT", [P, T2, TOK])
        ex, sg = t("a_exp", [DM, 2, TOK]), t("a_sigma", [DM, 2, TOK])
        vaug = t("a_v", [P, B, DM + 1])
        amask = t("a_scores", [P, B, P])
        ktok = t("a_ktok", [P, B, DM])
        state = t("a_state", [DM, B, DM + 1])
        rd = t("a_rden", [P, 2, B])
        memn, comb = t("a_mem", [P, B, DM]), t("a_comb", [P, B, DM])
        cT = t("a_combT", [DM, TOK])
        hF = t("f_h", [P, T2, TOK])
        hS = t("f_hS", [P, 2, T2, TOK], F32R)
        hE = t("f_hE", [P, 2, T2, TOK], F32R)
        masks = t("f_masks", [P, 2, TOK], BF16)
        hid = t("f_hid", [P, 2, TOK])
        hidh, hidl = t("f_hidh", [P, 3, TOK], F32R), t("f_hidl", [P, 3, TOK], F32R)
        y = t("f_y", [P, T2, TOK])

        av, ap, aa, at = (sem(n, s) for n in ("attn_vec", "attn_pool", "attn_act", "attn_pe"))
        iv, ip, ia, it = (sem(n, s) for n in ("input_vec", "input_pool", "input_act", "input_pe"))
        low, masked, fa, ups, downs = (sem(n, s) for n in ("ffn_low_parts", "ffn_masked_inputs", "ffn_act", "ffn_ups", "ffn_downs"))
        rv, ra, rt = (sem(n, s) for n in ("result_vec", "result_act", "result_pe"))
        AV = Steps(LN_VEC + "sigma masked ktok state den recip coef mem loc comb x".split())
        AP, IP = Steps(LN_POOL), Steps(LN_POOL)
        AA = Steps("h neg relu exp v combT")
        AT = Steps("xT qk v scores kT mem loc state combT out")
        IV, IA, IT = Steps(LN_VEC + "mask0 mask1 hi lo".split()), Steps("h"), Steps("xT gate")
        MK = Steps("e0h e0l e1h e1l")
        STEP = Steps([f"{i}" for i in range(NSTEP)])
        FA = Steps([n for i in range(NSTEP) for n in (f"relu{i}", f"hi{i}")])
        RES = Steps("done")
        init, seen = sem("layer0_init", s), sem("attn_seen_pe", s)
        whole = [sem(f"weights_in{i}", s) for i in range(3)]
        high, low_w, x_in, zero_out = (sem(n, s) for n in ("weights_high", "weights_low", "x_rest_in", "zero_out"))
        mod1_in, mod1_t, mod1_a = (sem(n, s) for n in ("mod1_in", "mod1_pe", "mod1_act"))
        zeros = t("zeros", [P, ROW // 2])
        block = s.enter_context(nc.Block())
        X2 = X[:, 0:2].rearrange("p a n -> p (a n)")

        parts = []
        for e in range(3):
            w1 = a["L0_ffn_sw1"] if e == 0 else a["L0_ffn_w1"][e - 1]
            w2 = a["L0_ffn_sw2"] if e == 0 else a["L0_ffn_w2"][e - 1]
            for t_ in range(T2):
                parts.append((w1[t_ * P:(t_ + 1) * P].rearrange("(t p) n -> p t n", p=P), w["w1h"][:, e, t_:t_ + 1], w["w1l"][:, e, t_:t_ + 1]))
            for g in range(T2):
                hs = slice(g * HT0 // 2, (g + 1) * HT0 // 2)
                parts.append((w2[g * H0 // 2:(g + 1) * H0 // 2].rearrange("(h p) n -> p h n", p=P), w["w2h"][:, e, hs], w["w2l"][:, e, hs]))
        NW = len(parts)
        raws = [(hF, hid, y)[i % 3][:].rearrange("p i n -> p (i n)").rearrange("p (t n) -> p t n", n=parts[i][0].shape[2]) for i in range(NW)]

        def step(c, i):
            return STEP(c, "0") + i

        def pipeline(eng, start, turn, end):
            start()
            turn(0, True, False)
            with eng.Fori(1, NC - 1) as c:
                turn(c, True, True)
            turn(NC - 1, False, True)
            end()

        @block.sync
        def _(sp):
            sp.dma_start(y[:], a["L1_wmod"].rearrange("(t p) n -> p t n", p=P)[:, :, 0:2 * D]).then_inc(mod1_in, 16)
            for i, (src, _, _) in enumerate(parts):
                if i == 2:
                    sp.wait_ge(mod1_t, 1)
                if i >= 3:
                    sp.wait_ge(low_w, i - 2)
                sp.dma_start(raws[i], src).then_inc(whole[i % 3], 16)
            for b in range(B):
                sp.dma_start(x[:, b, 1:NC, 0:D], x_of(a)[:, b, 1:NC, :]).then_inc(x_in, 16)
            sp.wait_ge(init, 3)
            sp.dma_start(dram["rows"].rearrange("(p q) (i r) -> p (q i) r", p=P, i=2),
                         zeros[:].unsqueeze(1).to_broadcast([P, 2 * SLOTS // P, ROW // 2])).then_inc(zero_out, 16)
            sp.wait_ge(zero_out, 16)

        @block.gpsimd
        def _(pool):
            def mask(c):
                pool.wait_ge(iv, IV(c, "lo"))
                reach(pool, ups, step(c, -HT0 - 1))
                for i in (0, 1):
                    pool.tensor_tensor(hE[:, i], hS[:, i].bitcast(F32), masks[:, 0:1].to_broadcast([P, T2, TOK]), ALU.mult).then_inc(masked, 1)

            def mask_rest(c):
                pool.wait_ge(ups, step(c, HT0 - 1))
                pool.wait_ge(masked, MK(c, "e0l"))
                for i in (0, 1):
                    pool.tensor_tensor(hS[:, i], hS[:, i].bitcast(F32), masks[:, 1:2].to_broadcast([P, T2, TOK]), ALU.mult).then_inc(masked, 1)

            def start():
                def split(i):
                    pool.wait_ge(high, i + 1)
                    pool.tensor_tensor(parts[i][2], raws[i], parts[i][1].bitcast(F32), ALU.subtract).then_inc(low_w, 1)
                norm_pool(pool, lna, ap, k["mhalf"], av, AV(0, "eps"))
                for i in range(NW):
                    if i == 10:
                        norm_pool(pool, lnf, ip, k["mhalf"], iv, IV(0, "eps"))
                    split(i)

            def turn(c, ahead, behind):
                mask(c)
                if ahead:
                    norm_pool(pool, lna, ap, k["mhalf"], av, AV(c + 1, "eps"))
                mask_rest(c)
                if ahead:
                    norm_pool(pool, lnf, ip, k["mhalf"], iv, IV(c + 1, "eps"))
            pipeline(pool, start, turn, lambda: None)

        @block.scalar
        def _(act):
            def attn_h(c):
                act.wait_ge(at, AT(c, "xT"))
                modulate(act, hT, X, mod, 1, 0).then_inc(aa, 1)

            def attn_sigma(c):
                act.wait_ge(at, AT(c, "qk"))
                qk = X[0:DM, 2:4]
                act.activation(ex[:], qk, ACT.Relu, scale=-1.0).then_inc(aa, 1)
                act.activation(sg[:], qk, ACT.Relu).then_inc(aa, 1)
                act.wait_ge(aa, AA(c, "neg"))
                act.activation(ex[:], ex[:], ACT.Exp, scale=-1.0).then_inc(aa, 1)
                act.wait_ge(at, AT(c, "v"))
                act.wait_ge(init, 3)
                act.copy(vaug[:, :, 0:DM], X[:, 0, 0:B * DM].rearrange("p (b d) -> p b d", b=B)).then_inc(aa, 1)

            def attn_comb(c):
                act.wait_ge(at, AT(c, "combT"))
                act.copy(cT[:], X[0:DM, 2]).then_inc(aa, 1)

            def inputs(c):
                act.wait_ge(it, IT(c, "xT"))
                modulate(act, hF, X, mod, 4, 3).then_inc(ia, 1)

            def hidden(c, i):
                e, h = divmod(i, HT0)
                act.wait_ge(ups, step(c, i))
                reach(act, low, step(c, i - 2))
                act.activation(hid[:, i % 2], Y[:, i % 2], ACT.Relu, bias=w["b1"][:, e, h:h + 1]).then_inc(fa, 1)
                reach(act, downs, step(c, i - 3))
                act.wait_ge(fa, FA(c, f"relu{i}"))
                act.copy(hidh[:, i % 3], hid[:, i % 2]).then_inc(fa, 1)

            def result(c):
                act.wait_ge(downs, step(c, NSTEP - 1))
                for b in range(B):
                    for t_ in range(T2):
                        ins = act.activation(y[:, t_, b * P:(b + 1) * P], Y[:, 2 + t_, b * P:(b + 1) * P], ACT.Identity,
                                             bias=k["gbb"][:, t_, b:b + 1], scale=mod[:, 2, t_, b:b + 1])
                ins.then_inc(ra, 1)

            def start():
                def split(i0, i1):
                    for i in range(i0, i1):
                        act.wait_ge(whole[i % 3], 16 * (i // 3 + 1))
                        act.copy(parts[i][1], raws[i]).then_inc(high, 1)
                act.wait_ge(mod1_t, 1)
                m4 = Y[:, 3, 0:4 * B].rearrange("p (j t b) -> p j t b", j=2, t=T2)
                act.copy(k["mod1"][:, 0], m4[:, 0]).then_inc(mod1_a, 1)
                act.add(k["mod1"][:, 1], m4[:, 1], 1.0).then_inc(mod1_a, 1)
                attn_h(0)
                split(0, 2)
                attn_sigma(0)
                split(2, 6)
                attn_comb(0)
                split(6, 10)
                act.wait_ge(low_w, 10)
                inputs(0)
                split(10, NW)

            def turn(c, ahead, behind):
                for i in range(NSTEP):
                    hidden(c, i)
                    if behind and i == 1:
                        result(c - 1)
                    if ahead and i == 4:
                        attn_h(c + 1)
                    if ahead and i == 6:
                        attn_sigma(c + 1)
                    if ahead and i == 14:
                        attn_comb(c + 1)
                    if ahead and i == 19:
                        inputs(c + 1)
            pipeline(act, start, turn, lambda: result(NC - 1))

        @block.vector
        def _(v):
            v.memset(state[:], 0.0).then_inc(init, 1)
            v.memset(vaug[:, :, DM:DM + 1], 1.0).then_inc(init, 1)
            v.memset(zeros[:], 0.0).then_inc(init, 1)
            mem = X[:, 3, 0:B * (DM + 1)].rearrange("p (b d) -> p b d", b=B)
            loc = X[:, 0, 0:B * (DM + 1)].rearrange("p (b d) -> p b d", b=B)

            def attn_stats(c):
                norm_stats(v, lna, av, AV, c, x)

            def attn_norm(c):
                norm_vector(v, lna, av, AV, c, x, xn, ap, AP(c, "pow"), it, IT(c - 1, "xT"))

            def attn_sigma(c):
                v.wait_ge(aa, AA(c, "exp"))
                v.tensor_tensor(sg[:], ex[:], sg[:], ALU.add).then_inc(av, 1)

            def attn_scores(c):
                v.wait_ge(at, AT(c, "scores"))
                v.tensor_tensor(amask[:], X[:, 1].rearrange("p (b q) -> p b q", b=B),
                                w["causal"][:].unsqueeze(1).to_broadcast([P, B, P]), ALU.mult).then_inc(av, 1)
                v.wait_ge(at, AT(c, "kT"))
                v.tensor_copy(ktok[:], X[:, 2, 0:B * DM].rearrange("p (b d) -> p b d", b=B)).then_inc(av, 1)

            def attn_weights(c):
                v.wait_ge(at, AT(c, "state"))
                v.wait_ge(init, 3)
                v.tensor_tensor(state[:], state[:], X[0:DM, 1, 0:B * (DM + 1)].rearrange("p (b d) -> p b d", b=B), ALU.add).then_inc(av, 1)
                v.tensor_scalar(rd[:, 0, :], mem[:, :, DM], MEM_EPS, None, ALU.max)
                v.tensor_scalar(rd[:, 1, :], loc[:, :, DM], MEM_EPS, None, ALU.max).then_inc(av, 1)
                v.wait_ge(av, AV(c, "den"))
                v.reciprocal(rd[:], rd[:]).then_inc(av, 1)
                v.wait_ge(av, AV(c, "recip"))
                v.tensor_tensor(rd[:], rd[:], w["coef"][:], ALU.mult).then_inc(av, 1)

            def attn_combine(c):
                v.wait_ge(av, AV(c, "coef"))
                v.tensor_tensor(memn[:], mem[:, :, 0:DM], rd[:, 0, :].unsqueeze(2).to_broadcast([P, B, DM]), ALU.mult).then_inc(av, 1)
                v.tensor_tensor(comb[:], loc[:, :, 0:DM], rd[:, 1, :].unsqueeze(2).to_broadcast([P, B, DM]), ALU.mult).then_inc(av, 1)
                v.wait_ge(av, AV(c, "loc"))
                v.tensor_tensor(comb[:], comb[:], memn[:], ALU.add).then_inc(av, 1)

            def attn_add(c):
                v.wait_ge(at, AT(c, "out"))
                v.tensor_tensor(x[:, :, c, 0:D], x[:, :, c, 0:D], X2.rearrange("p (b d) -> p b d", b=B), ALU.add).then_inc(av, 1)

            def input_stats(c):
                apart(v, av, AV(c, "x"), lnf.seen)
                norm_stats(v, lnf, iv, IV, c, x)

            def input_norm(c):
                norm_vector(v, lnf, iv, IV, c, x, xn, ip, IP(c, "pow"), at, AT(c, "xT"))

            def input_masks(c):
                v.wait_ge(it, IT(c, "gate"))
                reach(v, masked, MK(c - 1, "e1l"))
                v.tensor_scalar(masks[:, 0, :], X[:, 2], 0.0, None, ALU.is_le).then_inc(iv, 1)
                v.tensor_scalar(masks[:, 1, :], X[:, 2], 0.0, None, ALU.is_gt).then_inc(iv, 1)

            def inputs(c):
                v.wait_ge(ia, IA(c, "h"))
                if isinstance(c, int) and c == 0:
                    v.wait_ge(low_w, NW)
                reach(v, ups, step(c, -1))
                v.tensor_copy(hS[:, 0], hF[:]).then_inc(iv, 1)
                v.wait_ge(iv, IV(c, "hi"))
                v.tensor_tensor(hS[:, 1], hF[:], hS[:, 0].bitcast(F32), ALU.subtract).then_inc(iv, 1)

            def hidden(c, i):
                v.wait_ge(fa, FA(c, f"hi{i}"))
                v.tensor_tensor(hidl[:, i % 3], hid[:, i % 2], hidh[:, i % 3].bitcast(F32), ALU.subtract).then_inc(low, 1)

            def result(c):
                v.wait_ge(rt, RES(c, "done"))
                v.tensor_tensor(x[:, :, c, 0:D], x[:, :, c, 0:D], X2.rearrange("p (b d) -> p b d", b=B), ALU.add).then_inc(rv, 1)

            def start():
                for part in (attn_stats, attn_norm, attn_sigma, attn_scores, attn_weights, attn_combine, attn_add,
                             input_stats, input_norm, input_masks, inputs):
                    part(0)

            def turn(c, ahead, behind):
                for i in range(NSTEP):
                    if ahead and i == NSTEP - 1:
                        inputs(c + 1)
                    hidden(c, i)
                    if ahead and not behind and i == 1:
                        v.wait_ge(x_in, 16 * B)
                    if ahead and i == 1:
                        attn_stats(c + 1)
                    if ahead and i == 2:
                        attn_norm(c + 1)
                    if behind and i == 3:
                        result(c - 1)
                    if ahead and i == 7:
                        attn_sigma(c + 1)
                    if ahead and i == 9:
                        attn_scores(c + 1)
                    if ahead and i == 11:
                        attn_weights(c + 1)
                    if ahead and i == 12:
                        attn_combine(c + 1)
                    if ahead and i == 16:
                        attn_add(c + 1)
                        input_stats(c + 1)
                    if ahead and i == 17:
                        input_norm(c + 1)
                    if ahead and i == 21:
                        input_masks(c + 1)
            pipeline(v, start, turn, lambda: result(NC - 1))

        @block.tensor
        def _(pe):
            bs = [slice(b * P, (b + 1) * P) for b in range(B)]
            aug = [slice(b * (DM + 1), (b + 1) * (DM + 1)) for b in range(B)]
            dm = [slice(b * DM, (b + 1) * DM) for b in range(B)]

            def attn_in(c):
                pe.wait_ge(av, AV(c, "xn"))
                reach(pe, rv, RES(c - 2, "done"))
                transpose_chunk(pe, X, xn, ident).then_inc(at, 1)

            def attn_qkv(c):
                pe.wait_ge(aa, AA(c, "h"))
                for i in range(2):
                    for t_ in range(T2):
                        ins = pe.matmul(X[0:DM, 2 + i], w["wqkT"][:, t_, i * DM:(i + 1) * DM], hT[:, t_, :], start=t_ == 0, stop=t_ == T2 - 1)
                ins.then_inc(at, 1)
                for b in range(B):
                    for t_ in range(T2):
                        ins = pe.matmul(X[:, 0, dm[b]], hT[:, t_, bs[b]], w["wvT"][:, t_, :], start=t_ == 0, stop=t_ == T2 - 1)
                ins.then_inc(at, 1)

            def attn_scores(c):
                pe.wait_ge(av, AV(c, "sigma"))
                for b in range(B):
                    ins = pe.matmul(X[:, 1, bs[b]], sg[:, 1, bs[b]], sg[:, 0, bs[b]], start=True, stop=True)
                ins.then_inc(at, 1)
                for b in range(B):
                    ins = pe.transpose(X[:, 2, dm[b]], sg[:, 1, bs[b]], ident[0:DM, 0:DM])
                ins.then_inc(at, 1)
                for b in range(B):
                    ins = pe.matmul(X[:, 3, aug[b]], sg[:, 0, bs[b]], w["maug"][:], start=True, stop=True)
                ins.then_inc(at, 1)

            def attn_values(c):
                pe.wait_ge(aa, AA(c, "v"))
                pe.wait_ge(av, AV(c, "masked"))
                for b in range(B):
                    pe.matmul(X[:, 0, aug[b]], amask[:, b, :], vaug[:, b, :], start=True, stop=False)
                    ins = pe.matmul(X[:, 0, aug[b]], sg[:, 0, bs[b]], state[:, b, :], start=False, stop=True)
                ins.then_inc(at, 1)
                pe.wait_ge(av, AV(c, "ktok"))
                for b in range(B):
                    ins = pe.matmul(X[0:DM, 1, aug[b]], ktok[:, b, :], vaug[:, b, :], start=True, stop=True)
                ins.then_inc(at, 1)

            def attn_turn(c):
                apart(pe, av, AV(c, "comb"), seen)
                for b in range(B):
                    ins = pe.transpose(X[0:DM, 2, bs[b]], comb[:, b, :], ident[:])
                ins.then_inc(at, 1)

            def attn_out(c):
                pe.wait_ge(aa, AA(c, "combT"))
                for b in range(B):
                    ins = pe.matmul(X2[:, b * D:(b + 1) * D], cT[:, bs[b]], w["wog"][:, b, :], start=True, stop=True)
                ins.then_inc(at, 1)

            def inputs_in(c):
                pe.wait_ge(iv, IV(c, "xn"))
                pe.wait_ge(av, AV(c, "x"))
                transpose_chunk(pe, X, xn, ident).then_inc(it, 1)

            def gate(c):
                pe.wait_ge(ia, IA(c, "h"))
                for t_ in range(T2):
                    ins = pe.matmul(X[:, 2], w["gwd"][:, t_, :], hF[:, t_, :], start=t_ == 0, stop=t_ == T2 - 1)
                ins.then_inc(it, 1)

            def up(c, i):
                e, h = divmod(i, HT0)
                hin = hE if e == 1 else hS
                if h == 0:
                    if e == 0:
                        pe.wait_ge(iv, IV(c, "lo"))
                    else:
                        pe.wait_ge(masked, MK(c, f"e{e - 1}l"))
                if i >= 2:
                    pe.wait_ge(fa, FA(c, f"relu{i - 2}"))
                else:
                    reach(pe, fa, FA(c - 1, f"relu{NSTEP + i - 2}"))
                for t_ in range(T2):
                    cols = slice(h * P, (h + 1) * P)
                    ins = product3(pe, Y[:, i % 2], w["w1h"][:, e, t_, cols], w["w1l"][:, e, t_, cols],
                                   hin[:, 0, t_, :], hin[:, 1, t_, :], t_ == 0, t_ == T2 - 1)
                ins.then_inc(ups, 1)

            def down(c, i):
                e, h = divmod(i, HT0)
                pe.wait_ge(low, step(c, i))
                if i == 0:
                    reach(pe, ra, RES(c - 1, "done"))
                    if isinstance(c, int) and c == 0:
                        pe.wait_ge(mod1_a, 2)
                for t_ in range(T2):
                    cols = slice(t_ * P, (t_ + 1) * P)
                    ins = product3(pe, Y[:, 2 + t_], w["w2h"][:, e, h, cols], w["w2l"][:, e, h, cols],
                                   hidh[:, i % 3], hidl[:, i % 3], i == 0, i == NSTEP - 1)
                ins.then_inc(downs, 1)

            def result(c):
                pe.wait_ge(ra, RES(c, "done"))
                for b in range(B):
                    for t_ in range(T2):
                        ins = pe.transpose(X2[:, b * D + t_ * P:b * D + (t_ + 1) * P], y[:, t_, bs[b]], ident[:])
                ins.then_inc(rt, 1)

            def start():
                pe.wait_ge(mod1_in, 16)
                mod_columns(pe, Y[:, 3, 0:4 * B], y, k["scb"][:, 1], range(4)).then_inc(mod1_t, 1)
                for part in (attn_in, attn_qkv, attn_scores, attn_values, attn_turn, attn_out, inputs_in, gate):
                    part(0)

            def turn(c, ahead, behind):
                for i in range(NSTEP):
                    if behind and i == 0:
                        down(c - 1, NSTEP - 2)
                    up(c, i)
                    if behind and i == 1:
                        down(c - 1, NSTEP - 1)
                    if i >= 2:
                        down(c, i - 2)
                    if behind and i == 2:
                        result(c - 1)
                    if ahead and i == 4:
                        attn_in(c + 1)
                    if ahead and i == 6:
                        attn_qkv(c + 1)
                    if ahead and i == 9:
                        attn_scores(c + 1)
                    if ahead and i == 11:
                        attn_values(c + 1)
                    if ahead and i == 14:
                        attn_turn(c + 1)
                    if ahead and i == 16:
                        attn_out(c + 1)
                    if ahead and i == 19:
                        inputs_in(c + 1)
                    if ahead and i == 21:
                        gate(c + 1)

            def end():
                down(NC - 1, NSTEP - 2)
                down(NC - 1, NSTEP - 1)
                result(NC - 1)
            pipeline(pe, start, turn, end)


def layer1_weights(nc, sb, s):
    w = {}
    w["qkvh"], w["qkvl"] = sb("qkvh", [P, T2, 3 * D], F32R, s), sb("qkvl", [P, T2, 3 * D], F32R, s)
    w["bqk"] = sb("bqk", [P, 2 * D], F32, s)
    w["bv"] = sb("bv", [P, T2], F32, s)
    w["wog"] = sb("wog1", [P, B, T2, D], F32, s)
    w["bog"] = sb("bog1", [P, B, D], F32, s)
    w["cb"], w["sb"] = sb("cbrow", [P, B, D], F32, s), sb("sbrow", [P, B, D], F32, s)
    w["rw"], w["rb"] = sb("rw", [P, T2, E1], F32, s), sb("rb", [P, E1], F32, s)
    w["hm"] = sb("headmask", [P, 8], F32, s)
    w["par"] = sb("parity", [P, 2], F32, s)
    return w


def layer1_attention(nc, sb, sem, a, k, w, X, Y, dram, shared):
    with ExitStack() as s:
        t = lambda n, shape, dt=F32: sb(n, shape, dt, s)
        x, mod, ident, hm, par = k["x"], k["mod1"], k["ident"], w["hm"], w["par"]
        lna, lnf = Norm(sb, sem, s, "ln1a"), Norm(sb, sem, s, "ln1f")
        R = 4 * B
        xn, xnf = t("xn1", [P, B, D]), t("xnf", [P, B, D])
        hT = t("b_hT", [P, T2, B, HC * P])
        win = t("b_win", [P, 2, T2, B, P], F32R)
        qk = t("b_qk", [P, B, 2 * D])
        raw = t("b_raw", [P, R, 2 * HD])
        sc, ex = t("b_scores", [P, R, HD]), t("b_exp", [P, R, HD])
        mx, sm = t("b_max", [P, R]), t("b_sum", [P, R])
        pr, prT = t("b_pairs", [P, R, 2, HD]), t("b_pairsT", [P, R, 2, HD])
        attT = t("b_attT", [P, R, HD])
        abd = t("b_attdiag", [P, R, 8, HD])
        vT = t("b_vT", [P, T2, B, 2, WIN])
        zp, zT = t("b_zpairs", [P, R * WIN // HD, 2, HD]), t("b_zpairsT", [P, R * WIN // HD, 2, HD])
        z = t("b_z", [P, B, T2, P])
        h, xp = t("c_h", [P, B, D]), t("c_x", [P, B, D])
        hfT = t("c_hT", [P, T2, TOK])
        lg, top, topi = t("c_logits", [P, B, E1]), t("c_top", [P, B, 8]), t("c_topi", [P, B, 8], U32)

        sv, sp_, sa, st = (sem(n, s) for n in ("scores_vec", "scores_pool", "scores_act", "scores_pe"))
        pv, pa = sem("probs_vec", s), sem("probs_act", s)
        ov, oa, ot = (sem(n, s) for n in ("output_vec", "output_act", "output_pe"))
        nv, np_, na, nt = (sem(n, s) for n in ("norm_vec", "norm_pool", "norm_act", "norm_pe"))
        fv, fp, fa, ft = (sem(n, s) for n in ("route_vec", "route_pool", "route_act", "route_pe"))
        stored = sem("stream_stored", s)
        wm = t("wm1", [P, T2, 4 * D])
        qkv, wout, bout = t("qkv_raw", [P, T2, 3 * D]), t("wout_raw", [P, T2, D]), t("bout_raw", [P, D])
        sign, garow = t("sign1", [P, B * D]), t("garow1", [P, B, D])
        loads, loads2 = sem("loads1", s), sem("loads1_more", s)
        wa, wv, wt = (sem(n, s) for n in ("weights1_act", "weights1_vec", "weights1_pe"))
        WV = Steps("lo hm par0 par1 gage gasign gaabs ga wog bog gbge gbsign gbabs gb")
        WA, WT_ = Steps("hi sb cb"), Steps("ga gb sb cb")
        seen_v, seen_p = (sem(f"win_seen_{e}", s) for e in ("vec", "pool"))
        NV, NP, NA, NT_ = Steps(LN_VEC), Steps(LN_POOL), Steps("h"), Steps("xT")
        SV, SP = Steps("win0 win1 qk"), Steps("bias")
        SA, ST = Steps("win0 win1 pairs vT"), Steps("qk scores vT")
        PV, PA = Steps("even scores max sub sum recip prob pair0 pair1 pairsT attT"), Steps("exp diag")
        OV, OA, OT = Steps("zT z x"), Steps("zpairs"), Steps("z out")
        FV = Steps(LN_VEC + "scale h logits top topi kept".split())
        FP = Steps(LN_POOL + ["gate", "x"])
        FA, FT_ = Steps("hT keep"), Steps("hT logits")
        block = s.enter_context(nc.Block())
        Y2 = Y[:, 0:2].rearrange("p a n -> p (a n)")
        bd = lambda ap: ap.rearrange("p (b d) -> p b d", b=B)

        def norm_due(c):
            return isinstance(c, int) and c + 2 < HC

        def pipeline(eng, turn):
            turn(0, True, False, False, True)
            turn(1, True, True, False, True)
            turn(2, True, True, True, True)
            with eng.Fori(3, NC - 1) as c:
                turn(c, True, True, True, True)
            turn(NC - 1, True, True, True, False)
            turn(NC, False, True, True, False)
            turn(NC + 1, False, False, True, False)

        @block.sync
        def _(sp):
            first = (
                (qkv[:], a["L1_attn_W_qkv"].rearrange("(t p) n -> p t n", p=P)),
                (wm[:], a["L1_wmod"].rearrange("(t p) n -> p t n", p=P)[:, :, 2 * D:6 * D]),
            )
            then = (
                (w["bqk"][:], a["L1_attn_b_qkv"][0:2 * D].partition_broadcast(P)),
                (w["bv"][:, 0:1], a["L1_attn_b_qkv"][2 * D:2 * D + P].rearrange("(p o) -> p o", o=1)),
                (w["bv"][:, 1:2], a["L1_attn_b_qkv"][2 * D + P:3 * D].rearrange("(p o) -> p o", o=1)),
                (wout[:], a["L1_attn_W_out"].rearrange("(t p) n -> p t n", p=P)),
                (bout[:], a["L1_attn_b_out"].partition_broadcast(P)),
                (w["rw"][:], a["L1_ffn_router_w"].rearrange("(t p) n -> p t n", p=P)),
                (w["rb"][:], a["L1_ffn_router_b"].partition_broadcast(P)),
            )
            for dst, src in first:
                sp.dma_start(dst, src).then_inc(loads, 16)
            for dst, src in then:
                sp.dma_start(dst, src).then_inc(loads2, 16)

            sp.dma_start(shared["raw"][:, 0], a["L1_ffn_sw_gate"].rearrange("(t p) n -> p t n", p=P)).then_inc(shared["loads"], 16)
            sp.dma_start(shared["raw"][:, 1], a["L1_ffn_sw_up"].rearrange("(t p) n -> p t n", p=P)).then_inc(shared["loads"], 16)
            sp.dma_start(shared["rawd"][:, 0:2], a["L1_ffn_sw_down"][0:2 * P].rearrange("(t p) n -> p t n", p=P)).then_inc(shared["loads"], 16)
            sp.dma_start(shared["rawd"][0:F1 - 2 * P, 2], a["L1_ffn_sw_down"][2 * P:F1]).then_inc(shared["loads"], 16)

            def store(c):
                sp.wait_ge(fp, FP(c, "x"))
                sp.dma_start(dram["xres"].rearrange("(b c p) d -> p b c d", b=B, p=P)[:, :, c, :], xp[:]).then_inc(stored, 16)
            store(0)
            with sp.Fori(1, NC) as c:
                store(c)
            sp.wait_ge(stored, 16 * NC)

        @block.gpsimd
        def _(pool):
            def norm(c):
                norm_pool(pool, lna, np_, k["mhalf"], nv, NV(c, "eps"))
            norm(0)
            norm(1)

            def bias(c):
                pool.tensor_tensor(x[:, :, c, 0:D], x[:, :, c, 0:D], w["bog"][:], ALU.add).then_inc(sp_, 1)

            def route(c):
                norm_pool(pool, lnf, fp, k["mhalf"], fv, FV(c, "eps"))
                pool.wait_ge(fv, FV(c, "h"))
                reach(pool, stored, 16 * c)
                pool.tensor_tensor(xp[:], h[:], k["gbrow"][:], ALU.mult).then_inc(fp, 1)
                apart(pool, fp, FP(c, "gate"), seen_p)
                pool.tensor_tensor(xp[:], xp[:], x[:, :, c, 0:D], ALU.add).then_inc(fp, 1)

            def turn(c, a, b, d, more):
                if norm_due(c):
                    norm(c + 2)
                    if c == 0:
                        pool.wait_ge(wv, WV(0, "bog"))
                    pool.wait_ge(nv, NV(c + 2, "xn"))
                if a:
                    bias(c)
                if d:
                    route(c - 2)
            pipeline(pool, turn)

        @block.scalar
        def _(act):
            def norm(c):
                act.wait_ge(nt, NT_(c, "xT"))
                for b in range(B):
                    for t_ in range(T2):
                        ins = act.activation(hT[:, t_, b, bass.ds(c * P, P)], Y[:, t_, b * P:(b + 1) * P], ACT.Identity,
                                             bias=mod[:, 0, t_, b:b + 1], scale=mod[:, 1, t_, b:b + 1])
                ins.then_inc(na, 1)
            norm(0)
            act.wait_ge(loads, 32)
            act.copy(w["qkvh"][:], qkv[:]).then_inc(wa, 1)
            norm(1)
            act.wait_ge(na, NA(1, "h"))

            def window(c):
                reach(act, st, ST(c - 1, "vT"))
                for i, first in ((0, STEP), (1, 0)):
                    act.copy(win[:, 0, :, :, i * WIN:(i + 1) * WIN].rearrange("p t b n -> p (t b) n"),
                             hT[:].rearrange("p t b n -> p (t b) n")[:, :, bass.ds(c * WIN + first, WIN)]).then_inc(sa, 1)

            def pairs(c):
                act.wait_ge(st, ST(c, "scores"))
                reach(act, pv, PV(c - 1, "scores"))
                for q in range(4):
                    part = slice(32 * q, 32 * q + 32)
                    ins = act.copy(raw[part], X[part].rearrange("p b (r n) -> p (b r) n", n=P)[:, :, part])
                ins.then_inc(sa, 1)

            def values(c):
                act.wait_ge(st, ST(c, "vT"))
                reach(act, ot, OT(c - 1, "z"))
                for g in range(T2):
                    ins = act.activation(vT[:, g].rearrange("p b i n -> p (b i n)"), X[:, g], ACT.Identity, bias=w["bv"][:, g:g + 1])
                ins.then_inc(sa, 1)

            def exp(c):
                act.wait_ge(pv, PV(c, "sub"))
                act.activation(ex[:], sc[:], ACT.Exp, scale=HD ** -0.5).then_inc(pa, 1)

            def diagonal(c):
                act.wait_ge(pv, PV(c, "attT"))
                reach(act, ot, OT(c - 1, "z"))
                for h in range(8):
                    ins = act.mul(abd[:, :, h, :], attT[:], hm[:, h:h + 1])
                ins.then_inc(pa, 1)

            def split(c):
                act.wait_ge(ot, OT(c, "z"))
                reach(act, ov, OV(c - 1, "zT"))
                for i in range(2):
                    ins = act.mul(zp[:, :, i, :], Y[:, 2:4].rearrange("p a (r d) -> p (a r) d", d=HD), par[:, i:i + 1])
                ins.then_inc(oa, 1)

            def keep(c):
                act.wait_ge(fp, FP(c, "x"))
                act.copy(x[:, :, c, 0:D], h[:]).then_inc(fa, 1)

            def routed(c):
                act.wait_ge(ft, FT_(c, "hT"))
                act.copy(hfT[:].rearrange("p t n -> p (t n)"), Y[:, 2:4].rearrange("p a n -> p (a n)")).then_inc(fa, 1)

            window(0)
            act.wait_ge(loads2, 16 * 7)

            def turn(c, a, b, d, more):
                if norm_due(c):
                    norm(c + 2)
                if b:
                    split(c - 1)
                if a:
                    pairs(c)
                if d:
                    routed(c - 2)
                if isinstance(c, int) and c == 0:
                    act.wait_ge(wt, WT_(0, "sb"))
                    act.copy(w["sb"][:].rearrange("p b d -> p (b d)"), Y[:, 2:4].rearrange("p a n -> p (a n)")).then_inc(wa, 1)
                if a:
                    exp(c)
                if norm_due(c):
                    act.wait_ge(na, NA(c + 2, "h"))
                if more:
                    window(c + 1)
                if a:
                    values(c)
                    diagonal(c)
                if d:
                    keep(c - 2)
                if isinstance(c, int) and c == 0:
                    act.wait_ge(wt, WT_(0, "cb"))
                    act.add(w["cb"][:].rearrange("p b d -> p (b d)"), Y[:, 2:4].rearrange("p a n -> p (a n)"), 1.0).then_inc(wa, 1)
            pipeline(act, turn)

        @block.vector
        def _(v):
            def norm(c):
                norm_stats(v, lna, nv, NV, c, x)
                norm_vector(v, lna, nv, NV, c, x, xn, np_, NP(c, "pow"), nt, NT_(c - 1, "xT"))
            norm(0)
            norm(1)
            v.wait_ge(wa, WA(0, "hi"))
            v.tensor_tensor(w["qkvl"][:], qkv[:], w["qkvh"][:].bitcast(F32), ALU.subtract).then_inc(wv, 1)
            v.wait_ge(na, NA(1, "h"))

            def window(c):
                for i, first in ((0, STEP), (1, 0)):
                    v.wait_ge(sa, SA(c, f"win{i}"))
                    cols = slice(i * WIN, (i + 1) * WIN)
                    hi, lo = (win[:, j, :, :, cols].rearrange("p t b n -> p (t b) n") for j in range(2))
                    v.tensor_tensor(lo, hT[:].rearrange("p t b n -> p (t b) n")[:, :, bass.ds(c * WIN + first, WIN)],
                                    hi.bitcast(F32), ALU.subtract).then_inc(sv, 1)

            def projections(c):
                v.wait_ge(st, ST(c, "qk"))
                v.tensor_tensor(qk[:], X[:], w["bqk"][:].unsqueeze(1).to_broadcast([P, B, 2 * D]), ALU.add).then_inc(sv, 1)

            def less_max(c):
                v.wait_ge(sa, SA(c, "pairs"))
                v.tensor_scalar(sc[:], raw[:, :, 0:HD], par[:, 0:1], None, ALU.mult).then_inc(pv, 1)
                v.wait_ge(pv, PV(c, "even"))
                v.scalar_tensor_tensor(out=sc[:], in0=raw[:, :, HD:2 * HD], scalar=par[:, 1:2], in1=sc[:], op0=ALU.mult, op1=ALU.add).then_inc(pv, 1)
                v.wait_ge(pv, PV(c, "scores"))
                v.reduce_max(mx[:], sc[:], AX.X).then_inc(pv, 1)
                v.wait_ge(pv, PV(c, "max"))
                v.tensor_tensor(sc[:], sc[:], mx[:].unsqueeze(2).to_broadcast([P, R, HD]), ALU.subtract).then_inc(pv, 1)

            def softmax(c):
                v.wait_ge(pa, PA(c, "exp"))
                v.reduce_sum(sm[:], ex[:], AX.X).then_inc(pv, 1)
                v.wait_ge(pv, PV(c, "sum"))
                v.reciprocal(sm[:], sm[:]).then_inc(pv, 1)
                v.wait_ge(pv, PV(c, "recip"))
                v.tensor_tensor(ex[:], ex[:], sm[:].unsqueeze(2).to_broadcast([P, R, HD]), ALU.mult).then_inc(pv, 1)
                v.wait_ge(pv, PV(c, "prob"))
                for i in range(2):
                    v.tensor_scalar(pr[:, :, i, :], ex[:], par[:, i:i + 1], None, ALU.mult).then_inc(pv, 1)
                v.wait_ge(pv, PV(c, "pair1"))
                v.transpose(prT[:].rearrange("p r i d -> p (r i d)"), pr[:].rearrange("p r i d -> p (r i d)")).then_inc(pv, 1)
                v.wait_ge(pv, PV(c, "pairsT"))
                reach(v, pa, PA(c - 1, "diag"))
                v.tensor_tensor(attT[:], prT[:, :, 0, :], prT[:, :, 1, :], ALU.add).then_inc(pv, 1)

            def turned(c):
                v.wait_ge(oa, OA(c, "zpairs"))
                v.transpose(zT[:].rearrange("p r i d -> p (r i d)"), zp[:].rearrange("p r i d -> p (r i d)")).then_inc(ov, 1)
                v.wait_ge(ov, OV(c, "zT"))
                reach(v, ot, OT(c - 1, "out"))
                four = lambda i: zT[:, :, i, :].rearrange("p (r q) d -> p r q d", q=WIN // HD)
                v.tensor_tensor(z[:].rearrange("p b g (w d q) -> p (b g w) q d", w=2, d=HD), four(0), four(1), ALU.add).then_inc(ov, 1)

            def add(c):
                v.wait_ge(ot, OT(c, "out"))
                apart(v, sp_, SP(c, "bias"), seen_v)
                v.tensor_tensor(x[:, :, c, 0:D], x[:, :, c, 0:D], bd(Y2), ALU.add).then_inc(ov, 1)

            def stats(c):
                apart(v, ov, OV(c, "x"), lnf.seen)
                norm_stats(v, lnf, fv, FV, c, x)

            def normed(c):
                norm_vector(v, lnf, fv, FV, c, x, xnf, fp, FP(c, "pow"), fv, FV(c - 1, "scale"))

            def modulated(c):
                v.wait_ge(fv, FV(c, "xn"))
                reach(v, fa, FA(c - 1, "keep"))
                v.tensor_tensor(h[:], xnf[:], w["cb"][:], ALU.mult).then_inc(fv, 1)
                v.wait_ge(fv, FV(c, "scale"))
                v.tensor_tensor(h[:], h[:], w["sb"][:], ALU.add).then_inc(fv, 1)

            def logits(c):
                v.wait_ge(ft, FT_(c, "logits"))
                reach(v, fv, FV(c - 1, "kept"))
                v.tensor_tensor(lg[:], Y[:, 2, 0:B * E1].rearrange("p (b e) -> p b e", b=B),
                                w["rb"][:].unsqueeze(1).to_broadcast([P, B, E1]), ALU.add).then_inc(fv, 1)

            def largest(c):
                apart(v, fv, FV(c, "logits"), seen_v)
                for b in range(B):
                    ins = v.max(top[:, b, :], lg[:, b, :])
                ins.then_inc(fv, 1)
                apart(v, fv, FV(c, "top"), seen_v)
                for b in range(B):
                    ins = v.max_index(topi[:, b, :], top[:, b, :], lg[:, b, :])
                ins.then_inc(fv, 1)
                v.tensor_copy(k["logits"][:, :, c, :], lg[:])
                v.tensor_copy(k["top"][:, :, c, :], top[:, :, 0:2])
                v.wait_ge(fv, FV(c, "topi"))
                v.tensor_copy(k["topi"][:, :, c, :], topi[:, :, 0:2]).then_inc(fv, 1)

            window(0)
            v.reduce_sum(hm[:], ident[:].rearrange("p (h d) -> p h d", d=HD), AX.X).then_inc(wv, 1)
            pairs = hm[:].rearrange("p (q r) -> p r q", r=2)
            v.wait_ge(wv, WV(0, "hm"))
            for i in range(2):
                v.reduce_sum(par[:, i:i + 1], pairs[:, i], AX.X).then_inc(wv, 1)
            v.wait_ge(wt, WT_(0, "ga"))
            flat = lambda ap: ap.rearrange("p b d -> p (b d)")
            gate(v, wv, WV, ("gage", "gasign", "gaabs", "ga"), Y[:, 2:4].rearrange("p a n -> p (a n)"), flat(garow[:]), sign[:])
            v.wait_ge(wv, WV(0, "ga"))
            v.wait_ge(loads2, 16 * 7)
            for g in range(T2):
                ins = v.tensor_tensor(w["wog"][:, :, g, :], garow[:], wout[:, g:g + 1, :].to_broadcast([P, B, D]), ALU.mult)
            ins.then_inc(wv, 1)
            v.tensor_tensor(w["bog"][:], garow[:], bout[:].unsqueeze(1).to_broadcast([P, B, D]), ALU.mult).then_inc(wv, 1)

            def turn(c, a, b, d, more):
                first = isinstance(c, int) and c == 0
                if first:
                    projections(c)
                if norm_due(c):
                    norm(c + 2)
                if d:
                    stats(c - 2)
                    normed(c - 2)
                if a and not first:
                    projections(c)
                if d:
                    modulated(c - 2)
                if b:
                    turned(c - 1)
                if isinstance(c, int) and c == 0:
                    v.wait_ge(wt, WT_(0, "gb"))
                    gate(v, wv, WV, ("gbge", "gbsign", "gbabs", "gb"), Y[:, 2:4].rearrange("p a n -> p (a n)"), flat(k["gbrow"][:]), sign[:])
                if a:
                    less_max(c)
                    softmax(c)
                if norm_due(c):
                    v.wait_ge(na, NA(c + 2, "h"))
                if more:
                    window(c + 1)
                if b:
                    add(c - 1)
                if d:
                    logits(c - 2)
                    largest(c - 2)
                if isinstance(c, int) and c == 0:
                    v.wait_ge(wa, WA(0, "cb"))
            pipeline(v, turn)

        @block.tensor
        def _(pe):
            bs = [slice(b * P, (b + 1) * P) for b in range(B)]

            def norm(c):
                pe.wait_ge(nv, NV(c, "xn"))
                reach(pe, na, NA(c - 1, "h"))
                transpose_chunk(pe, Y, xn, ident).then_inc(nt, 1)
            scb = k["scb"][:, 1]

            def rows(name, j):
                before_ = {"ga": None, "gb": (wv, WV(0, "gaabs")), "sb": (wv, WV(0, "gbabs")), "cb": (wa, WA(0, "sb"))}[name]
                if before_:
                    pe.wait_ge(*before_)
                mod_rows(pe, Y[:, 2:4], wm, scb, j, P).then_inc(wt, 1)
            norm(0)
            norm(1)
            pe.wait_ge(loads, 32)
            rows("ga", 0)

            def projections(c):
                pe.wait_ge(sv, SV(c, "win1"))
                reach(pe, sa, SA(c - 1, "vT"))
                for b in range(B):
                    for t_ in range(T2):
                        ins = product3(pe, X[:, b], win[:, 0, t_, b, :], win[:, 1, t_, b, :],
                                       w["qkvh"][:, t_, 0:2 * D], w["qkvl"][:, t_, 0:2 * D], t_ == 0, t_ == T2 - 1)
                ins.then_inc(st, 1)

            def scores(c):
                pe.wait_ge(sv, SV(c, "qk"))
                for b in range(B):
                    for wi in range(2):
                        part = slice(WIN * (1 - wi), WIN * (2 - wi))
                        for g in range(T2):
                            r = 2 * (b % 2) + g
                            ins = pe.matmul(X[:, 2 * wi + b // 2, r * P:(r + 1) * P], qk[part, b, g * P:(g + 1) * P],
                                            qk[part, b, D + g * P:D + (g + 1) * P], start=True, stop=True)
                ins.then_inc(st, 1)

            def values(c):
                pe.wait_ge(sa, SA(c, "pairs"))
                for g in range(T2):
                    for t_ in range(T2):
                        cols = slice(2 * D + g * P, 2 * D + (g + 1) * P)
                        ins = product3(pe, X[:, g], w["qkvh"][:, t_, cols], w["qkvl"][:, t_, cols],
                                       win[:, 0, t_], win[:, 1, t_], t_ == 0, t_ == T2 - 1)
                ins.then_inc(st, 1)

            def weigh(c):
                pe.wait_ge(pa, PA(c, "diag"))
                if isinstance(c, int) and c == 0:
                    pe.wait_ge(wa, WA(0, "cb"))
                reach(pe, fv, FV(c - 2, "logits"))
                pe.wait_ge(sa, SA(c, "vT"))
                Y23 = Y[:, 2:4].rearrange("p a n -> p (a n)")
                for b in range(B):
                    for g in range(T2):
                        for wi in range(2):
                            n = ((b * T2 + g) * 2 + wi) * WIN
                            r = 2 * (B * wi + b) + g
                            ins = pe.matmul(Y23[:, n:n + WIN], abd[:, r].rearrange("p h d -> p (h d)"), vT[:, g, b, 1 - wi, :],
                                            start=True, stop=True)
                ins.then_inc(ot, 1)

            def out(c):
                pe.wait_ge(ov, OV(c, "z"))
                if norm_due(c + 1):
                    pe.wait_ge(na, NA(c + 3, "h"))
                reach(pe, ov, OV(c - 1, "x"))
                for b in range(B):
                    for g in range(T2):
                        ins = pe.matmul(Y2[:, b * D:(b + 1) * D], z[:, b, g, :], w["wog"][:, b, g, :], start=g == 0, stop=g == T2 - 1)
                ins.then_inc(ot, 1)

            def turn_in(c, after):
                if after:
                    pe.wait_ge(oa, OA(c + 1, "zpairs"))
                pe.wait_ge(fv, FV(c, "h"))
                transpose_chunk(pe, Y[:, 2:4], h, ident).then_inc(ft, 1)

            def logits(c):
                pe.wait_ge(fa, FA(c, "hT"))
                for b in range(B):
                    for t_ in range(T2):
                        ins = pe.matmul(Y[:, 2, b * E1:(b + 1) * E1], hfT[:, t_, bs[b]], w["rw"][:, t_, :], start=t_ == 0, stop=t_ == T2 - 1)
                ins.then_inc(ft, 1)

            def turn(c, a, b, d, more):
                if a:
                    projections(c)
                if norm_due(c):
                    if c == 2:
                        pe.wait_ge(ov, OV(0, "x"))
                    norm(c + 2)
                first = isinstance(c, int) and c == 0
                if first:
                    rows("gb", 3)
                if b:
                    weigh(c - 1)
                if a:
                    scores(c)
                if first:
                    rows("sb", 1)
                if d:
                    turn_in(c - 2, b)
                if a:
                    values(c)
                if first:
                    rows("cb", 2)
                if b:
                    out(c - 1)
                if d:
                    logits(c - 2)
            pipeline(pe, turn)


class Unit:

    def __init__(self, pair, q):
        self.pair, self.q = pair, q
        self.u = 2 * pair + q

    def next(self):
        return Unit(self.pair + self.q, 1 - self.q)

    def last(self):
        return Unit(self.pair - 1 + self.q, 1 - self.q)


class Swiglu:

    PRE_A, PRE_V, PRE_T = ["hin0", "hin1"], ["hin0", "hin1"], ["turn0", "turn1"]
    MAIN_A = [f"{n}{f}" for f in range(3) for n in ("silu", "hi")]
    MAIN_V = [f"{n}{f}" for f in range(3) for n in ("mul", "lo")]
    MAIN_T = [f"{n}{f}" for f in range(3) for n in ("gate", "up")]

    def __init__(self, nc, sb, sem, s, name, X, Y, ident, tiles, halves, units, out=None):
        self.X, self.Y, self.ident, self.tiles, self.halves, self.units = X, Y, ident, tiles, halves, units
        n = tiles * P
        t = lambda m, shape, dt=F32: sb(f"{name}_{m}", shape, dt, s)
        self.hin = t("hin", [P, 2, 2, T2, n], F32R)
        self.sil, self.act = t("silu", [P, 3, n]), t("act", [P, 3, n])
        self.acth, self.actl = t("acth", [P, 2, 3, n], F32R), t("actl", [P, 2, 3, n], F32R)
        self.out = t("out", [P, 2, tiles, D]) if out is None else out
        self.pre_a, self.pre_v, self.pre_t = (sem(f"{name}_next_{e}", s) for e in ("act", "vec", "pe"))
        self.main_a, self.main_v, self.main_t = (sem(f"{name}_{e}", s) for e in ("act", "vec", "pe"))
        self.down_a, self.down_t = (sem(f"{name}_down_{e}", s) for e in ("act", "pe"))
        self.PA, self.PV, self.PT = Steps(self.PRE_A), Steps(self.PRE_V), Steps(self.PRE_T)
        self.MA, self.MV, self.MT = Steps(self.MAIN_A), Steps(self.MAIN_V), Steps(self.MAIN_T)
        self.DN = Steps([f"tile{j}" for j in range(tiles)])

    def run(self, turn, first, end):
        first(Unit(0, 0))
        turn(Unit(0, 0), True, False)
        turn(Unit(0, 1), True, True)
        with self.eng.Fori(1, self.units // 2 - 1) as i:
            turn(Unit(i, 0), True, True)
            turn(Unit(i, 1), True, True)
        turn(Unit(self.units // 2 - 1, 0), True, True)
        turn(Unit(self.units // 2 - 1, 1), False, True)
        end(Unit(self.units // 2 - 1, 1))

    def turn_in(self, pe, un, t, rows):
        if t == 0:
            reach(pe, self.pre_v, self.PV(un.u - 1, "hin1"))
        else:
            pe.wait_ge(self.pre_v, self.PV(un.u, "hin0"))
        Y2 = self.Y[:, 0:2].rearrange("p a n -> p (a n)")
        for j in range(self.tiles):
            ins = pe.transpose(Y2[:, j * P:(j + 1) * P], rows[:, j, t * P:(t + 1) * P], self.ident[:])
        ins.then_inc(self.pre_t, 1)

    def gate_up(self, pe, un, f, wg, wu):
        f0, m = FT[f]
        if f == 0:
            pe.wait_ge(self.pre_v, self.PV(un.u, "hin1"))
        for base, wt, name in ((0, wg, "gate"), (2, wu, "up")):
            if name == "gate":
                if f:
                    pe.wait_ge(self.main_a, self.MA(un.u, f"silu{f - 1}"))
                else:
                    reach(pe, self.main_a, self.MA(un.u - 1, "silu2"))
            elif f:
                pe.wait_ge(self.main_v, self.MV(un.u, f"mul{f - 1}"))
            else:
                reach(pe, self.main_v, self.MV(un.u - 1, "mul2"))
            for hf, (n0, n) in enumerate(self.halves):
                for t in range(T2):
                    ins = product3(pe, self.X[0:m, base + hf, 0:n], wt[0][:, t, f0:f0 + m], wt[1][:, t, f0:f0 + m],
                                   self.hin[:, un.q, 0, t, n0:n0 + n], self.hin[:, un.q, 1, t, n0:n0 + n], t == 0, t == T2 - 1)
            ins.then_inc(self.main_t, 1)

    def down(self, pe, un, wd):
        pe.wait_ge(self.main_v, self.MV(un.u, "lo2"))
        for j in range(self.tiles):
            if j >= 2:
                pe.wait_ge(self.down_a, self.DN(un.u, f"tile{j - 2}"))
            else:
                reach(pe, self.down_a, self.DN(un.u - 1, f"tile{self.tiles - 2 + (j + self.tiles) % 2}"))
            for f, (_, m) in enumerate(FT):
                rows = slice(j * P, (j + 1) * P)
                ins = product3(pe, self.Y[:, 2 + j % 2, 0:D], self.acth[0:m, un.q, f, rows], self.actl[0:m, un.q, f, rows],
                               wd[0][0:m, f, :], wd[1][0:m, f, :], f == 0, f == 2)
            ins.then_inc(self.down_t, 1)

    def hin_hi(self, act, un, t):
        act.wait_ge(self.pre_t, self.PT(un.u, f"turn{t}"))
        reach(act, self.main_t, self.MT(un.u - 2, "up2"))
        n = self.tiles * P
        act.copy(self.hin[:, un.q, 0, t, :], self.Y[:, 0:2].rearrange("p a n -> p (a n)")[:, 0:n]).then_inc(self.pre_a, 1)

    def psum(self, base, m):
        nh, n = len(self.halves), self.halves[0][1]
        return self.X[0:m, base:base + nh, 0:n]

    def split(self, ap):
        return ap.rearrange("p (h n) -> p h n", h=len(self.halves))

    def silu(self, act, un, f, between=lambda: None):
        m = FT[f][1]
        act.wait_ge(self.main_t, self.MT(un.u, f"gate{f}"))
        reach(act, self.main_v, self.MV(un.u - 1, f"mul{f}"))
        act.activation(self.split(self.sil[0:m, f, :]), self.psum(0, m), ACT.Silu).then_inc(self.main_a, 1)
        between()
        act.wait_ge(self.main_v, self.MV(un.u, f"mul{f}"))
        reach(act, self.down_t, self.DN(un.u - 2, f"tile{self.tiles - 1}"))
        act.copy(self.acth[0:m, un.q, f, :], self.act[0:m, f, :]).then_inc(self.main_a, 1)

    def take_down(self, act, un, scale=None, free=None):
        for j in range(self.tiles):
            act.wait_ge(self.down_t, self.DN(un.u, f"tile{j}"))
            if j == 0 and free is not None:
                reach(act, *free)
            if scale is None:
                ins = act.copy(self.out[:, un.q, j, :], self.Y[:, 2 + j % 2, 0:D])
            else:
                ins = act.mul(self.out[:, un.q, j, :], self.Y[:, 2 + j % 2, 0:D], scale[:, j:j + 1])
            ins.then_inc(self.down_a, 1)

    def hin_lo(self, v, un, t):
        v.wait_ge(self.pre_a, self.PA(un.u, f"hin{t}"))
        n = self.tiles * P
        v.tensor_tensor(self.hin[:, un.q, 1, t, :], self.Y[:, 0:2].rearrange("p a n -> p (a n)")[:, 0:n],
                        self.hin[:, un.q, 0, t, :].bitcast(F32), ALU.subtract).then_inc(self.pre_v, 1)

    def mul(self, v, un, f, between=lambda: None):
        m = FT[f][1]
        v.wait_ge(self.main_t, self.MT(un.u, f"up{f}"))
        v.wait_ge(self.main_a, self.MA(un.u, f"silu{f}"))
        v.tensor_tensor(self.split(self.act[0:m, f, :]), self.psum(2, m), self.split(self.sil[0:m, f, :]), ALU.mult).then_inc(self.main_v, 1)
        between()
        v.wait_ge(self.main_a, self.MA(un.u, f"hi{f}"))
        v.tensor_tensor(self.actl[0:m, un.q, f, :], self.act[0:m, f, :], self.acth[0:m, un.q, f, :].bitcast(F32),
                        ALU.subtract).then_inc(self.main_v, 1)


def expert_inputs(sb, sem, s):
    return {
        "raw": sb("ew_raw", [P, 2, 2, T2, F1], F32, s), "rawd": sb("ew_rawd", [P, 2, 3, D], F32, s),
        "rows": sb("ew_rows", [P, 2, CAP // P, ROW], F32, s),
        "sums": sb("shared_sums", [P, 2, 4, D], F32, s), "stored": [sem(f"sw_stored{q}", s) for q in range(2)],
        "weights_in": [sem(f"ew_weights{q}", s) for q in range(2)], "rows_in": [sem(f"ew_rows{q}", s) for q in range(2)],
    }


def load_expert_weights(sp, a, pre, un):
    q = un.q
    e_of = lambda name: a[name][un.u] if isinstance(un.u, int) else a[name][bass.ds(un.u, 1)].rearrange("o k n -> (o k) n")
    wd = e_of("L1_ffn_w_down")
    for dst, src in (
        (pre["raw"][:, q, 0], e_of("L1_ffn_w_gate").rearrange("(t p) n -> p t n", p=P)),
        (pre["raw"][:, q, 1], e_of("L1_ffn_w_up").rearrange("(t p) n -> p t n", p=P)),
        (pre["rawd"][:, q, 0:2], wd[0:2 * P].rearrange("(t p) n -> p t n", p=P)),
        (pre["rawd"][0:F1 - 2 * P, q, 2], wd[2 * P:F1]),
    ):
        sp.dma_start(dst, src).then_inc(pre["weights_in"][q], 16)


def load_expert_rows(sp, dram, pre, un):
    sp.dma_start(pre["rows"][:, un.q], dram["rows"][bass.ds(un.u * CAP, CAP)].rearrange("(j p) r -> p j r", p=P)).then_inc(pre["rows_in"][un.q], 16)


def shared_and_routing(nc, sb, sem, a, k, X, Y, dram, shared, pre):
    with ExitStack() as s:
        t = lambda n, shape, dt=F32: sb(n, shape, dt, s)
        x = k["x"]
        sw = Swiglu(nc, sb, sem, s, "shared", X, Y, k["ident"], 4, [(0, 4 * P)], 2 * B, pre["sums"])
        raw, rawd, loads = shared["raw"], shared["rawd"], shared["loads"]
        wg = (t("sw_gh", [P, T2, F1], F32R), t("sw_gl", [P, T2, F1], F32R))
        wu = (t("sw_uh", [P, T2, F1], F32R), t("sw_ul", [P, T2, F1], F32R))
        wd = (t("sw_dh", [P, 3, D], F32R), t("sw_dl", [P, 3, D], F32R))
        rows = t("sw_rows", [P, 2, 4, D])
        stream = t("sw_stream", [P, 2, 4, D])
        NK = 2
        tri, onesb = t("tri", [P, P], BF16), t("onesb", [P, P], BF16)
        trif = t("trif", [P, P])
        ie, ief = t("ie", [P, E1], U32), t("ief", [P, E1])
        tok = t("tok", [P, NT], U32)
        ti = t("ti", [P, NK, NT])
        one_hot, prod = t("one_hot", [P, NK, NT, E1]), t("prod", [P, NK, NT, E1])
        lg, ex = t("lg", [P, NT, E1]), t("ex", [P, NT, E1])
        cnt = t("cnt", [P, NT * E1], BF16)
        keep, tot, incl = t("keep", [P, E1, NT]), t("tot", [P, E1, NT]), t("incl", [P, E1, NT])
        before = t("before", [P, NT, E1])
        z, e2, val, pos, inside = t("z", [P, NT]), t("e2", [P, NT]), t("val", [P, NK, NT]), t("pos", [P, NK, NT]), t("inside", [P, NK, NT])
        slotf, slot = t("slotf", [P, NK, NT]), t("slot", [P, NK, NT], U32)

        rows_in = [sem(f"sw_rows{q}", s) for q in range(2)]
        stream_in, mixed = [sem(f"sw_stream_in{q}", s) for q in range(2)], sem("sw_mixed", s)
        MX, tail = Steps("gated whole"), sem("sw_mixed_last", s)
        wts_a, wts_v, rt_v, rt_a, rt_t, rt_p = (sem(n, s) for n in ("sw_split_act", "sw_split_vec", "slots_vec", "slots_act", "slots_pe", "slots_pool"))
        sent = [sem(f"scattered{i}", s) for i in range(2)]
        stored = pre["stored"]
        RV = Steps("sub gap ti oh0 oh1 cnt keep1 keep0 tot scan excl before prod pos inside z rz p2 sum rs v1 v2 w slotf over slot tok w0")
        RA = Steps("exp e2 tri ones")
        RT = Steps("count")
        RP = Steps("tri0 tri ie tok w1")
        block = s.enter_context(nc.Block())
        tiles = x[:].rearrange("p b c r -> p (b c) r")
        lgt = k["logits"][:].rearrange("p b c e -> p (b c) e")
        top = k["top"][:].rearrange("p b c e -> p (b c) e")
        topi = k["topi"][:].rearrange("p b c e -> p (b c) e")

        @block.sync
        def _(sp):
            def load(un):
                reach(sp, sw.pre_t, sw.PT(un.u - 2, "turn1"))
                sp.dma_start(rows[:, un.q], tiles[:, bass.ds(4 * un.u, 4), 0:D]).then_inc(rows_in[un.q], 16)

            def load_stream(un):
                sp.dma_start(stream[:, un.q], dram["xres"][bass.ds(un.u * 4 * P, 4 * P)].rearrange("(j p) d -> p j d", p=P)).then_inc(stream_in[un.q], 16)

            def first(un):
                load(un)
                load(un.next())
                load_stream(un)
                load_stream(un.next())
                for q in range(2):
                    load_expert_weights(sp, a, pre, Unit(0, q))

            def turn(un, after, before_):
                if not (isinstance(un.pair, int) and un.pair == B - 1):
                    load(Unit(un.pair + 1, un.q))
                if before_:
                    store(un.last())
                if after and before_:
                    load_stream(un.next())
                if not after:
                    for q in range(2):
                        sp.wait_ge(sent[q], 16 * NT)
                    for q in range(2):
                        load_expert_rows(sp, dram, pre, Unit(0, q))

            def store_last(un):
                sp.wait_ge(tail, 2 * 4)
                send(un)

            def store(un):
                sp.wait_ge(mixed, MX(un.u, "whole"))
                send(un)

            def send(un):
                sp.dma_start(dram["out"][bass.ds(un.u * 4 * P, 4 * P)].rearrange("(j p) d -> p j d", p=P), sw.out[:, un.q]).then_inc(stored[un.q], 16)
            sw.eng = sp
            sw.run(turn, first, store_last)

        @block.gpsimd
        def _(pool):
            pool.memset(trif[:], 1.0).then_inc(rt_p, 1)
            pool.wait_ge(rt_p, RP(0, "tri0"))
            pool.affine_select(out=trif[:], in_=trif[:], compare_op=ALU.is_ge, fill=0.0, base=-1,
                               pattern=[[1, P]], channel_multiplier=-1).then_inc(rt_p, 1)
            pool.iota(ie[:], pattern=[[1, E1]], base=0, channel_multiplier=0).then_inc(rt_p, 1)
            pool.iota(tok[:], pattern=[[P, NT]], base=1, channel_multiplier=1).then_inc(rt_p, 1)
            pool.wait_ge(rt_v, RV(0, "w0"))
            for kk in range(NK):
                if kk:
                    pool.wait_ge(sent[0], 16 * NT)
                    pool.tensor_copy(tiles[:, :, D], val[:, 1, :]).then_inc(rt_p, 1)
                    pool.wait_ge(rt_p, RP(0, "w1"))
                for tt in range(NT):
                    pool.indirect_dma_start(dram["rows"], bass.IndirectOffsetOnAxis(slot[:, kk, tt:tt + 1], 0), tiles[:, tt, :], None,
                                            bounds_check=SLOTS - 1, oob_is_err=False).then_inc(sent[kk], 16)
            for kk in range(NK):
                pool.wait_ge(sent[kk], 16 * NT)

        @block.scalar
        def _(act):
            act.wait_ge(loads, 16 * 4)
            for i, (dst, src) in enumerate(((wg[0][:], raw[:, 0]), (wu[0][:], raw[:, 1]), (wd[0][:, 0:2], rawd[:, 0:2]),
                                            (wd[0][0:F1 - 2 * P, 2], rawd[0:F1 - 2 * P, 2]))):
                act.copy(dst, src).then_inc(wts_a, 1)

            def first(un):
                for t_ in range(T2):
                    sw.hin_hi(act, un, t_)
                act.wait_ge(rt_v, RV(0, "gap"))
                act.activation(ex[:], lg[:], ACT.Exp).then_inc(rt_a, 1)
                act.activation(e2[:], e2[:], ACT.Exp).then_inc(rt_a, 1)
                act.wait_ge(rt_p, RP(0, "tri"))
                act.copy(tri[:], trif[:]).then_inc(rt_a, 1)
                act.activation(onesb[:], trif[:], ACT.Identity, bias=1.0, scale=0.0).then_inc(rt_a, 1)

            def turn(un, after, before_):
                sw.silu(act, un, 0)
                if after:
                    sw.hin_hi(act, un.next(), 0)
                if before_:
                    down(un.last())
                sw.silu(act, un, 1)
                if after:
                    sw.hin_hi(act, un.next(), 1)
                sw.silu(act, un, 2)

            def down(un):
                sw.take_down(act, un, free=(stored[un.q], 16 * un.pair))
            sw.eng = act
            sw.run(turn, first, down)

        def did(ins):
            ins.then_inc(rt_v, 1)

        def route_pairs(v):
            bc = lambda ap: ap.unsqueeze(2).to_broadcast([P, NT, E1])
            did(v.tensor_tensor(lg[:], lgt, top[:, :, 0:1].to_broadcast([P, NT, E1]), ALU.subtract))
            did(v.tensor_tensor(e2[:], top[:, :, 1], top[:, :, 0], ALU.subtract))
            did(v.tensor_copy(ti[:], topi[:, :, 0:NK].rearrange("p t k -> p k t")))
            v.wait_ge(rt_p, RP(0, "ie"))
            v.tensor_copy(ief[:], ie[:])
            v.wait_ge(rt_v, RV(0, "ti"))
            v.drain()
            for kk in range(NK):
                did(v.tensor_tensor(one_hot[:, kk], ief[:].unsqueeze(1).to_broadcast([P, NT, E1]), bc(ti[:, kk]), ALU.is_equal))
            v.wait_ge(rt_v, RV(0, "oh1"))
            did(v.tensor_tensor(cnt[:].rearrange("p (t e) -> p t e", e=E1), one_hot[:, 0], one_hot[:, 1], ALU.add))
            did(v.memset(keep[:], 1.0))
            v.wait_ge(rt_v, RV(0, "keep1"))
            did(v.memset(keep[:, :, 0:1], 0.0))

        def route_tiles_before(v):
            v.wait_ge(rt_t, RT(0, "count"))
            did(v.tensor_copy(tot[:], Y[:, 3, 0:NT * E1].rearrange("p (t e) -> p e t", e=E1)))
            v.wait_ge(rt_v, RV(0, "tot"))
            flat = lambda ap: ap.rearrange("p e t -> p (e t)")
            did(v.tensor_tensor_scan(flat(incl[:]), flat(keep[:]), flat(tot[:]), 0.0, ALU.mult, ALU.add))
            v.wait_ge(rt_v, RV(0, "scan"))
            did(v.tensor_tensor(incl[:], incl[:], tot[:], ALU.subtract))
            v.wait_ge(rt_v, RV(0, "excl"))
            did(v.tensor_tensor(before[:], Y[:, 2, 0:NT * E1].rearrange("p (t e) -> p t e", e=E1), incl[:].rearrange("p e t -> p t e"), ALU.add))
            v.wait_ge(rt_v, RV(0, "before"))

        def route_places(v):
            for kk in range(NK):
                ins = v.tensor_tensor(prod[:, kk], one_hot[:, kk], before[:], ALU.mult)
            did(ins)
            v.wait_ge(rt_v, RV(0, "prod"))
            did(v.reduce_sum(pos[:].rearrange("p k t -> p (k t)"), prod[:].rearrange("p k t e -> p (k t) e"), AX.X))
            v.wait_ge(rt_v, RV(0, "pos"))
            did(v.tensor_scalar(inside[:], pos[:], float(CAP), None, ALU.is_lt))

        def route_weights(v):
            v.wait_ge(rt_a, RA(0, "e2"))
            did(v.reduce_sum(z[:], ex[:], AX.X))
            v.wait_ge(rt_v, RV(0, "z"))
            did(v.reciprocal(z[:], z[:]))
            v.wait_ge(rt_v, RV(0, "rz"))
            did(v.tensor_tensor(e2[:], e2[:], z[:], ALU.mult))
            v.wait_ge(rt_v, RV(0, "p2"))
            did(v.scalar_tensor_tensor(out=val[:, 0], in0=z[:], scalar=1e-9, in1=e2[:], op0=ALU.add, op1=ALU.add))
            v.wait_ge(rt_v, RV(0, "sum"))
            did(v.reciprocal(val[:, 0], val[:, 0]))
            v.wait_ge(rt_v, RV(0, "rs"))
            did(v.tensor_tensor(val[:, 1], val[:, 0], e2[:], ALU.mult))
            v.wait_ge(rt_v, RV(0, "v1"))
            did(v.tensor_tensor(val[:, 0], val[:, 0], z[:], ALU.mult))
            v.wait_ge(rt_v, RV(0, "v2"))
            did(v.tensor_tensor(val[:], val[:], inside[:], ALU.mult))
            did(v.scalar_tensor_tensor(out=slotf[:], in0=ti[:], scalar=float(CAP), in1=pos[:], op0=ALU.mult, op1=ALU.add))
            v.wait_ge(rt_v, RV(0, "slotf"))
            did(v.tensor_scalar(pos[:], inside[:], -float(4 * SLOTS), float(4 * SLOTS), ALU.mult, ALU.add))
            v.wait_ge(rt_v, RV(0, "over"))
            did(v.tensor_tensor(slot[:], slotf[:], pos[:], ALU.add))
            v.wait_ge(rt_p, RP(0, "tok"))
            did(v.tensor_copy(tiles[:, :, D + 1], tok[:]))
            v.wait_ge(rt_v, RV(0, "w"))
            did(v.tensor_copy(tiles[:, :, D], val[:, 0, :]))

        @block.vector
        def _(v):
            for i, (lo, src, hi) in enumerate(((wg[1][:], raw[:, 0], wg[0][:]), (wu[1][:], raw[:, 1], wu[0][:]),
                                               (wd[1][:, 0:2], rawd[:, 0:2], wd[0][:, 0:2]),
                                               (wd[1][0:F1 - 2 * P, 2], rawd[0:F1 - 2 * P, 2], wd[0][0:F1 - 2 * P, 2]))):
                v.wait_ge(wts_a, i + 1)
                v.tensor_tensor(lo, src, hi.bitcast(F32), ALU.subtract).then_inc(wts_v, 1)

            def first(un):
                for t_ in range(T2):
                    sw.hin_lo(v, un, t_)
                route_pairs(v)

            def turn(un, after, before_):
                at = un.u if isinstance(un.u, int) else None
                sw.mul(v, un, 0)
                if after:
                    sw.hin_lo(v, un.next(), 0)
                if at == 0:
                    route_tiles_before(v)
                if at == 1:
                    route_weights(v)
                if before_:
                    mix(un.last())
                sw.mul(v, un, 1)
                if at == 0:
                    route_places(v)
                if after:
                    sw.hin_lo(v, un.next(), 1)
                sw.mul(v, un, 2)

            def mix(un):
                o = sw.out[:, un.q]
                v.wait_ge(sw.down_a, sw.DN(un.u, "tile3"))
                v.tensor_tensor(o, o, k["gbrow"][:, bass.ds(un.pair, 1), :].to_broadcast([P, 4, D]), ALU.mult).then_inc(mixed, 1)
                v.wait_ge(stream_in[un.q], 16 * (un.pair + 1))
                v.wait_ge(mixed, MX(un.u, "gated"))
                v.tensor_tensor(o, o, stream[:, un.q], ALU.add).then_inc(mixed, 1)

            def mix_tiles(un):
                v.wait_ge(stream_in[un.q], 16 * (un.pair + 1))
                for j in range(4):
                    o = sw.out[:, un.q, j]
                    v.wait_ge(sw.down_a, sw.DN(un.u, f"tile{j}"))
                    v.tensor_tensor(o, o, k["gbrow"][:, un.pair, :], ALU.mult).then_inc(tail, 1)
                    v.wait_ge(tail, 2 * j + 1)
                    v.tensor_tensor(o, o, stream[:, un.q, j], ALU.add).then_inc(tail, 1)
            sw.eng = v
            sw.run(turn, first, mix_tiles)

        @block.tensor
        def _(pe):
            def counts():
                pe.wait_ge(rt_v, RV(0, "cnt"))
                pe.wait_ge(rt_a, RA(0, "ones"))
                pe.matmul(Y[:, 2], tri[:], cnt[:], start=True, stop=True)
                pe.matmul(Y[:, 3], onesb[:], cnt[:], start=True, stop=True).then_inc(rt_t, 1)

            def turn_in(un, t_):
                pe.wait_ge(rows_in[un.q], 16 * (un.pair + 1))
                sw.turn_in(pe, un, t_, rows[:, un.q])

            def first(un):
                for t_ in range(T2):
                    turn_in(un, t_)
                pe.wait_ge(wts_v, 4)

            def turn(un, after, before_):
                sw.gate_up(pe, un, 0, wg, wu)
                if after:
                    turn_in(un.next(), 0)
                if before_:
                    if isinstance(un.u, int) and un.u == 1:
                        pe.wait_ge(rt_v, RV(0, "before"))
                    sw.down(pe, un.last(), wd)
                else:
                    counts()
                sw.gate_up(pe, un, 1, wg, wu)
                if after:
                    turn_in(un.next(), 1)
                sw.gate_up(pe, un, 2, wg, wu)
            sw.eng = pe
            sw.run(turn, first, lambda un: sw.down(pe, un, wd))


def experts(nc, sb, sem, a, k, X, Y, dram, pre):
    with ExitStack() as s:
        t = lambda n, shape, dt=F32: sb(n, shape, dt, s)
        NTE = CAP // P
        sw = Swiglu(nc, sb, sem, s, "expert", X, Y, k["ident"], NTE, [(0, CAP // 2), (CAP // 2, CAP // 2)], E1)
        raw, rawd, rows, weights_in, rows_in = (pre[n] for n in ("raw", "rawd", "rows", "weights_in", "rows_in"))
        wgu = [t(f"ew_{n}", [P, 2, 2, T2, F1], F32R) for n in ("h", "l")]
        wdn = [t(f"ew_d{n}", [P, 2, 3, D], F32R) for n in ("h", "l")]
        above = t("ew_above", [P, B + 1, NTE])
        wt = t("ew_weight", [P, 2, B, NTE])
        gains = t("ew_gains", [P, 2, NTE, D])
        none = t("ew_none", [P, 2, NTE])
        idx = t("ew_idx", [P, 2, NTE], U32)
        added = [sem(f"ew_added{q}", s) for q in range(2)]
        high, split, seen = sem("ew_high", s), sem("ew_split", s), sem("ew_seen", s)
        weighed, placed, gain_a, gain_v, gated = (sem(f"ew_{n}", s) for n in ("weighed", "placed", "gain_act", "gain_vec", "gated"))
        cleared = sem("ew_cleared", s)
        SPL, WE, PL = Steps("gul d01h d01l d2h d2l"), Steps("above weight"), Steps("none idx")
        NEAR = 3
        GV = Steps(["ahead"] + [f"batch{b}" for b in range(1, B)])
        M2 = F1 - 2 * P
        block = s.enter_context(nc.Block())

        @block.sync
        def _(sp):
            def load(un):
                if isinstance(un.u, int) and un.u < 2:
                    return
                reach(sp, split, SPL(un.u - 2, "d2l"))
                load_expert_weights(sp, a, pre, un)
                reach(sp, sw.pre_t, sw.PT(un.u - 2, "turn1"))
                reach(sp, placed, PL(un.u - 2, "idx"))
                load_expert_rows(sp, dram, pre, un)

            def turn(un, after, before):
                if after:
                    load(un.next())
            sw.eng = sp
            sw.run(turn, load, lambda un: None)

        @block.gpsimd
        def _(pool):
            def add(un, tilewise=False):
                reach(pool, added[1 - un.q], 16 * NTE * (un.pair + un.q))
                pool.wait_ge(placed, PL(un.u, "idx"))
                if not tilewise:
                    apart(pool, gated, un.u + 1, seen)
                for j in range(NTE):
                    if tilewise:
                        pool.wait_ge(gated, un.u + 1 + j)
                    pool.indirect_dma_start(dram["out"], bass.IndirectOffsetOnAxis(idx[:, un.q, j:j + 1], 0), sw.out[:, un.q, j, :], None,
                                            compute_op=ALU.add,
                                            bounds_check=B * S - 1, oob_is_err=False).then_inc(added[un.q], 16)

            def split_part(un, name, hi, lo, whole):
                pool.tensor_copy(hi, whole).then_inc(split, 1)
                pool.wait_ge(split, SPL(un.u, name + "h"))
                pool.tensor_tensor(lo, whole, hi.bitcast(F32), ALU.subtract).then_inc(split, 1)

            def split_in(un):
                q = un.q
                pool.wait_ge(high, un.u + 1)
                pool.tensor_tensor(wgu[1][:, q], raw[:, q], wgu[0][:, q].bitcast(F32), ALU.subtract).then_inc(split, 1)

            def split_out(un):
                q = un.q
                apart(pool, weights_in[q], 64 * (un.pair + 1), seen)
                split_part(un, "d01", wdn[0][:, q, 0:2], wdn[1][:, q, 0:2], rawd[:, q, 0:2])
                split_part(un, "d2", wdn[0][0:M2, q, 2], wdn[1][0:M2, q, 2], rawd[0:M2, q, 2])

            def first(un):
                pool.wait_ge(split, SPL(un.u, "gul"))
                split_out(un)
                for q in range(2):
                    pool.wait_ge(pre["stored"][q], 16 * B)

            def turn(un, after, before):
                if after:
                    split_in(un.next())
                    split_out(un.next())
                if before:
                    add(un.last())
            sw.eng = pool
            sw.run(turn, first, lambda un: add(un, True))
            for q in range(2):
                pool.wait_ge(added[q], 16 * NTE * E1 // 2)

        @block.scalar
        def _(act):
            def split(un):
                act.wait_ge(weights_in[un.q], 64 * (un.pair + 1))
                reach(act, sw.main_t, sw.MT(un.u - 2, "up2"))
                act.copy(wgu[0][:, un.q], raw[:, un.q]).then_inc(high, 1)

            def first(un):
                sw.hin_hi(act, un, 0)
                split(un)
                sw.hin_hi(act, un, 1)
                gains_first(un)

            def gains_first(un):
                act.wait_ge(weighed, WE(un.u, "weight"))
                reach(act, gated, un.u - 1)
                for j in range(NTE):
                    ins = act.mul(gains[:, un.q, j, :], k["gbrow"][:, 0, :], wt[:, un.q, 0, j:j + 1])
                ins.then_inc(gain_a, 1)

            def turn(un, after, before):
                sw.silu(act, un, 0)
                if after:
                    sw.hin_hi(act, un.next(), 0)
                if before:
                    down(un.last())
                if after:
                    split(un.next())
                sw.silu(act, un, 1)
                if after:
                    sw.hin_hi(act, un.next(), 1)
                if after:
                    sw.silu(act, un, 2, lambda: gains_first(un.next()))
                else:
                    sw.silu(act, un, 2)

            def down(un):
                sw.take_down(act, un, free=(added[un.q], 16 * NTE * un.pair))
            sw.eng = act
            sw.run(turn, first, down)

        @block.vector
        def _(v):
            def weights(un):
                q = un.q
                v.wait_ge(rows_in[q], 16 * (un.pair + 1))
                for b in range(B):
                    ins = v.scalar_tensor_tensor(out=above[:, b], in0=rows[:, q, :, D + 1], scalar=float(b * S), in1=rows[:, q, :, D],
                                                 op0=ALU.is_gt, op1=ALU.mult)
                ins.then_inc(weighed, 1)
                v.wait_ge(weighed, WE(un.u, "above"))
                v.tensor_tensor(wt[:, q], above[:, 0:B], above[:, 1:B + 1], ALU.subtract).then_inc(weighed, 1)

            def gains_term(un, b, tiles):
                for j in tiles:
                    g = gains[:, un.q, j, :]
                    ins = v.scalar_tensor_tensor(out=g, in0=k["gbrow"][:, b, :], scalar=wt[:, un.q, b, j:j + 1], in1=g, op0=ALU.mult, op1=ALU.add)
                ins.then_inc(gain_v, 1)

            def gains_ahead(un):
                v.wait_ge(weighed, WE(un.u, "weight"))
                v.wait_ge(gain_a, un.u + 1)
                gains_term(un, 1, range(NEAR))

            def gains_rest(un, first=2, end=B):
                for b in range(first, end):
                    v.wait_ge(gain_v, GV(un.u, f"batch{b - 1}"))
                    gains_term(un, b, range(NTE))

            def tokens(un):
                q = un.q
                v.tensor_scalar(none[:, q], rows[:, q, :, D + 1], 0.0, float(4 * SLOTS), ALU.is_equal, ALU.mult).then_inc(placed, 1)
                v.wait_ge(placed, PL(un.u, "none"))
                reach(v, added[q], 16 * NTE * un.pair)
                v.scalar_tensor_tensor(out=idx[:, q], in0=rows[:, q, :, D + 1], scalar=-1.0, in1=none[:, q], op0=ALU.add, op1=ALU.add).then_inc(placed, 1)

            def mix(un):
                v.wait_ge(sw.down_a, sw.DN(un.u, f"tile{NTE - 1}"))
                v.wait_ge(gain_v, GV(un.u, f"batch{B - 1}"))
                v.tensor_tensor(sw.out[:, un.q], sw.out[:, un.q], gains[:, un.q], ALU.mult).then_inc(gated, 1)

            def first(un):
                v.memset(above[:, B], 0.0).then_inc(cleared, 1)
                v.wait_ge(cleared, 1)
                weights(un)
                sw.hin_lo(v, un, 0)
                v.wait_ge(high, un.u + 1)
                v.tensor_tensor(wgu[1][:, un.q], raw[:, un.q], wgu[0][:, un.q].bitcast(F32), ALU.subtract).then_inc(split, 1)
                sw.hin_lo(v, un, 1)
                gains_ahead(un)
                gains_term(un, 1, range(NEAR, NTE))
                gains_rest(un, 2, B - 1)

            def turn(un, after, before):
                if before:
                    sw.mul(v, un, 0, lambda: gains_term(un, 1, range(NEAR, NTE)))
                else:
                    sw.mul(v, un, 0)
                if after:
                    sw.hin_lo(v, un.next(), 0)
                gains_rest(un, 2 if before else B - 1)
                if before:
                    mix(un.last())
                if after:
                    sw.mul(v, un, 1, lambda: weights(un.next()))
                else:
                    sw.mul(v, un, 1)
                tokens(un)
                if after:
                    sw.hin_lo(v, un.next(), 1)
                sw.mul(v, un, 2)
                if after:
                    gains_ahead(un.next())
            def mix_tiles(un):
                v.wait_ge(gain_v, GV(un.u, f"batch{B - 1}"))
                for j in range(NTE):
                    v.wait_ge(sw.down_a, sw.DN(un.u, f"tile{j}"))
                    v.tensor_tensor(sw.out[:, un.q, j], sw.out[:, un.q, j], gains[:, un.q, j], ALU.mult).then_inc(gated, 1)
            sw.eng = v
            sw.run(turn, first, mix_tiles)

        @block.tensor
        def _(pe):
            wd = lambda q: (wdn[0][:, q], wdn[1][:, q])
            wg = lambda q: (wgu[0][:, q, 0], wgu[1][:, q, 0])
            wu = lambda q: (wgu[0][:, q, 1], wgu[1][:, q, 1])

            def turn_in(un, t_):
                pe.wait_ge(rows_in[un.q], 16 * (un.pair + 1))
                sw.turn_in(pe, un, t_, rows[:, un.q])

            def first(un):
                for t_ in range(T2):
                    turn_in(un, t_)

            def down(un):
                pe.wait_ge(split, SPL(un.u, "d2l"))
                sw.down(pe, un, wd(un.q))

            def turn(un, after, before):
                pe.wait_ge(split, SPL(un.u, "gul"))
                sw.gate_up(pe, un, 0, wg(un.q), wu(un.q))
                if after:
                    turn_in(un.next(), 0)
                if before:
                    down(un.last())
                sw.gate_up(pe, un, 1, wg(un.q), wu(un.q))
                if after:
                    turn_in(un.next(), 1)
                sw.gate_up(pe, un, 2, wg(un.q), wu(un.q))
            sw.eng = pe
            sw.run(turn, first, down)


_INS = ["L0_attn_hidden_states", "L0_attn_w_q", "L0_attn_w_k", "L0_attn_w_v", "L0_attn_w_o", "L0_attn_gate",
        "L0_attn_memory", "L0_attn_memory_norm", "L0_ffn_gate_w", "L0_ffn_w1", "L0_ffn_b1", "L0_ffn_w2", "L0_ffn_b2",
        "L0_ffn_sw1", "L0_ffn_sb1", "L0_ffn_sw2", "L0_ffn_sb2", "L0_c", "L0_wmod", "L1_attn_W_qkv", "L1_attn_b_qkv",
        "L1_attn_W_out", "L1_attn_b_out", "L1_ffn_router_w", "L1_ffn_router_b", "L1_ffn_w_gate", "L1_ffn_w_up",
        "L1_ffn_w_down", "L1_ffn_sw_gate", "L1_ffn_sw_up", "L1_ffn_sw_down", "L1_c", "L1_wmod"]


def kernel(**inputs):
    import numpy as np
    import concourse.bacc as bacc
    from concourse.bass_utils import run_bass_kernel_spmd

    nc = bacc.Bacc("TRN2", target_bir_lowering=False, num_devices=1)
    arrays, aps = {}, {}
    for name in _INS:
        arr = np.ascontiguousarray(inputs[name])
        arrays[f"in_{name}"] = arr
        aps[name] = nc.dram_tensor(f"in_{name}", arr.shape, mybir.dt.from_np(arr.dtype), kind="ExternalInput").ap()
    out = nc.dram_tensor("out_0", (B, S, D), F32, kind="ExternalOutput").ap()
    build(nc, aps, out)
    r = run_bass_kernel_spmd(nc, [arrays], core_ids=[0])
    return r.results[0]["out_0"]
```
